# Optimizing a Trainium2 kernel written in Bass

```python
import numpy as np
import jax
import jax.numpy as jnp

def _softmax(x, axis=-1):
    return jax.nn.softmax(x, axis=axis)

def _gelu(x):
    return jax.nn.gelu(x, approximate=True)

def _silu(x):
    return jax.nn.silu(x)

def _sigmoid(x):
    return jax.nn.sigmoid(x)

def _layernorm(x, axis=-1, eps=1e-05):
    m = jnp.mean(x, axis=axis, keepdims=True)
    v = jnp.var(x, axis=axis, keepdims=True)
    return (x - m) / jnp.sqrt(v + eps)

def _scatter_add(tgt, idx, src, axis=0):
    return tgt.at[idx].add(src)

def _segment_sum(src, seg, n):
    return jax.ops.segment_sum(src, seg, n)
kernel_name = 'mk_perceiver_d2_seqx_r4_71cb23'

def setup_inputs(seed: int=0):
    np.random.seed(seed)
    _w = jnp.asarray

    def _rec_inputs():
        import jax
        import jax.numpy as jnp
        _rk = jax.random.key(seed)
        x = -0.0002928 + 1 * jax.random.normal(jax.random.fold_in(_rk, 1), (2, 256, 256), jnp.float32)
        _lenS = 256 - jax.random.randint(jax.random.fold_in(_rk, 7), (2,), 0, max(1, 256 // 4) + 1, jnp.int32)
        _lenS2 = 4096 - jax.random.randint(jax.random.fold_in(_rk, 8), (2,), 0, max(1, 4096 // 4) + 1, jnp.int32)
        _ctx_512P = jax.random.normal(jax.random.fold_in(_rk, 11), (2, 16, 128), jnp.float32)
        _ctx_512c = jax.random.dirichlet(jax.random.fold_in(_rk, 511), 0.3 * jnp.ones((16,), jnp.float32), (2, 4096))
        _ctx_512t = jnp.einsum('bsk,bkd->bsd', _ctx_512c, _ctx_512P)
        _ctx_512t = _ctx_512t * jax.lax.rsqrt(jnp.mean(jnp.square(_ctx_512t)) + 1e-12) * 0.953939
        ctx_512 = -0.000514642 + 1.00011 * (_ctx_512t + 0.3 * jax.random.normal(jax.random.fold_in(_rk, 611), (2, 4096, 128), jnp.float32))
        return (x, ctx_512)
    x, ctx_512 = _rec_inputs()

    def _L0_xattn_setup():
        import jax, jax.numpy as jnp
        import numpy as np
        DIM = 256
        LATENT_DIM = 128
        NUM_HEADS = 16
        HEAD_DIM = DIM // NUM_HEADS
        SCALE = HEAD_DIM ** (-0.5)
        key = jax.random.key(seed)
        k1, k2, k3, k4, k5 = jax.random.split(key, 5)
        B, xN, zN = (2, 512, 512)
        x = jax.random.normal(k1, (B, xN, DIM), dtype=jnp.float32)
        z = jax.random.normal(k2, (B, zN, LATENT_DIM), dtype=jnp.float32)
        Wq = jax.random.normal(k3, (DIM, DIM), dtype=jnp.float32) * DIM ** (-0.5)
        Wkv = jax.random.normal(k4, (2 * DIM, LATENT_DIM), dtype=jnp.float32) * LATENT_DIM ** (-0.5)
        Wo = jax.random.normal(k5, (DIM, DIM), dtype=jnp.float32) * DIM ** (-0.5)
        return {'x': x, 'z': z, 'Wq': Wq, 'Wkv': Wkv, 'Wo': Wo}
    _L0_xattn_all = _L0_xattn_setup()
    _L0_xattn_in = {k: v for k, v in _L0_xattn_all.items() if k in ('Wq', 'Wkv', 'Wo')}
    del _L0_xattn_all

    def _L0_attn_setup():
        import jax, jax.numpy as jnp
        import numpy as np
        import math
        BATCH, SEQ = (8, 1024)
        D_MODEL, D_STATE, D_CONV = (256, 16, 4)
        LN_EPS = 1e-05
        key = jax.random.key(seed)
        ks = jax.random.split(key, 12)
        s_d = 1.0 / math.sqrt(D_MODEL)
        x = jax.random.normal(ks[0], (BATCH, SEQ, D_MODEL), jnp.float32)
        conv_w = jax.random.normal(ks[1], (D_MODEL, 1, D_CONV), jnp.float32) * 0.3
        conv_b = jax.random.normal(ks[2], (D_MODEL,), jnp.float32) * 0.02
        A = jnp.broadcast_to(jnp.linspace(math.log(0.001), math.log(5.0), D_STATE, dtype=jnp.float32)[None, :], (D_MODEL, D_STATE)).copy()
        Bp_w = jax.random.normal(ks[3], (D_STATE, D_MODEL), jnp.float32) * s_d
        Bp_b = jnp.zeros((D_STATE,), jnp.float32)
        Cp_w = jax.random.normal(ks[4], (D_STATE, D_MODEL), jnp.float32) * s_d
        Cp_b = jnp.zeros((D_STATE,), jnp.float32)
        D = jnp.ones((D_MODEL,), jnp.float32)
        gate_w = jax.random.normal(ks[5], (D_MODEL, D_MODEL), jnp.float32) * s_d
        gate_b = jnp.zeros((D_MODEL,), jnp.float32)
        out_w = jax.random.normal(ks[6], (D_MODEL, D_MODEL), jnp.float32) * s_d
        out_b = jnp.zeros((D_MODEL,), jnp.float32)
        ln_g = jnp.ones((D_MODEL,), jnp.float32)
        ln_b = jnp.zeros((D_MODEL,), jnp.float32)
        return {'x': x, 'conv_w': conv_w, 'conv_b': conv_b, 'A': A, 'Bp_w': Bp_w, 'Bp_b': Bp_b, 'Cp_w': Cp_w, 'Cp_b': Cp_b, 'D': D, 'gate_w': gate_w, 'gate_b': gate_b, 'out_w': out_w, 'out_b': out_b, 'ln_g': ln_g, 'ln_b': ln_b}
    _L0_attn_all = _L0_attn_setup()
    _L0_attn_in = {k: v for k, v in _L0_attn_all.items() if k in ('conv_w', 'conv_b', 'A', 'Bp_w', 'Bp_b', 'Cp_w', 'Cp_b', 'D', 'gate_w', 'gate_b', 'out_w', 'out_b', 'ln_g', 'ln_b')}
    del _L0_attn_all

    def _L0_ffn_setup():
        import jax, jax.numpy as jnp
        import numpy as np
        B, N, D = (4, 512, 256)
        SPARSITY = 0.01
        key = jax.random.key(seed)
        k1, k2, k3 = jax.random.split(key, 3)
        x = jax.random.normal(k1, (B, N, D), dtype=jnp.float32)
        spatial = jax.random.normal(k2, (D, D), dtype=jnp.float32) * 0.02
        freq = jnp.fft.fft(spatial, axis=-1)
        k = int(D * SPARSITY)
        mag = jnp.abs(freq)
        kth = jax.lax.top_k(mag, k)[0][:, -1:]
        w_sparse = jnp.where(mag >= kth, freq, 0.0 + 0j)
        bias = jax.random.normal(k3, (D,), dtype=jnp.float32) * 0.01
        return {'x': x, 'w_freq_real': jnp.real(w_sparse).astype(jnp.float32), 'w_freq_imag': jnp.imag(w_sparse).astype(jnp.float32), 'bias': bias}
    _L0_ffn_all = _L0_ffn_setup()
    _L0_ffn_in = {k: v for k, v in _L0_ffn_all.items() if k in ('w_freq_real', 'w_freq_imag', 'bias')}
    del _L0_ffn_all

    def _L1_xattn_setup():
        import jax, jax.numpy as jnp
        import numpy as np
        B, LQ, LK = (8, 512, 512)
        QD, KD, VD = (256, 128, 128)
        key = jax.random.key(seed)
        ks = jax.random.split(key, 9)
        s = 0.02
        return {'query': jax.random.normal(ks[0], (B, LQ, QD), jnp.float32), 'key': jax.random.normal(ks[1], (B, LK, KD), jnp.float32), 'value': jax.random.normal(ks[2], (B, LK, VD), jnp.float32), 'Wq': jax.random.normal(ks[3], (QD, QD), jnp.float32) * s, 'bq': jnp.zeros((QD,), jnp.float32), 'Wk': jax.random.normal(ks[4], (KD, QD), jnp.float32) * s, 'bk': jnp.zeros((QD,), jnp.float32), 'Wv': jax.random.normal(ks[5], (VD, QD), jnp.float32) * s, 'bv': jnp.zeros((QD,), jnp.float32)}
    _L1_xattn_all = _L1_xattn_setup()
    _L1_xattn_in = {k: v for k, v in _L1_xattn_all.items() if k in ('Wq', 'bq', 'Wk', 'bk', 'Wv', 'bv')}
    del _L1_xattn_all

    def _L1_attn_setup():
        import jax, jax.numpy as jnp
        import numpy as np
        D_MODEL = 256
        N_HEADS = 16
        key = jax.random.key(seed)
        ks = jax.random.split(key, 9)
        B, L, D = (4, 512, D_MODEL)
        s = 1.0 / np.sqrt(D)
        return {'x': jax.random.normal(ks[0], (B, L, D), dtype=jnp.float32), 'wq': jax.random.normal(ks[1], (D, D), dtype=jnp.float32) * s, 'bq': jnp.zeros((D,), dtype=jnp.float32), 'wk': jax.random.normal(ks[2], (D, D), dtype=jnp.float32) * s, 'bk': jnp.zeros((D,), dtype=jnp.float32), 'wv': jax.random.normal(ks[3], (D, D), dtype=jnp.float32) * s, 'bv': jnp.zeros((D,), dtype=jnp.float32), 'wo': jax.random.normal(ks[4], (D, D), dtype=jnp.float32) * s, 'bo': jnp.zeros((D,), dtype=jnp.float32)}
    _L1_attn_all = _L1_attn_setup()
    _L1_attn_in = {k: v for k, v in _L1_attn_all.items() if k in ('wq', 'bq', 'wk', 'bk', 'wv', 'bv', 'wo', 'bo')}
    del _L1_attn_all

    def _L1_ffn_setup():
        import jax, jax.numpy as jnp
        import numpy as np
        B, T, D = (2, 512, 256)
        E, DFF, TOPK = (8, 1024, 2)
        TEMPERATURE = 1.0
        key = jax.random.key(seed)
        k_x, k_w1, k_w2, k_r = jax.random.split(key, 4)
        x = jax.random.normal(k_x, (B, T, D), dtype=jnp.float32)
        W1 = jax.random.normal(k_w1, (E, DFF, D), dtype=jnp.float32) * 0.02
        W2 = jax.random.normal(k_w2, (E, D, DFF), dtype=jnp.float32) * 0.02
        Wr = jax.random.normal(k_r, (E, D), dtype=jnp.float32) * 0.02
        return {'x': x, 'W1': W1, 'W2': W2, 'Wr': Wr}
    _L1_ffn_all = _L1_ffn_setup()
    _L1_ffn_in = {k: v for k, v in _L1_ffn_all.items() if k in ('W1', 'W2', 'Wr')}
    del _L1_ffn_all
    return {'x': x, 'ctx_512': ctx_512, 'L0_xattn_Wq': _L0_xattn_in['Wq'], 'L0_xattn_Wkv': _L0_xattn_in['Wkv'], 'L0_xattn_Wo': _L0_xattn_in['Wo'], 'L0_attn_conv_w': _L0_attn_in['conv_w'], 'L0_attn_conv_b': _L0_attn_in['conv_b'], 'L0_attn_A': _L0_attn_in['A'], 'L0_attn_Bp_w': _L0_attn_in['Bp_w'], 'L0_attn_Bp_b': _L0_attn_in['Bp_b'], 'L0_attn_Cp_w': _L0_attn_in['Cp_w'], 'L0_attn_Cp_b': _L0_attn_in['Cp_b'], 'L0_attn_D': _L0_attn_in['D'], 'L0_attn_gate_w': _L0_attn_in['gate_w'], 'L0_attn_gate_b': _L0_attn_in['gate_b'], 'L0_attn_out_w': _L0_attn_in['out_w'], 'L0_attn_out_b': _L0_attn_in['out_b'], 'L0_attn_ln_g': _L0_attn_in['ln_g'], 'L0_attn_ln_b': _L0_attn_in['ln_b'], 'L0_ffn_w_freq_real': _L0_ffn_in['w_freq_real'], 'L0_ffn_w_freq_imag': _L0_ffn_in['w_freq_imag'], 'L0_ffn_bias': _L0_ffn_in['bias'], 'L1_xattn_Wq': _L1_xattn_in['Wq'], 'L1_xattn_bq': _L1_xattn_in['bq'], 'L1_xattn_Wk': _L1_xattn_in['Wk'], 'L1_xattn_bk': _L1_xattn_in['bk'], 'L1_xattn_Wv': _L1_xattn_in['Wv'], 'L1_xattn_bv': _L1_xattn_in['bv'], 'L1_attn_wq': _L1_attn_in['wq'], 'L1_attn_bq': _L1_attn_in['bq'], 'L1_attn_wk': _L1_attn_in['wk'], 'L1_attn_bk': _L1_attn_in['bk'], 'L1_attn_wv': _L1_attn_in['wv'], 'L1_attn_bv': _L1_attn_in['bv'], 'L1_attn_wo': _L1_attn_in['wo'], 'L1_attn_bo': _L1_attn_in['bo'], 'L1_ffn_W1': _L1_ffn_in['W1'], 'L1_ffn_W2': _L1_ffn_in['W2'], 'L1_ffn_Wr': _L1_ffn_in['Wr']}

def reference(x, ctx_512, L0_xattn_Wq, L0_xattn_Wkv, L0_xattn_Wo, L0_attn_conv_w, L0_attn_conv_b, L0_attn_A, L0_attn_Bp_w, L0_attn_Bp_b, L0_attn_Cp_w, L0_attn_Cp_b, L0_attn_D, L0_attn_gate_w, L0_attn_gate_b, L0_attn_out_w, L0_attn_out_b, L0_attn_ln_g, L0_attn_ln_b, L0_ffn_w_freq_real, L0_ffn_w_freq_imag, L0_ffn_bias, L1_xattn_Wq, L1_xattn_bq, L1_xattn_Wk, L1_xattn_bk, L1_xattn_Wv, L1_xattn_bv, L1_attn_wq, L1_attn_bq, L1_attn_wk, L1_attn_bk, L1_attn_wv, L1_attn_bv, L1_attn_wo, L1_attn_bo, L1_ffn_W1, L1_ffn_W2, L1_ffn_Wr):
    import jax
    import jax.numpy as jnp

    def _L0_xattn_ref(x, z, Wq, Wkv, Wo):
        import jax, jax.numpy as jnp
        import numpy as np
        DIM = 256
        LATENT_DIM = 128
        NUM_HEADS = 16
        HEAD_DIM = DIM // NUM_HEADS
        SCALE = HEAD_DIM ** (-0.5)
        B, xN, _ = x.shape
        _, zN, _ = z.shape
        Q = (x @ Wq.T).reshape(B, xN, NUM_HEADS, HEAD_DIM)
        KV = (z @ Wkv.T).reshape(B, zN, 2, NUM_HEADS, HEAD_DIM)
        K = KV[:, :, 0]
        V = KV[:, :, 1]
        attn = jnp.einsum('bqhd,bkhd->bhqk', Q, K) * SCALE
        attn = jax.nn.softmax(attn, axis=-1)
        O = jnp.einsum('bhqk,bkhd->bqhd', attn, V).reshape(B, xN, DIM)
        return O @ Wo.T

    def _L0_attn_ref(x, conv_w, conv_b, A, Bp_w, Bp_b, Cp_w, Cp_b, D, gate_w, gate_b, out_w, out_b, ln_g, ln_b):
        import jax, jax.numpy as jnp
        import numpy as np
        import math
        BATCH, SEQ = (8, 1024)
        D_MODEL, D_STATE, D_CONV = (256, 16, 4)
        LN_EPS = 1e-05
        residual = x
        xT = jnp.transpose(x, (0, 2, 1))
        conv = jax.lax.conv_general_dilated(xT, conv_w, window_strides=(1,), padding=[(D_CONV - 1, 0)], feature_group_count=D_MODEL, dimension_numbers=('NCH', 'OIH', 'NCH'))
        u = jax.nn.silu(jnp.transpose(conv + conv_b[None, :, None], (0, 2, 1)))
        Bt = u @ Bp_w.T + Bp_b
        Ct = u @ Cp_w.T + Cp_b
        A_exp = jnp.exp(-jnp.exp(A))

        def step(h, inp):
            ut, bt, ct = inp
            h = h * A_exp + ut[:, :, None] * bt[:, None, :]
            y = jnp.einsum('bdn,bn->bd', h, ct) + D * ut
            return (h, y)
        h0 = jnp.zeros((x.shape[0], D_MODEL, D_STATE), x.dtype)
        xs = (jnp.swapaxes(u, 0, 1), jnp.swapaxes(Bt, 0, 1), jnp.swapaxes(Ct, 0, 1))
        _, ys = jax.lax.scan(step, h0, xs)
        y = jnp.swapaxes(ys, 0, 1)
        y = y * jax.nn.silu(x @ gate_w.T + gate_b)
        y = y @ out_w.T + out_b
        z = y + residual
        mu = jnp.mean(z, axis=-1, keepdims=True)
        var = jnp.var(z, axis=-1, keepdims=True)
        return (z - mu) / jnp.sqrt(var + LN_EPS) * ln_g + ln_b

    def _L0_ffn_ref(x, w_freq_real, w_freq_imag, bias):
        import jax, jax.numpy as jnp
        import numpy as np
        B, N, D = (4, 512, 256)
        SPARSITY = 0.01
        w = jax.lax.complex(w_freq_real, w_freq_imag)
        x_freq = jnp.fft.fft(x, axis=-1)
        y_freq = jnp.einsum('bnd,do->bno', x_freq, w)
        y = jnp.real(jnp.fft.ifft(y_freq, axis=-1))
        return y + bias

    def _L1_xattn_ref(query, key, value, Wq, bq, Wk, bk, Wv, bv):
        import jax, jax.numpy as jnp
        import numpy as np
        B, LQ, LK = (8, 512, 512)
        QD, KD, VD = (256, 128, 128)
        q = jnp.einsum('bld,de->ble', query, Wq) + bq
        k = jnp.einsum('bld,de->ble', key, Wk) + bk
        v = jnp.einsum('bld,de->ble', value, Wv) + bv
        scores = jnp.einsum('bqe,bke->bqk', q, k)
        attn = jax.nn.softmax(scores, axis=-1)
        out = jnp.einsum('bqk,bke->bqe', attn, v)
        return out

    def _L1_attn_ref(x, wq, bq, wk, bk, wv, bv, wo, bo):
        import jax, jax.numpy as jnp
        import numpy as np
        D_MODEL = 256
        N_HEADS = 16
        B, L, D = x.shape
        H = N_HEADS
        d_k = D // H
        scale = 1.0 / np.sqrt(d_k).astype(np.float32)

        def proj(w, b):
            return (x @ w.T + b).reshape(B, L, H, d_k).transpose(0, 2, 1, 3)
        Q = proj(wq, bq)
        K = proj(wk, bk)
        V = proj(wv, bv)
        scores = jnp.einsum('bhqd,bhkd->bhqk', Q, K) * scale
        u = min(L, max(1, int(np.log(L))))
        top_u = jax.lax.top_k(scores.max(axis=-1), u)[1]
        q_sel = jnp.take_along_axis(Q, top_u[..., None], axis=2)
        attn = jax.nn.softmax(jnp.einsum('bhud,bhkd->bhuk', q_sel, K) * scale, axis=-1)
        ctx = jnp.einsum('bhuk,bhkd->bhud', attn, V)
        bi = jnp.arange(B)[:, None, None]
        hi = jnp.arange(H)[None, :, None]
        padded = jnp.zeros((B, H, L, d_k), dtype=x.dtype).at[bi, hi, top_u].set(ctx)
        out = padded.transpose(0, 2, 1, 3).reshape(B, L, D)
        return out @ wo.T + bo

    def _L1_ffn_ref(x, W1, W2, Wr):
        import jax, jax.numpy as jnp
        import numpy as np
        B, T, D = (2, 512, 256)
        E, DFF, TOPK = (8, 1024, 2)
        TEMPERATURE = 1.0
        logits = jnp.einsum('btd,ed->bte', x, Wr)
        probs = jax.nn.softmax(logits / TEMPERATURE, axis=-1)
        topk_vals, topk_idx = jax.lax.top_k(probs, TOPK)
        router_weights = topk_vals / topk_vals.sum(-1, keepdims=True)
        one_hot = jax.nn.one_hot(topk_idx, E, dtype=x.dtype)
        gate = jnp.einsum('btk,btke->bte', router_weights, one_hot)
        h = jax.nn.silu(jnp.einsum('btd,efd->btef', x, W1))
        y = jnp.einsum('btef,edf->bted', h, W2)
        out = jnp.einsum('bte,bted->btd', gate, y)
        return out
    x = x + _L0_xattn_ref(_layernorm(x, axis=-1), ctx_512, L0_xattn_Wq, L0_xattn_Wkv, L0_xattn_Wo)
    x = x + _L0_attn_ref(_layernorm(x, axis=-1), L0_attn_conv_w, L0_attn_conv_b, L0_attn_A, L0_attn_Bp_w, L0_attn_Bp_b, L0_attn_Cp_w, L0_attn_Cp_b, L0_attn_D, L0_attn_gate_w, L0_attn_gate_b, L0_attn_out_w, L0_attn_out_b, L0_attn_ln_g, L0_attn_ln_b)
    x = x + _L0_ffn_ref(_layernorm(x, axis=-1), L0_ffn_w_freq_real, L0_ffn_w_freq_imag, L0_ffn_bias)
    x = x + _L1_xattn_ref(_layernorm(x, axis=-1), ctx_512, ctx_512, L1_xattn_Wq, L1_xattn_bq, L1_xattn_Wk, L1_xattn_bk, L1_xattn_Wv, L1_xattn_bv)
    x = x + _L1_attn_ref(_layernorm(x, axis=-1), L1_attn_wq, L1_attn_bq, L1_attn_wk, L1_attn_bk, L1_attn_wv, L1_attn_bv, L1_attn_wo, L1_attn_bo)
    x = x + _L1_ffn_ref(_layernorm(x, axis=-1), L1_ffn_W1, L1_ffn_W2, L1_ffn_Wr)
    return x

_drawn_inputs = setup_inputs


def setup_inputs(seed=0):
    import zlib

    import numpy as np

    out = dict(_drawn_inputs(seed))
    spreads = {'L0_attn_Bp_b': (0.0, 0.1),
     'L0_attn_Cp_b': (0.0, 0.1),
     'L0_attn_D': (1.0, 0.6),
     'L0_attn_gate_b': (0.0, 0.1),
     'L0_attn_out_b': (0.0, 0.1),
     'L0_attn_ln_g': (1.0, 0.2),
     'L0_attn_ln_b': (0.0, 0.1),
     'L1_xattn_bq': (0.0, 0.8),
     'L1_xattn_bk': (0.0, 0.8),
     'L1_xattn_bv': (0.0, 0.1),
     'L1_attn_bq': (0.0, 0.733),
     'L1_attn_bk': (0.0, 0.527),
     'L1_attn_bv': (0.0, 0.8),
     'L1_attn_bo': (0.0, 0.1)}
    factors = {'L0_ffn_bias': 8.0}
    for name, (base, spread) in spreads.items():
        noise = np.random.default_rng([zlib.crc32(name.encode()), seed]).standard_normal(out[name].shape)
        drawn = base * np.exp(spread * noise) if base else spread * noise
        out[name] = jnp.asarray(drawn.astype(out[name].dtype))
    for name, factor in factors.items():
        out[name] = (out[name] * factor).astype(out[name].dtype)
    return out
```

```python
from contextlib import ExitStack

import numpy as np

import concourse.bass as bass
from concourse import mybir

F32 = mybir.dt.float32
F32R = mybir.dt.float32r
U32 = mybir.dt.uint32
ALU = mybir.AluOpType
ACT = mybir.ActivationFunctionType
AX = mybir.AxisListType

P = 128
B, L, D = 2, 256, 256
T = B * L
NT = T // P
QT = L // P
KF = D // P
S, LAT = 4096, 128
H, DH = 16, 16
SCALE = DH ** -0.5
EPS = 1e-5
NST, TAPS = 16, 4
E, F = 8, 1024
FT = F // P
TOPU = 5
HU = H * TOPU

GH = 4
NG = B * H // GH
KT = S // P
CK = 1024
NC = S // CK
PK = 512
NPC = B * S // PK
RB = 3 * DH
RS = 2 * RB
VW = GH * (DH + 1)
UNITS = 32
PRING = 4
TURNS = {0: 1, 1: 2, 3: 3, 4: 4, 5: 5, 6: 6}
CRED = 16 * 12


VECS = ("L0_attn_conv_b", "L0_attn_D", "L0_attn_gate_b", "L1_xattn_bq", "L1_xattn_bk", "L1_attn_bq", "L1_attn_bk")
ROWS = ("L0_attn_out_b", "L0_attn_ln_g", "L0_attn_ln_b", "L0_ffn_bias", "L1_xattn_bv", "L1_attn_bv", "L1_attn_bo",
        "L1_attn_bq")


def perceiver(nc, a):
    ctx = ExitStack()
    with ctx:
        def sb(name, shape, dt=F32):
            return ctx.enter_context(nc.sbuf_tensor(name, shape, dt))

        def sem(name):
            return ctx.enter_context(nc.semaphore(name))

        ps = ctx.enter_context(nc.psum_tensor("ps", [P, 8, 512], F32))

        k_stack = sb("k_stack", [P, 2, 2, S], F32R)
        qm_stack = sb("qm_stack", [P, 2, 2, 2 * L], F32R)
        qe_stack = sb("qe_stack", [P, 2, 2, 2 * L], F32R)
        k_hi = sb("k_hi", [P, 2, 2, PK], F32R)
        k_lo = sb("k_lo", [P, 2, 2, PK], F32R)
        nm_t = sb("nm", [P, 8], F32R)
        ident_r = sb("ident_r", [P, P], F32R)
        bc_hl = sb("bc_hl", [64, T], F32R)
        sel_n = sb("sel_n", [64, 2 * NST], F32R)
        nm4 = sb("nm4", [1, L], F32R)
        ones_r = sb("ones_r", [1, P], F32R)
        q_hi = k_stack[:, 1, 0, 0:2 * T].rearrange("p (c t) -> p c t", c=2)
        q_lo = k_stack[:, 1, 0, 2 * T:4 * T].rearrange("p (c t) -> p c t", c=2)

        ident = sb("ident", [P, P])
        X = sb("X", [P, NT, D])
        xn = sb("xn", [P, NT, D])
        xnT = sb("xnT", [P, KF, T])
        stats = sb("stats", [P, NT, 6])
        mv = sb("mv", [P, NT, 2])
        sd = sb("sd", [P, NT])
        rstd = sb("rstd", [P, NT])
        w_a = sb("w_a", [P, KF, D])
        w_kv = sb("w_kv", [P, 2 * D])
        w_o = sb("w_o", [P, NG // B, D])
        w_gate = sb("w_gate", [P, KF, D])
        w_out = sb("w_out", [P, KF, D])
        bc_w = sb("bc_w", [P, KF, 64])
        bc_b = sb("bc_b", [64, 1])
        conv_w = sb("conv_w", [P, KF, TAPS])
        vecs = sb("vecs", [P, len(VECS), KF])
        a_log = sb("a_log", [P, KF, NST])
        a_dec = sb("a_dec", [P, KF, NST])
        rows = sb("rows", [P, len(ROWS), D])
        m_dft = sb("m_dft", [P, KF, D])
        w_q1 = sb("w_q1", [P, KF, D])
        w_k1 = sb("w_k1", [P, KF, LAT])
        w_v1 = sb("w_v1", [P, D])
        w5 = sb("w5", [P, 4, KF, D])
        w_r = sb("w_r", [P, KF, E])
        head_mask = sb("head_mask", [P, 8])
        arena = sb("arena", [P, 13568])

        CB, DD, GB, BQ1, BK1, BQ5, BK5 = range(len(VECS))
        OB, LG, LB, FB, BV1, BV5, BO5, BQ5R = range(len(ROWS))

        off = [0]

        def carve(*shape):
            n = int(np.prod(shape))
            v = arena[:, off[0]:off[0] + n]
            off[0] += n
            assert off[0] <= 13568, off[0]
            names = "abcd"[:len(shape)]
            if len(shape) == 1:
                return v
            return v.rearrange("p (%s) -> p %s" % (" ".join(names), " ".join(names)),
                               **{c: s for c, s in zip(names[1:], shape[1:])})

        v_grp = carve(2, KT, VW)
        probs = carve(PRING, 512)
        o_raw = carve(NG + 1, L)
        cx = carve(2, PK)
        v_stage = carve(2, NG // B, PK // P, VW)
        mxp = carve(8, NC)
        off[0] = 0
        dft = carve(5, KF, D)
        wf = carve(2, KF, D)
        uf = carve(2, KF, D)
        assert off[0] <= 2 * KT * VW + PRING * 512 + (NG + 1) * L
        off[0] = 2 * KT * VW + PRING * 512 + (NG + 1) * L
        o_sum = carve(2, L)
        o_n = carve(NG, L)
        head_ones_t = sb("head_ones", [P, P])
        head_ones = head_ones_t[:, :]
        off[0] = 0
        xpad = carve(KF, B, L + TAPS - 1)
        conv = carve(KF, T)
        u = carve(KF, T)
        gate = carve(KF, T)
        b_in = carve(4, T)
        h_st = carve(4, T)
        c_bc = carve(2, T)
        hc = carve(4, T)
        yT = carve(KF, T)
        bcf = carve(T)
        off[0] = 0
        ctxT = carve(S)
        ctxN = carve(KT, LAT)
        q1T = carve(KF, T)
        qpT = carve(T)
        qbk = carve(8)
        p4 = carve(2, 4 * L)
        psumP = carve(4 * L)
        mx4 = carve(QT, 8)
        ones = carve(P)
        ocT = carve(L)
        rs4 = carve(L)
        nm4f = carve(QT)
        off[0] = 0
        qT5 = carve(KF, T)
        kT5 = carve(KF, T)
        qn5 = carve(NT, D)
        vn5 = carve(NT, D)
        mx5 = carve(QT, B * H)
        mT5 = carve(L)
        i5 = carve(16)
        idx5 = carve(8)
        c5 = carve(2, 16)
        s5 = carve(2, 16)
        oneT = carve(B, L)
        oneN = carve(B, QT, HU)
        qsel = carve(B, KF, HU)
        p5 = carve(B, L)
        pT5 = carve(B, QT, HU)
        sum5 = carve(B)
        rs5 = carve(B)
        om5 = carve(B, D)
        oT5 = carve(KF, T)
        qm5 = carve(4, 4, P)
        off[0] = 0
        w1 = carve(2, KF, F)
        w2 = carve(2, FT, D)
        hT = carve(FT, T)
        gates_t = sb("gates", [P, NT, E])
        gates = gates_t[:, :, :]
        r6_t = sb("r6", [P, NT, 8])
        r6 = r6_t[:, :, :]
        p6_t = sb("p6", [P, NT, 8])
        p6 = p6_t[:, :, :]
        t6_t = sb("t6", [P, NT, 8])
        t6 = t6_t[:, :, :]
        i6_t = sb("i6", [P, NT, 8])
        i6 = i6_t[:, :, :]
        f6_t = sb("f6", [P, NT, 8])
        f6 = f6_t[:, :, :]
        g6_t = sb("g6", [P, NT, 8])
        g6 = g6_t[:, :, :]
        c6_t = sb("c6", [P, NT, 8])
        c6 = c6_t[:, :, :]
        iota_t = sb("iota", [P, L])
        iota5, iota6 = iota_t[:, :], iota_t[:, 0:E]

        umask3 = sb("umask3", [HU, H, TOPU])
        umask = sb("umask", [HU, 8])
        sel_e = sb("sel_e", [2 * H, B, HU])
        bd5 = sb("bd5", [P, KF, HU])
        bdT5 = sb("bdT5", [HU, D])

        qd = nc.dram_tensor("q_parts", [NG, 2, GH * DH, L], F32, kind="Internal").ap()
        kd = nc.dram_tensor("k_parts", [NG, 2, GH * DH, S], F32, kind="Internal").ap()
        vd = nc.dram_tensor("v_parts", [NG, P, KT, VW], F32, kind="Internal").ap()

        sems = {}

        def s(name):
            if name not in sems:
                sems[name] = ctx.enter_context(nc.semaphore(name))
            return sems[name]

        block = ctx.enter_context(nc.Block())

        def f32(v):
            return v.bitcast(F32)

        def scaled_rows(v, n):
            return v.unsqueeze(1).to_broadcast([P, n, D])

        @block.sync
        def _(sp):
            for par in range(2):
                sp.sem_inc(s(f"st_out{par}"), CRED)
            sp.dma_start(X[:, :, :], a["x"].rearrange("(j p) f -> p j f", p=P)).then_inc(s("x_in"), 16)
            sp.dma_start(w_kv[:, :], a["wkvT"]).then_inc(s("w0_in"), 16)
            sp.dma_start(w_a[:, :, :], a["wqT"].rearrange("(c p) n -> p c n", p=P)).then_inc(s("w0_in"), 16)
            for n in range(2):
                sp.dma_start(cx[:, n, :], a["ctxT"][:, n * PK:(n + 1) * PK]).then_inc(s(f"cx_in{n}"), 16)

            sp.wait_ge(s("q_hi_ready"), KF)
            sp.wait_ge(s("q_lo_ready"), KF)
            for g in range(NG):
                b, c, r = g // 4, (g % 4) // 2, 64 * (g % 2)
                for i, part in enumerate((q_hi, q_lo)):
                    sp.dma_start(qd[g, i], f32(part[r:r + 64, c, b * L:(b + 1) * L])).then_inc(s("q_out"), 16)

            def load_ctx(n, par):
                sp.dma_start(cx[:, par, :], a["ctxT"][:, bass.ds(n * PK, PK)]).then_inc(s(f"cx_in{par}"), 16)

            def store_parts(b, nb, n, par):
                sp.wait_ge(s("kl_done"), 2 * n + 2 + 4)
                sp.wait_ge(s("v_done"), 2 * n + 2 + 4)
                for g in range(4):
                    for i, part in enumerate((k_hi, k_lo)):
                        sp.dma_start(kd[b * 4 + g, i, :, bass.ds(nb * PK, PK)],
                                     f32(part[64 * (g % 2):64 * (g % 2) + 64, par, g // 2, :])
                                     ).then_inc(s(f"st_out{par}"), 16)
                for g in range(4):
                    sp.dma_start(vd[b * 4 + g, :, bass.ds(nb * 4, 4), :],
                                 v_stage[:, par, g, :, :]).then_inc(s(f"st_out{par}"), 16)

            for b in range(B):
                with sp.Fori(0, 4 if b == 0 else 3) as i:
                    for par in range(2):
                        n = (i + 4 * b) * 2 + par
                        sp.wait_ge(s("kv_ready"), 4 * n + 4)
                        load_ctx(n + 2, par)
                        store_parts(b, i * 2 + par, n, par)
            for par in range(2):
                store_parts(1, 6 + par, NPC - 2 + par, par)

            def load_q(buf, name, g, par):
                for ab in range(2):
                    for blk, hl in enumerate((0, 0, 1)):
                        r = ab * RB + blk * DH
                        src = qd[bass.ds(g, 1), hl].rearrange("g (r a d) q -> d (g r) a q", a=2, d=DH)[:, :, ab, :]
                        sp.dma_start(f32(buf[r:r + DH, par, :, ab * L:(ab + 1) * L]), src).then_inc(s(f"{name}{par}"), 16)

            def load_k(g, par, c):
                for ab in range(2):
                    for blk, hl in enumerate((0, 1, 0)):
                        r = ab * RB + blk * DH
                        src = kd[bass.ds(g, 1), hl, :, c * CK:(c + 1) * CK].rearrange(
                            "g (r a d) k -> d (g r) a k", a=2, d=DH)[:, :, ab, :]
                        sp.dma_start(f32(k_stack[r:r + DH, par, :, c * CK:(c + 1) * CK]), src
                                     ).then_inc(s(f"ks_in{par}{c}"), 16)

            def load_v(g, par):
                sp.dma_start(v_grp[:, par, :, :], vd[bass.ds(g, 1)].rearrange("g p k v -> p (g k) v")
                             ).then_inc(s(f"vs_in{par}"), 16)

            sp.wait_ge(s("q_out"), 16 * 2 * NG)
            for par in range(2):
                sp.wait_ge(s(f"st_out{par}"), 16 * 12 * NPC // 2 + CRED)
            sp.wait_ge(s("q_zero"), 2)
            sp.wait_ge(s("dft_done"), 1)
            for g in range(2):
                load_q(qm_stack, "qm_in", g, g)
                for c in range(NC):
                    load_k(g, g, c)
                load_q(qe_stack, "qe_in", g, g)
                load_v(g, g)

            with sp.Fori(0, NG // 2 - 1) as i:
                for par in range(2):
                    g = i * 2 + par
                    sp.wait_ge(s("mx_ready"), (g + 1) * UNITS)
                    load_q(qm_stack, "qm_in", g + 2, par)
                    for c in range(NC):
                        sp.wait_ge(s("s_ready"), 2 * KT * g + 2 * (KT // NC) * (c + 1))
                        load_k(g + 2, par, c)
                    load_q(qe_stack, "qe_in", g + 2, par)
                    sp.wait_ge(s("pv_done"), KT * (g + 1) + 2)
                    load_v(g + 2, par)

            for b in range(B):
                if b == 0:
                    sp.wait_ge(s("y2_ready"), 1)
                else:
                    sp.wait_ge(s("oc_ready"), 1)
                sp.dma_start(ctxT, a["ctxT"][:, b * S:(b + 1) * S]).then_inc(s("c4_in"), 16)
                sp.dma_start(ctxN, a["ctx"][b].rearrange("(k p) l -> p k l", p=P)).then_inc(s("c4_in"), 16)

            def load_expert(e, par):
                sp.dma_start(w1[:, par, :, :], a["w1T"][bass.ds(e, 1)].rearrange("e (c p) f -> p (e c) f", p=P)
                             ).then_inc(s(f"w1_in{par}"), 16)
                sp.dma_start(w2[:, par, :, :], a["w2T"][bass.ds(e, 1)].rearrange("e (c p) d -> p (e c) d", p=P)
                             ).then_inc(s(f"w2_in_{par}"), 16)

            sp.wait_ge(s("a5_done"), 1)
            for e in range(2):
                load_expert(e, e)
            with sp.Fori(0, E // 2 - 1) as i:
                for par in range(2):
                    sp.wait_ge(s("y_ready"), NT * (2 * i + par + 1) + NT)
                    load_expert(2 * i + par + 2, par)
            sp.wait_ge(s("x_done"), 1)
            sp.dma_start(a["out"].rearrange("(j p) f -> p j f", p=P), X[:, :, :]).then_inc(s("out_done"), 16)
            sp.wait_ge(s("out_done"), 16)

        @block.gpsimd
        def _(pool):
            steps = [0]

            def step(ins):
                steps[0] += 1
                ins.then_inc(s("pool_step"), 1)
                pool.wait_ge(s("pool_step"), steps[0])

            def onezero(view, conds, fill=0.0):
                step(pool.memset(view, 1.0))
                for op, base, pat, mul in conds:
                    step(pool.affine_select(out=view, in_=view, compare_op=op, fill=fill, base=base,
                                            pattern=pat, channel_multiplier=mul))

            onezero(ident[:, :], [(ALU.is_equal, 0, [[-1, P]], 1)])
            step(pool.memset(f32(ident_r[:, :]), 1.0))
            step(pool.affine_select(out=ident_r[:, :], in_=f32(ident_r[:, :]), compare_op=ALU.is_equal, fill=0.0,
                                    base=0, pattern=[[-1, P]], channel_multiplier=1))
            pool.memset(f32(qm_stack[:, :, :, :]), 0.0).then_inc(s("q_zero"), 1)
            pool.wait_ge(s("q_zero"), 1)
            pool.memset(f32(qe_stack[:, :, :, :]), 0.0).then_inc(s("q_zero"), 1)
            pool.wait_ge(s("q_zero"), 2)
            step(pool.memset(v_stage, 1.0))
            pool.memset(f32(k_stack[RS:RS + 1, 0, :, :]), 1.0).then_inc(s("ones_rows"), 1)
            pool.wait_ge(s("ones_rows"), 1)
            step(pool.memset(w_o[:, :, :], 0.0))
            pool.sem_inc(s("pool_ready"), 1)
            for j in range(GH):
                pool.dma_start(w_o[32 * j:32 * j + DH, :, :],
                               a["woT"].rearrange("(g j d) o -> j d g o", j=GH, d=DH)[j]).then_inc(s("wo_in"), 16)
            step(pool.memset(head_ones, 1.0))
            hv = head_ones.rearrange("p (g c) -> p g c", g=4)
            step(pool.affine_select(out=hv, in_=hv, compare_op=ALU.is_equal, fill=0.0, base=-DH,
                                    pattern=[[-32, 4], [0, 32]], channel_multiplier=1))
            onezero(head_mask[:, :], [(ALU.is_ge, 0, [[-DH, 8]], 1), (ALU.is_ge, DH - 1, [[DH, 8]], -1)])
            sn = f32(sel_n[:, :])
            step(pool.memset(sn[0:32, :], 1.0))
            step(pool.memset(sn[32:64, :], 1.0))
            for r in (0, 32):
                step(pool.affine_select(out=sel_n[r:r + 32, :], in_=sn[r:r + 32, :], compare_op=ALU.is_equal,
                                        fill=0.0, base=0, pattern=[[-1, 32]], channel_multiplier=1))
            step(pool.memset(f32(ones_r[:, :]), 1.0))
            onezero(umask3[:, :, :], [(ALU.is_equal, 0, [[-TOPU, H], [-1, TOPU]], 1)])
            onezero(sel_e[:, :, :].rearrange("p b (h u) -> p b h u", u=TOPU),
                    [(ALU.is_equal, 0, [[-H, B], [-1, H], [0, TOPU]], 1)])
            onezero(bd5[:, :, :].rearrange("p c (h u) -> p c h u", u=TOPU),
                    [(ALU.is_ge, 0, [[P, KF], [-DH, H], [0, TOPU]], 1),
                     (ALU.is_ge, DH - 1, [[-P, KF], [DH, H], [0, TOPU]], -1)])
            onezero(bdT5[:, :].rearrange("p (h d) -> p h d", d=DH),
                    [(ALU.is_ge, 0, [[-TOPU, H], [0, DH]], 1), (ALU.is_ge, TOPU - 1, [[TOPU, H], [0, DH]], -1)])
            pool.wait_ge(s("q_out"), 16 * 2 * NG)
            pool.memset(f32(k_stack[RS:RS + 1, 1, :, :]), 1.0).then_inc(s("ones_rows"), 1)
            pool.wait_ge(s("ones_rows"), 2)

            pool.sem_inc(s("masks_ready"), 1)

            k = 0
            for n in range(NST):
                for c in range(KF):
                    pool.wait_ge(s("c_bc_ready"), n + 1)
                    pool.wait_ge(s("h_ready"), k + 1)
                    if k >= 4:
                        pool.wait_ge(s("hc_used"), k - 3)
                    pool.tensor_tensor(hc[:, k % 4, :], h_st[:, k % 4, :], c_bc[:, n % 2, :], ALU.mult
                                       ).then_inc(s("hc_ready"), 1)
                    k += 1

            pool.wait_ge(s("q5_ready"), 1)
            step(pool.iota(iota5.bitcast(mybir.dt.int32), pattern=[[1, L]], base=0, channel_multiplier=0))
            pool.tensor_copy(iota5, iota5.bitcast(mybir.dt.int32)).then_inc(s("iota_ready"), 1)
            for k in range(16):
                b, qt, hq = k // 8, (k // 4) % 2, k % 4
                if k >= 4:
                    pool.wait_ge(s("mx5_ready"), k - 3)
                c = hq // 2
                q = qT5[:, c, b * L + qt * P:b * L + (qt + 1) * P]
                pool.tensor_tensor(qm5[:, k % 4, :, :], q.unsqueeze(1).to_broadcast([P, 4, P]),
                                   head_mask[:, 4 * (hq % 2):4 * (hq % 2) + 4].unsqueeze(2).to_broadcast([P, 4, P]),
                                   ALU.mult).then_inc(s("qm5_ready"), 1)

        @block.scalar
        def _(act):
            act.sem_inc(s("v_done"), 4)
            act.sem_inc(s("p_ready"), 2)
            act.sem_inc(s("o_evac"), 1)
            act.sem_inc(s("hs_ready"), 4)

            act.dma_start(dft[:, :, :, :], a["dft"].rearrange("m (c p) n -> p m c n", p=P)).then_inc(s("dft_in"), 16)
            act.dma_start(wf[:, 0, :, :], a["frT"].rearrange("(c p) n -> p c n", p=P)).then_inc(s("dft_in"), 16)
            act.dma_start(wf[:, 1, :, :], a["fiT"].rearrange("(c p) n -> p c n", p=P)).then_inc(s("dft_in"), 16)

            def std(k):
                act.wait_ge(s("ln_var"), k + 1)
                act.activation(sd[:, :], mv[:, :, 1], ACT.Sqrt).then_inc(s("ln_sd"), 1)

            def xnT_0(k):
                act.wait_ge(s("ln_tr"), TURNS[k])
                act.activation(xnT[:, 0, :], ps[:, 6, :], ACT.Copy).then_inc(s("lnT_a"), 1)

            std(0)
            xnT_0(0)
            for name, dst, src in (
                    ("w2_in", w_gate[:, :, :], a["gateT"].rearrange("(c p) n -> p c n", p=P)),
                    ("w2_in", w_out[:, :, :], a["outT"].rearrange("(c p) n -> p c n", p=P)),
                    ("w2_in", bc_w[:, :, 0:16], a["bpT"].rearrange("(c p) n -> p c n", p=P)),
                    ("w2_in", bc_w[:, :, 16:32], a["cpT"].rearrange("(c p) n -> p c n", p=P)),
                    ("w2_in", bc_w[:, :, 32:48], a["bpT"].rearrange("(c p) n -> p c n", p=P)),
                    ("w2_in", bc_w[:, :, 48:64], a["cpT"].rearrange("(c p) n -> p c n", p=P)),
                    ("w2_in", bc_b[0:16, :], a["bpb"].rearrange("(n o) -> n o", o=1)),
                    ("w2_in", bc_b[16:32, :], a["cpb"].rearrange("(n o) -> n o", o=1)),
                    ("w2_in", bc_b[32:48, :], a["bpb"].rearrange("(n o) -> n o", o=1)),
                    ("w2_in", bc_b[48:64, :], a["cpb"].rearrange("(n o) -> n o", o=1)),
                    ("w2_in", conv_w[:, :, :], a["conv_w"].rearrange("(c p) k -> p c k", p=P)),
                    ("w2_in", a_log[:, :, :], a["a_log"].rearrange("(c p) n -> p c n", p=P)),
                    ("w4_in", w_q1[:, :, :], a["wq1"].rearrange("(c p) n -> p c n", p=P)),
                    ("w4_in", w_k1[:, :, :], a["wk1T"].rearrange("(c p) n -> p c n", p=P)),
                    ("w4_in", w_v1[:, :], a["wv1"]),
                    ("w5_in", w5[:, 0, :, :], a["wq5T"].rearrange("(c p) n -> p c n", p=P)),
                    ("w5_in", w5[:, 1, :, :], a["wk5T"].rearrange("(c p) n -> p c n", p=P)),
                    ("w5_in", w5[:, 2, :, :], a["wv5T"].rearrange("(c p) n -> p c n", p=P)),
                    ("w5_in", w5[:, 3, :, :], a["wo5T"].rearrange("(c p) n -> p c n", p=P)),
                    ("w6_in", w_r[:, :, :], a["wrT"].rearrange("(c p) n -> p c n", p=P))):
                act.dma_start(dst, src).then_inc(s(name), 16)
            act.dma_start(vecs[:, :, :], a["vecs"]).then_inc(s("vec_in"), 16)
            act.dma_start(rows[:, :, :], a["rows"].unsqueeze(0).to_broadcast([P, len(ROWS), D])
                          ).then_inc(s("row_in"), 16)

            for c in range(KF):
                act.wait_ge(s("q_ready"), c + 1)
                act.activation(q_hi[:, c, :], ps[:, 4 + c, :], ACT.Copy).then_inc(s("q_hi_ready"), 1)
            act.wait_ge(s("uf_ready"), 1)
            act.activation(uf[:, :, :, :].rearrange("p a b c -> p (a b c)"),
                           ps[:, 0:2, :].rearrange("p a b -> p (a b)"), ACT.Copy).then_inc(s("uf_done"), 1)

            with act.Fori(0, NPC // 2) as i:
                for par in range(2):
                    n = 2 * i + par
                    for k in range(2):
                        act.wait_ge(s("kv_ready"), 4 * n + k + 1)
                        act.wait_ge(s(f"st_out{par}"), CRED * (i + 1))
                        act.activation(k_hi[:, par, k, :], ps[:, 4 * par + k, :], ACT.Copy).then_inc(s("kh_done"), 1)
                    for k in range(2):
                        act.wait_ge(s("kv_ready"), 4 * n + k + 3)
                        if k == 0 and par == 0:
                            act.wait_ge(s("pool_ready"), 1)
                        for kk in range(2):
                            dst = v_stage[:, par, :, 2 * k + kk, :].rearrange("p g (j v) -> p g j v", v=DH + 1)
                            src = ps[:, 4 * par + 2 + k, kk * D:(kk + 1) * D].rearrange(
                                "p (g j v) -> p g j v", g=4, j=GH)
                            ins = act.activation(dst[:, :, :, 0:DH], src, ACT.Copy)
                        ins.then_inc(s("v_done"), 1)

            def exp_pass(g, par):
                for st in range(KT):
                    for bk in range(2):
                        act.wait_ge(s("s_ready"), 2 * KT * g + 2 * st + bk + 1)
                        act.wait_ge(s("pv_done"), KT * g + st + 1)
                        act.activation(probs[:, (2 * st + bk) % PRING, :], ps[:, 4 + bk, :], ACT.Exp,
                                       scale=SCALE).then_inc(s("p_ready"), 1)
                    if st == 2:
                        if isinstance(g, int) or par == 0:
                            pass
                        act.wait_ge(s("pv_done"), KT * g + 2)
                        act.activation(o_raw[:, bass.ds(g, 1), :], ps[:, 7 - par, 0:L].unsqueeze(1),
                                       ACT.Copy).then_inc(s("o_evac"), 1)

            act.wait_ge(s("pv_zero"), 1)
            with act.Fori(0, NG // 2 - 1) as i:
                for par in range(2):
                    exp_pass(2 * i + par, par)
            for par in range(2):
                exp_pass(NG - 2 + par, par)
            act.wait_ge(s("pv_done"), KT * NG + 2)
            act.activation(o_raw[:, NG, :], ps[:, 7, 0:L], ACT.Copy).then_inc(s("o_evac"), 1)

            act.wait_ge(s("w2_in"), 16 * 12)
            act.activation(a_dec[:, :, :], a_log[:, :, :], ACT.Exp).then_inc(s("act_step"), 1)
            act.wait_ge(s("act_step"), 1)
            act.activation(a_dec[:, :, :], a_dec[:, :, :], ACT.Exp, scale=-1.0).then_inc(s("a_dec_ready"), 1)
            std(1)
            xnT_0(1)
            act.wait_ge(s("vec_in"), 16)
            for c in range(KF):
                act.wait_ge(s("conv_ready"), c + 1)
                act.activation(u[:, c, :], conv[:, c, :], ACT.Silu).then_inc(s("u_ready"), 1)
            for c in range(KF):
                act.wait_ge(s("gate_mm"), c + 1)
                act.activation(gate[:, c, :], ps[:, c, :], ACT.Silu, bias=vecs[:, GB, c:c + 1]
                               ).then_inc(s("gate_ready"), 1)
            for n in range(NST):
                act.wait_ge(s("c_ready"), n + 1)
                if n >= 2:
                    act.wait_ge(s("hc_ready"), 2 * (n - 1))
                act.activation(c_bc[:, n % 2, :], ps[:, 2 + n % 2, :], ACT.Copy).then_inc(s("c_bc_ready"), 1)
            std(2)

            std(3)
            xnT_0(3)

            std(4)
            xnT_0(4)
            for c in range(KF):
                act.wait_ge(s("q1_mm"), c + 1)
                act.activation(q1T[:, c, :], ps[:, c, :], ACT.Identity, bias=vecs[:, BQ1, c:c + 1]
                               ).then_inc(s("q1_ready"), 1)
            for b in range(B):
                for un in range(8):
                    k = b * 8 + un
                    act.wait_ge(s("s4_ready"), k + 1)
                    if k >= 2:
                        act.wait_ge(s("av4_done"), k - 1)
                        act.wait_ge(s("p4_summed"), k - 1)
                    act.activation(p4[:, k % 2, :], ps[:, 4 + 2 * (k % 2):6 + 2 * (k % 2), :].rearrange(
                        "p a b -> p (a b)"), ACT.Exp).then_inc(s("p4_ready"), 1)

            std(5)
            xnT_0(5)
            for c in range(KF):
                act.wait_ge(s("qk5_mm"), c + 1)
                ins = act.activation(qT5[:, c, :], ps[:, c, :], ACT.Identity, bias=vecs[:, BQ5, c:c + 1])
            ins.then_inc(s("q5_ready"), 1)
            for c in range(KF):
                act.wait_ge(s("qk5_mm"), c + 3)
                ins = act.activation(kT5[:, c, :], ps[:, 2 + c, :], ACT.Identity, bias=vecs[:, BK5, c:c + 1])
            ins.then_inc(s("k5_ready"), 1)
            for b in range(B):
                act.wait_ge(s("ss5_ready"), b + 1)
                act.wait_ge(s("nm5_ready"), b + 1)
                act.activation(p5[0:HU, b, :], ps[0:HU, 2 + b, 0:L], ACT.Exp, scale=SCALE, bias=c5[0:HU, b, 0:1],
                               accum_out=sum5[0:HU, b:b + 1]).then_inc(s("p5_ready"), 1)

            std(6)
            xnT_0(6)
            act.wait_ge(s("r_ready"), 1)
            act.activation(p6.rearrange("p a b -> p (a b)"), r6.rearrange("p a b -> p (a b)"), ACT.Exp
                           ).then_inc(s("r_exp"), 1)
            with act.Fori(0, E // 2) as i:
                for par in range(2):
                    e = 2 * i + par
                    for ft in range(FT):
                        act.wait_ge(s("hm_ready"), FT * e + ft + 1)
                        if ft == 0:
                            act.wait_ge(s("y_ready"), NT * e + NT)
                        act.activation(hT[:, ft, :], ps[:, ft % 4, :], ACT.Silu).then_inc(s("hs_ready"), 1)

        @block.tensor
        def _(pe):
            def mm(out, lhsT, rhs, start=True, stop=True):
                return pe.matmul(out, lhsT, rhs, start=start, stop=stop, skip_group_check=True)

            pe.sem_inc(s("pv_done"), 2)
            pe.sem_inc(s("y_ready"), NT)

            def transpose_xn(k):
                pe.wait_ge(s("ln_xn"), TURNS[k])
                for c in range(KF):
                    for j in range(NT):
                        ins = pe.transpose(ps[:, 6 + c, j * P:(j + 1) * P], xn[:, j, c * P:(c + 1) * P], ident[:, :])
                ins.then_inc(s("ln_tr"), 1)
                pe.wait_ge(s("lnT_a"), TURNS[k])
                pe.wait_ge(s("lnT_d"), TURNS[k])

            pe.wait_ge(s("pool_step"), 2)
            transpose_xn(0)
            pe.wait_ge(s("w0_in"), 32)
            for m in range(KF):
                for c in range(KF):
                    ins = mm(ps[:, 4 + m, :], w_a[:, c, m * P:(m + 1) * P], xnT[:, c, :], c == 0, c == KF - 1)
                ins.then_inc(s("q_ready"), 1)

            pe.wait_ge(s("dft_in"), 48)
            terms = (((0, 0), (1, 2)), ((0, 1), (1, 0)))
            for r in range(2):
                for m in range(KF):
                    n = 0
                    for wi, ti in terms[r]:
                        for c in range(KF):
                            ins = mm(ps[:, r, m * D:(m + 1) * D], wf[:, wi, c, m * P:(m + 1) * P], dft[:, ti, c, :],
                                     n == 0, n == 3)
                            n += 1
            ins.then_inc(s("uf_ready"), 1)
            pe.wait_ge(s("uf_done"), 1)
            for m in range(KF):
                n = 0
                for r in range(2):
                    for c in range(KF):
                        ins = mm(ps[:, 2, m * D:(m + 1) * D], dft[:, 3 + r, c, m * P:(m + 1) * P], uf[:, r, c, :],
                                 n == 0, n == 3)
                        n += 1
            ins.then_inc(s("m_mm"), 1)
            pe.wait_ge(s("m_ready"), 1)
            pe.wait_ge(s("q_hi_ready"), KF)
            pe.wait_ge(s("q_lo_ready"), KF)

            with pe.Fori(0, NPC // 2) as i:
                for par in range(2):
                    n = 2 * i + par
                    pe.wait_ge(s(f"cx_in{par}"), 16 * (i + 1))
                    for m in range(2):
                        pe.wait_ge(s("kl_done"), 2 * n + m + 1)
                        mm(ps[:, 4 * par + m, :], w_kv[:, m * P:(m + 1) * P], cx[:, par, :]).then_inc(s("kv_ready"), 1)
                    for m in range(2):
                        pe.wait_ge(s("v_done"), 2 * n + m + 1)
                        for kk in range(2):
                            t = 2 * m + kk
                            ins = mm(ps[:, 4 * par + 2 + m, kk * D:(kk + 1) * D], cx[:, par, t * P:(t + 1) * P],
                                     w_kv[:, D:2 * D])
                        ins.then_inc(s("kv_ready"), 1)

            def max_unit(g, par, un):
                c, j, qt = un // 8, (un % 8) // 2, un % 2
                if un == 0:
                    pe.wait_ge(s(f"qm_in{par}"), 96 * grp(g, par))
                if un % 8 == 0:
                    pe.wait_ge(s(f"ks_in{par}{c}"), 96 * grp(g, par))
                if un == 0 and not (isinstance(g, int) and g == 0):
                    pe.wait_ge(s("nm_row"), g)
                pe.wait_ge(s("mx_used"), UNITS * g + un + 1)
                q0 = (j % 2) * L + qt * P
                for hf in range(2):
                    k0 = c * CK + hf * 512
                    ins = mm(ps[:, 2 * (un % 2) + hf, :], qm_stack[0:RS, par, j // 2, q0:q0 + P],
                             k_stack[0:RS, par, j // 2, k0:k0 + 512])
                ins.then_inc(s("mx_ready"), 1)

            def grp(g, par):
                if isinstance(g, int):
                    return g // 2 + 1
                return loads[0]

            loads = [None]

            def max_turn(g):
                pe.wait_ge(s("nm_ready"), g + 1)
                for c in range(8):
                    ins = mm(ps[0:1, c // 4, (c % 4) * P:(c % 4 + 1) * P], nm_t[:, c:c + 1], ident_r[:, :])
                ins.then_inc(s("nmt_ready"), 1)

            def scores(g, par, st):
                if st == 0:
                    pe.wait_ge(s(f"qe_in{par}"), 96 * grp(g, par))
                    pe.wait_ge(s("nm_row"), g + 1)
                for bk in range(2):
                    pe.wait_ge(s("p_ready"), 2 * KT * g + 2 * st + bk + 1)
                    for ab in range(2):
                        ins = mm(ps[:, 4 + bk, ab * L:(ab + 1) * L],
                                 k_stack[0:RS + 1, par, bk, st * P:(st + 1) * P],
                                 qe_stack[0:RS + 1, par, bk, ab * L:(ab + 1) * L])
                    ins.then_inc(s("s_ready"), 1)

            def values(g, par, st):
                if st == 0:
                    pe.wait_ge(s(f"vs_in{par}"), 16 * grp(g, par))
                    pe.wait_ge(s("o_evac"), g + 1)
                pe.wait_ge(s("p_ready"), 2 * KT * g + 2 * st + 4)
                for j in range(GH):
                    ins = mm(ps[32 * j:32 * j + DH + 1, 6 + par, 0:L],
                             v_grp[:, par, st, j * (DH + 1):(j + 1) * (DH + 1)],
                             probs[:, (2 * st + j // 2) % PRING, (j % 2) * L:(j % 2 + 1) * L], st == 0, st == KT - 1)
                ins.then_inc(s("pv_done"), 1)

            def units_at(st):
                lo = min(UNITS, (st * UNITS + 27) // 28)
                hi = min(UNITS, ((st + 1) * UNITS + 27) // 28)
                return range(lo, hi)

            def group_pass(g, par, following, load_now, load_next):
                for st in range(KT):
                    if st + 1 < KT:
                        loads[0] = load_now
                        scores(g, par, st + 1)
                    elif following:
                        loads[0] = load_next
                        scores(g + 1, 1 - par, 0)
                    if following:
                        loads[0] = load_next
                        for un in units_at(st):
                            max_unit(g + 1, 1 - par, un)
                            if un == UNITS - 1:
                                max_turn(g + 1)
                    loads[0] = load_now
                    values(g, par, st)

            pe.wait_ge(s("kl_done"), 2 * NPC + 4)
            pe.wait_ge(s("v_done"), 2 * NPC + 4)
            pe.wait_ge(s("pv_zero"), 1)
            pe.wait_ge(s("ones_rows"), 2)
            for un in range(UNITS):
                max_unit(0, 0, un)
            max_turn(0)
            scores(0, 0, 0)
            with pe.Fori(0, NG // 2 - 1) as i:
                group_pass(2 * i, 0, True, i + 1, i + 1)
                group_pass(2 * i + 1, 1, True, i + 1, i + 2)
            group_pass(NG - 2, 0, True, NG // 2, NG // 2)
            group_pass(NG - 1, 1, False, NG // 2, NG // 2)

            pe.wait_ge(s("o_evac"), NG + 2)
            pe.wait_ge(s("masks_ready"), 1)
            for g in range(NG):
                if g >= 2:
                    pe.wait_ge(s("o_norm"), g - 1)
                mm(ps[:, g % 2, 0:L], head_ones, o_raw[:, g + 1, :]).then_inc(s("o_sums"), 1)
            pe.wait_ge(s("wo_in"), 16 * GH)
            for j in range(NT):
                b = j // QT
                pe.wait_ge(s("o_norm"), 4 * (b + 1))
                for g in range(4):
                    ins = mm(ps[:, 2 + j // 2, (j % 2) * D:(j % 2 + 1) * D], o_n[:, 4 * b + g, (j % 2) * P:(j % 2 + 1) * P],
                             w_o[:, g, :], g == 0, g == 3)
            ins.then_inc(s("y1_ready"), 1)

            transpose_xn(1)
            pe.wait_ge(s("w2_in"), 16 * 12)
            for m in range(KF):
                for c in range(KF):
                    ins = mm(ps[:, m, :], w_gate[:, c, m * P:(m + 1) * P], xnT[:, c, :], c == 0, c == KF - 1)
                ins.then_inc(s("gate_mm"), 1)
            pe.wait_ge(s("u_ready"), KF)
            for c in range(KF):
                ins = mm(ps[0:64, 2, :], bc_w[:, c, :], u[:, c, :], c == 0, c == KF - 1)
            ins.then_inc(s("bc_mm"), 1)
            pe.wait_ge(s("gate_ready"), KF)
            pe.wait_ge(s("bc_ready"), 1)

            def add_states(n):
                for c in range(KF):
                    k = KF * n + c
                    pe.wait_ge(s("hc_ready"), k + 1)
                    mm(ps[:, 4 + c, :], ident[:, :], hc[:, k % 4, :], n == 0, n == NST - 1).then_inc(s("hc_used"), 1)

            for n in range(NST):
                if n >= 2:
                    pe.wait_ge(s("b_used"), n - 1)
                mm(ps[:, n % 2, :], sel_n[:, n:n + 1].to_broadcast([64, P]), bc_hl[:, :]).then_inc(s("b_ready"), 1)
                if n >= 2:
                    pe.wait_ge(s("c_bc_ready"), n - 1)
                mm(ps[:, 2 + n % 2, :], sel_n[:, 16 + n:17 + n].to_broadcast([64, P]), bc_hl[:, :]
                   ).then_inc(s("c_ready"), 1)
                if n >= 1:
                    add_states(n - 1)
            add_states(NST - 1)
            pe.wait_ge(s("yT_ready"), 1)
            for j in range(NT):
                for c in range(KF):
                    ins = mm(ps[:, 6 + j // 2, (j % 2) * D:(j % 2 + 1) * D], yT[:, c, j * P:(j + 1) * P], w_out[:, c, :],
                             c == 0, c == KF - 1)
            ins.then_inc(s("y2_ready"), 1)

            transpose_xn(3)
            for j in range(NT):
                for c in range(KF):
                    ins = mm(ps[:, j // 2, (j % 2) * D:(j % 2 + 1) * D], xnT[:, c, j * P:(j + 1) * P], m_dft[:, c, :],
                             c == 0, c == KF - 1)
            ins.then_inc(s("y3_ready"), 1)

            transpose_xn(4)
            pe.wait_ge(s("w4_in"), 48)
            for m in range(KF):
                for c in range(KF):
                    ins = mm(ps[:, m, :], w_q1[:, c, m * P:(m + 1) * P], xnT[:, c, :], c == 0, c == KF - 1)
                ins.then_inc(s("q1_mm"), 1)
            pe.wait_ge(s("q1_ready"), KF)
            for c in range(KF):
                ins = mm(ps[:, 2, :], w_k1[:, c, :], q1T[:, c, :], c == 0, c == KF - 1)
            ins.then_inc(s("qp_mm"), 1)
            for j in range(NT):
                for c in range(KF):
                    ins = mm(ps[:, 3, j:j + 1], q1T[:, c, j * P:(j + 1) * P], vecs[:, BK1, c:c + 1], c == 0, c == KF - 1)
            ins.then_inc(s("qbk_mm"), 1)
            pe.wait_ge(s("qp_ready"), 1)
            pe.wait_ge(s("qbk_ready"), 1)
            for b in range(B):
                pe.wait_ge(s("c4_in"), 32 * (b + 1))
                for un in range(8):
                    k = b * 8 + un
                    qt, c = un // 4, un % 4
                    if k >= 2:
                        pe.wait_ge(s("mx4_used"), k - 1)
                    if b and un < 2:
                        pe.wait_ge(s("p4_ready"), 8 * b)
                    for hf in range(2):
                        ins = mm(ps[:, 4 + 2 * (k % 2) + hf, :], qpT[:, b * L + qt * P:b * L + (qt + 1) * P],
                                 ctxT[:, c * CK + hf * 512:c * CK + (hf + 1) * 512])
                    ins.then_inc(s("mx4_ready"), 1)
                pe.wait_ge(s("nm4_cols"), b + 1)
                for qt in range(QT):
                    ins = mm(ps[0:1, 3, qt * P:(qt + 1) * P], nm4f[:, qt:qt + 1], ident[:, :])
                ins.then_inc(s("nm4_turned"), 1)
                pe.wait_ge(s("nm4_ready"), b + 1)

                def scores4(un):
                    k = b * 8 + un
                    if un >= 2:
                        pe.wait_ge(s("p4_ready"), k - 1)
                    for t in range(4):
                        kt = 4 * un + t
                        o = ps[:, 4 + 2 * (k % 2) + t // 2, (t % 2) * L:(t % 2 + 1) * L]
                        mm(o, ctxT[:, kt * P:(kt + 1) * P], qpT[:, b * L:(b + 1) * L], True, False)
                        ins = mm(o, ones_r[:, :], nm4[:, :], False, True)
                    ins.then_inc(s("s4_ready"), 1)

                def values4(un):
                    k = b * 8 + un
                    pe.wait_ge(s("p4_ready"), k + 1)
                    for t in range(4):
                        kt = 4 * un + t
                        ins = mm(ps[:, 0, 0:L], ctxN[:, kt, :], p4[:, k % 2, t * L:(t + 1) * L], kt == 0, kt == KT - 1)
                    ins.then_inc(s("av4_done"), 1)

                scores4(0)
                for un in range(8):
                    if un < 7:
                        scores4(un + 1)
                    values4(un)
                pe.wait_ge(s("p4_summed"), 8 * (b + 1))
                for t in range(4):
                    ins = mm(ps[:, 1, 0:L], ones, psumP[:, t * L:(t + 1) * L], t == 0, t == 3)
                ins.then_inc(s("oc_sum"), 1)
                pe.wait_ge(s("oc_ready"), b + 1)
                for qt in range(QT):
                    ins = mm(ps[:, 2, qt * D:(qt + 1) * D], ocT[:, qt * P:(qt + 1) * P], w_v1[:, :])
                ins.then_inc(s("y4_ready"), 1)

            transpose_xn(5)
            pe.wait_ge(s("w5_in"), 64)
            for w in range(2):
                for m in range(KF):
                    for c in range(KF):
                        ins = mm(ps[:, 2 * w + m, :], w5[:, w, c, m * P:(m + 1) * P], xnT[:, c, :], c == 0, c == KF - 1)
                    ins.then_inc(s("qk5_mm"), 1)
            for w in range(2):
                for j in range(NT):
                    for c in range(KF):
                        ins = mm(ps[:, 4 + 2 * w + j // 2, (j % 2) * D:(j % 2 + 1) * D], xnT[:, c, j * P:(j + 1) * P],
                                 w5[:, 2 * w, c, :], c == 0, c == KF - 1)
                ins.then_inc(s("qv5_mm"), 1)
            pe.wait_ge(s("k5_ready"), 1)
            pe.wait_ge(s("qv5_ready"), 2)
            for k in range(16):
                b, qt, hq = k // 8, (k // 4) % 2, k % 4
                pe.wait_ge(s("qm5_ready"), k + 1)
                if k >= 2:
                    pe.wait_ge(s("mx5_used"), k - 1)
                for j in range(4):
                    ins = mm(ps[:, 2 * (k % 2) + j // 2, (j % 2) * L:(j % 2 + 1) * L], qm5[:, k % 4, j, :],
                             kT5[:, hq // 2, b * L:(b + 1) * L])
                ins.then_inc(s("mx5_ready"), 1)
            pe.wait_ge(s("mx5_used"), 16)
            for qt in range(QT):
                ins = pe.transpose(ps[0:B * H, 4, qt * P:(qt + 1) * P], mx5[:, qt, :], ident[:, :])
            ins.then_inc(s("mT5_mm"), 1)
            pe.wait_ge(s("idx5_ready"), 1)
            for b in range(B):
                ins = mm(ps[0:HU, 5, 16 * b:16 * b + 16], sel_e[:, b, :], i5[0:B * H, :])
            ins.then_inc(s("c5_mm"), 1)
            pe.wait_ge(s("oneT_ready"), 1)
            for b in range(B):
                for qt in range(QT):
                    ins = pe.transpose(ps[:, 4, (2 * b + qt) * P:(2 * b + qt) * P + HU],
                                       oneT[0:HU, b, qt * P:(qt + 1) * P], ident[0:HU, 0:HU])
            ins.then_inc(s("oneN_mm"), 1)
            pe.wait_ge(s("oneN_ready"), 1)
            for b in range(B):
                for c in range(KF):
                    for qt in range(QT):
                        ins = mm(ps[:, 0, (2 * b + c) * P:(2 * b + c) * P + HU], qn5[:, 2 * b + qt, c * P:(c + 1) * P],
                                 oneN[:, b, qt, :], qt == 0, qt == QT - 1)
            ins.then_inc(s("qsel_mm"), 1)
            pe.wait_ge(s("qsel_ready"), 1)
            for b in range(B):
                for c in range(KF):
                    ins = mm(ps[0:HU, 2 + b, 0:L], qsel[:, b, c, :], kT5[:, c, b * L:(b + 1) * L], c == 0, c == KF - 1)
                ins.then_inc(s("ss5_ready"), 1)
            for b in range(B):
                pe.wait_ge(s("p5_ready"), b + 1)
                for kt in range(QT):
                    ins = pe.transpose(ps[:, 4 + b, kt * P:kt * P + HU],
                                       p5[0:HU, b, kt * P:(kt + 1) * P], ident[0:HU, 0:HU])
                ins.then_inc(s("pT5_mm"), 1)
            for b in range(B):
                pe.wait_ge(s("pT5_ready"), b + 1)
                for kt in range(QT):
                    ins = mm(ps[0:HU, 6 + b, 0:D], pT5[:, b, kt, :], vn5[:, 2 * b + kt, :], kt == 0, kt == QT - 1)
                ins.then_inc(s("o5_mm"), 1)
            for b in range(B):
                pe.wait_ge(s("om5_ready"), b + 1)
                for c in range(KF):
                    ins = mm(ps[:, c, b * L:(b + 1) * L], om5[0:HU, b, c * P:(c + 1) * P], oneT[0:HU, b, :])
                ins.then_inc(s("oT5_mm"), 1)
            pe.wait_ge(s("oT5_ready"), 1)
            for j in range(NT):
                for c in range(KF):
                    ins = mm(ps[:, 2 + j // 2, (j % 2) * D:(j % 2 + 1) * D], oT5[:, c, j * P:(j + 1) * P], w5[:, 3, c, :],
                             c == 0, c == KF - 1)
            ins.then_inc(s("y5_ready"), 1)

            transpose_xn(6)
            pe.wait_ge(s("w6_in"), 16)
            for j in range(NT):
                for c in range(KF):
                    ins = mm(ps[:, 4, E * j:E * (j + 1)], xnT[:, c, j * P:(j + 1) * P], w_r[:, c, :], c == 0, c == KF - 1)
            ins.then_inc(s("r_mm"), 1)
            pe.wait_ge(s("r_copied"), 1)
            with pe.Fori(0, E // 2) as i:
                for par in range(2):
                    e = 2 * i + par
                    pe.wait_ge(s(f"w1_in{par}"), 16 * (i + 1))
                    for ft in range(FT):
                        pe.wait_ge(s("hs_ready"), FT * e + ft + 1)
                        for c in range(KF):
                            ins = mm(ps[:, ft % 4, :], w1[:, par, c, ft * P:(ft + 1) * P], xnT[:, c, :],
                                     c == 0, c == KF - 1)
                        ins.then_inc(s("hm_ready"), 1)
                    pe.wait_ge(s(f"w2_in_{par}"), 16 * (i + 1))
                    pe.wait_ge(s("hs_ready"), FT * e + FT + 4)
                    for j in range(NT):
                        pe.wait_ge(s("y_used"), NT * e + j + 1)
                        for ft in range(FT):
                            ins = mm(ps[:, 4 + j, 0:D], hT[:, ft, j * P:(j + 1) * P], w2[:, par, ft, :],
                                     ft == 0, ft == FT - 1)
                        ins.then_inc(s("y_ready"), 1)

        @block.vector
        def _(dve):
            steps = [0]

            def step(ins):
                steps[0] += 1
                ins.then_inc(s("dve_step"), 1)
                dve.wait_ge(s("dve_step"), steps[0])

            dve.sem_inc(s("kl_done"), 4)
            dve.sem_inc(s("mx_used"), 2)
            dve.sem_inc(s("y_used"), NT)

            def tiles(bank):
                return ps[:, bank:bank + 2, :].rearrange("p a (b d) -> p (a b) d", d=D)

            def layernorm(k, src, transposed=True):
                for j in range(NT):
                    ins = dve.bn_stats(stats[:, j, :], src[:, j, :])
                step(ins)
                for j in range(NT):
                    ins = dve.bn_aggr(mv[:, j, :], stats[:, j, :])
                step(ins)
                dve.tensor_scalar(mv[:, :, 1], mv[:, :, 1], EPS, None, ALU.add).then_inc(s("ln_var"), 1)
                dve.wait_ge(s("ln_sd"), k + 1)
                step(dve.reciprocal(rstd[:, :], sd[:, :]))
                for j in range(NT):
                    ins = dve.tensor_scalar(xn[:, j, :], src[:, j, :], mv[:, j, 0:1], rstd[:, j:j + 1],
                                            ALU.subtract, ALU.mult)
                if not transposed:
                    step(ins)
                    return
                ins.then_inc(s("ln_xn"), 1)

            def xnT_1(k):
                dve.wait_ge(s("ln_tr"), TURNS[k])
                dve.tensor_copy(xnT[:, 1, :], ps[:, 7, :]).then_inc(s("lnT_d"), 1)

            dve.wait_ge(s("x_in"), 16)
            layernorm(0, X)
            xnT_1(0)
            for c in range(KF):
                dve.wait_ge(s("q_hi_ready"), c + 1)
                dve.tensor_tensor(q_lo[:, c, :], ps[:, 4 + c, :], f32(q_hi[:, c, :]), ALU.subtract
                                  ).then_inc(s("q_lo_ready"), 1)
            dve.wait_ge(s("m_mm"), 1)
            dve.tensor_copy(m_dft[:, :, :].rearrange("p a b -> p (a b)"), ps[:, 2, :]).then_inc(s("m_ready"), 1)
            dve.wait_ge(s("m_ready"), 1)
            dve.sem_inc(s("dft_done"), 1)

            with dve.Fori(0, NPC // 2) as i:
                for par in range(2):
                    n = 2 * i + par
                    for k in range(2):
                        dve.wait_ge(s("kh_done"), 2 * n + k + 1)
                        dve.wait_ge(s(f"st_out{par}"), CRED * (i + 1))
                        dve.tensor_tensor(k_lo[:, par, k, :], ps[:, 4 * par + k, :], f32(k_hi[:, par, k, :]),
                                          ALU.subtract).then_inc(s("kl_done"), 1)
            dve.wait_ge(s("kv_ready"), 4 * NPC)
            dve.wait_ge(s("v_done"), 2 * NPC + 4)
            dve.wait_ge(s("kl_done"), 2 * NPC + 4)
            dve.memset(ps[:, 6:8, 0:L], 0.0).then_inc(s("pv_zero"), 1)

            def max_pass(g, par):
                for un in range(UNITS):
                    c, j, qt = un // 8, (un % 8) // 2, un % 2
                    dve.wait_ge(s("mx_ready"), UNITS * g + un + 1)
                    dve.tensor_reduce(mxp[:, 2 * j + qt, c:c + 1],
                                      ps[:, 2 * (un % 2):2 * (un % 2) + 2, :].rearrange("p a b -> p (a b)"),
                                      AX.X, ALU.max).then_inc(s("mx_used"), 1)
                dve.wait_ge(s("mx_used"), UNITS * (g + 1) + 2)
                dve.tensor_reduce(nm_t[:, :], mxp, AX.X, ALU.max, negate=True).then_inc(s("nm_ready"), 1)
                dve.wait_ge(s("nmt_ready"), g + 1)
                dve.tensor_copy(qe_stack[RS:RS + 1, par, :, :], ps[0:1, 0:2, :]).then_inc(s("nm_row"), 1)

            dve.wait_ge(s("q_zero"), 2)
            max_pass(0, 0)
            with dve.Fori(0, NG // 2 - 1) as i:
                for par in range(2):
                    max_pass(2 * i + par + 1, 1 - par)
            max_pass(NG - 1, 1)

            for g in range(NG):
                dve.wait_ge(s("o_sums"), g + 1)
                step(dve.reciprocal(o_sum[:, g % 2, :], ps[:, g % 2, 0:L]))
                dve.tensor_tensor(o_n[:, g, :], o_raw[:, g + 1, :], o_sum[:, g % 2, :], ALU.mult
                                  ).then_inc(s("o_norm"), 1)
            dve.wait_ge(s("y1_ready"), 1)
            step(dve.tensor_tensor(X[:, :, :], X[:, :, :], tiles(2), ALU.add))

            layernorm(1, X)
            for c in range(KF):
                step(dve.memset(xpad[:, c, :, 0:TAPS - 1], 0.0))
            dve.wait_ge(s("ln_tr"), 2)
            xnT_1(1)
            dve.wait_ge(s("lnT_d"), 2)
            dve.wait_ge(s("lnT_a"), 2)
            dve.wait_ge(s("w2_in"), 16 * 12)
            dve.wait_ge(s("vec_in"), 16)
            for c in range(KF):
                step(dve.tensor_copy(xpad[:, c, :, TAPS - 1:], xnT[:, c, :].rearrange("p (b l) -> p b l", b=B)))
                cv = conv[:, c, :].rearrange("p (b l) -> p b l", b=B)
                step(dve.tensor_scalar(cv, xpad[:, c, :, 0:L], conv_w[:, c, 0:1], vecs[:, CB, c:c + 1],
                                       ALU.mult, ALU.add))
                for t in range(1, TAPS):
                    ins = dve.scalar_tensor_tensor(cv, xpad[:, c, :, t:t + L], conv_w[:, c, t:t + 1], cv,
                                                   ALU.mult, ALU.add)
                    if t < TAPS - 1:
                        step(ins)
                ins.then_inc(s("conv_ready"), 1)
            dve.wait_ge(s("bc_mm"), 1)
            step(dve.tensor_scalar(bcf[0:64, :], ps[0:64, 2, :], bc_b[:, 0:1], None, ALU.add))
            step(dve.tensor_copy(bc_hl[:, :], bcf[0:64, :]))
            dve.tensor_tensor(bc_hl[32:64, :], bcf[32:64, :], f32(bc_hl[32:64, :]), ALU.subtract
                              ).then_inc(s("bc_ready"), 1)
            dve.wait_ge(s("u_ready"), KF)
            dve.wait_ge(s("a_dec_ready"), 1)
            k = 0
            for n in range(NST):
                dve.wait_ge(s("b_ready"), n + 1)
                if n >= 2:
                    dve.wait_ge(s("h_ready"), KF * (n - 1))
                for c in range(KF):
                    ins = dve.tensor_tensor(b_in[:, 2 * (n % 2) + c, :], u[:, c, :], ps[:, n % 2, :], ALU.mult)
                    if c == KF - 1:
                        ins.then_inc(s("b_used"), 1)
                dve.wait_ge(s("b_used"), n + 1)
                for c in range(KF):
                    if k >= 4:
                        dve.wait_ge(s("hc_ready"), k - 3)
                    for b in range(B):
                        ins = dve.tensor_tensor_scan(h_st[:, k % 4, b * L:(b + 1) * L],
                                                     a_dec[:, c, n:n + 1].to_broadcast([P, L]),
                                                     b_in[:, 2 * (n % 2) + c, b * L:(b + 1) * L], 0.0, ALU.mult, ALU.add)
                    ins.then_inc(s("h_ready"), 1)
                    k += 1
            dve.wait_ge(s("h_ready"), k)
            dve.wait_ge(s("gate_ready"), KF)
            dve.wait_ge(s("hc_used"), k)
            for c in range(KF):
                step(dve.scalar_tensor_tensor(yT[:, c, :], u[:, c, :], vecs[:, DD, c:c + 1], ps[:, 4 + c, :],
                                              ALU.mult, ALU.add))
                ins = dve.tensor_tensor(yT[:, c, :], yT[:, c, :], gate[:, c, :], ALU.mult)
            ins.then_inc(s("yT_ready"), 1)
            dve.wait_ge(s("row_in"), 16)
            step(dve.tensor_tensor(xn[:, :, :], xn[:, :, :], scaled_rows(rows[:, OB, :], NT), ALU.add))
            dve.wait_ge(s("y2_ready"), 1)
            step(dve.tensor_tensor(xn[:, :, :], xn[:, :, :], tiles(6), ALU.add))
            layernorm(2, xn, transposed=False)
            step(dve.tensor_tensor(xn[:, :, :], xn[:, :, :], scaled_rows(rows[:, LG, :], NT), ALU.mult))
            step(dve.tensor_tensor(X[:, :, :], X[:, :, :], scaled_rows(rows[:, LB, :], NT), ALU.add))
            step(dve.tensor_tensor(X[:, :, :], X[:, :, :], xn[:, :, :], ALU.add))

            def add_rows(i):
                step(dve.tensor_tensor(X[:, :, :], X[:, :, :], scaled_rows(rows[:, i, :], NT), ALU.add))

            layernorm(3, X)
            xnT_1(3)
            add_rows(FB)
            dve.wait_ge(s("y3_ready"), 1)
            step(dve.tensor_tensor(X[:, :, :], X[:, :, :], tiles(0), ALU.add))

            layernorm(4, X)
            xnT_1(4)
            add_rows(BV1)
            step(dve.memset(ones, 1.0))
            dve.wait_ge(s("qp_mm"), 1)
            dve.tensor_copy(qpT, ps[:, 2, :]).then_inc(s("qp_ready"), 1)
            dve.wait_ge(s("qbk_mm"), 1)
            dve.tensor_copy(qbk[:, 0:NT], ps[:, 3, 0:NT]).then_inc(s("qbk_ready"), 1)
            for b in range(B):
                for un in range(8):
                    k = b * 8 + un
                    dve.wait_ge(s("mx4_ready"), k + 1)
                    dve.tensor_reduce(mx4[:, un // 4, un % 4:un % 4 + 1],
                                      ps[:, 4 + 2 * (k % 2):6 + 2 * (k % 2), :].rearrange("p a b -> p (a b)"),
                                      AX.X, ALU.max).then_inc(s("mx4_used"), 1)
                dve.wait_ge(s("mx4_used"), 8 * (b + 1))
                step(dve.tensor_reduce(mx4[:, :, 4:5], mx4[:, :, 0:4], AX.X, ALU.max))
                qb = qbk[:, 2 * b:2 * b + 2].unsqueeze(2)
                step(dve.tensor_tensor(mx4[:, :, 5:6], mx4[:, :, 4:5], qb, ALU.add))
                dve.tensor_tensor(nm4f.unsqueeze(2), qb, mx4[:, :, 5:6], ALU.subtract).then_inc(s("nm4_cols"), 1)
                dve.wait_ge(s("nm4_turned"), b + 1)
                dve.tensor_copy(nm4[:, :], ps[0:1, 3, 0:L]).then_inc(s("nm4_ready"), 1)
                for un in range(8):
                    k = b * 8 + un
                    dve.wait_ge(s("p4_ready"), k + 1)
                    if un == 0:
                        if b:
                            dve.wait_ge(s("oc_sum"), b)
                        dve.tensor_copy(psumP, p4[:, k % 2, :]).then_inc(s("p4_summed"), 1)
                    else:
                        dve.wait_ge(s("p4_summed"), k)
                        dve.tensor_tensor(psumP, psumP, p4[:, k % 2, :], ALU.add).then_inc(s("p4_summed"), 1)
                dve.wait_ge(s("oc_sum"), b + 1)
                step(dve.reciprocal(rs4, ps[:, 1, 0:L]))
                dve.wait_ge(s("av4_done"), 8 * (b + 1))
                dve.tensor_tensor(ocT, ps[:, 0, 0:L], rs4, ALU.mult).then_inc(s("oc_ready"), 1)
                dve.wait_ge(s("y4_ready"), b + 1)
                step(dve.tensor_tensor(X[:, 2 * b:2 * b + 2, :], X[:, 2 * b:2 * b + 2, :],
                                       ps[:, 2, :].rearrange("p (a d) -> p a d", d=D), ALU.add))

            layernorm(5, X)
            xnT_1(5)
            add_rows(BO5)
            for w, dst in ((0, qn5), (1, vn5)):
                dve.wait_ge(s("qv5_mm"), w + 1)
                dve.tensor_tensor(dst, tiles(4 + 2 * w), scaled_rows(rows[:, BQ5R if w == 0 else BV5, :], NT), ALU.add
                                  ).then_inc(s("qv5_ready"), 1)
            for k in range(16):
                b, qt, hq = k // 8, (k // 4) % 2, k % 4
                dve.wait_ge(s("mx5_ready"), k + 1)
                dve.tensor_reduce(mx5[:, qt, b * H + 4 * hq:b * H + 4 * hq + 4],
                                  ps[:, 2 * (k % 2):2 * (k % 2) + 2, :].rearrange("p a (b q) -> p (a b) q", q=L),
                                  AX.X, ALU.max).then_inc(s("mx5_used"), 1)
            dve.wait_ge(s("mT5_mm"), 1)
            mT = mT5[0:B * H, :]
            step(dve.tensor_copy(mT, ps[0:B * H, 4, 0:L]))
            step(dve.max(i5[0:B * H, 8:16], mT))
            ix = idx5[0:B * H, :].bitcast(U32)
            step(dve.max_index(ix, i5[0:B * H, 8:16], mT))
            dve.tensor_copy(i5[0:B * H, 0:8], ix).then_inc(s("idx5_ready"), 1)
            dve.wait_ge(s("masks_ready"), 1)
            step(dve.tensor_reduce(umask[:, 0:TOPU], umask3[:, :, :].rearrange("p h u -> p u h"), AX.X, ALU.max))
            dve.wait_ge(s("c5_mm"), 1)
            for b in range(B):
                for r in range(2):
                    step(dve.tensor_tensor(s5[0:HU, 0, 0:TOPU], ps[0:HU, 5, 16 * b + 8 * r:16 * b + 8 * r + TOPU],
                                           umask[:, 0:TOPU], ALU.mult))
                    step(dve.tensor_reduce(c5[0:HU, b, 1 - r:2 - r], s5[0:HU, 0, 0:TOPU], AX.X, ALU.add))
            dve.wait_ge(s("iota_ready"), 1)
            for b in range(B):
                ins = dve.tensor_scalar(oneT[0:HU, b, :], iota5[0:HU, :], c5[0:HU, b, 1:2], None, ALU.is_equal)
            ins.then_inc(s("oneT_ready"), 1)
            for b in range(B):
                dve.tensor_scalar(c5[0:HU, b, 0:1], c5[0:HU, b, 0:1], -SCALE, None, ALU.mult).then_inc(s("nm5_ready"), 1)
            dve.wait_ge(s("oneN_mm"), 1)
            dve.tensor_copy(oneN.rearrange("p b q h -> p (b q) h"),
                            ps[:, 4, :].rearrange("p (k h) -> p k h", h=P)[:, :, 0:HU]).then_inc(s("oneN_ready"), 1)
            dve.wait_ge(s("qsel_mm"), 1)
            for b in range(B):
                ins = dve.tensor_tensor(qsel[:, b, :, :], ps[:, 0, 2 * b * P:(2 * b + 2) * P].rearrange(
                    "p (c h) -> p c h", h=P)[:, :, 0:HU], bd5[:, :, :], ALU.mult)
            ins.then_inc(s("qsel_ready"), 1)
            for b in range(B):
                dve.wait_ge(s("pT5_mm"), b + 1)
                dve.tensor_copy(pT5[:, b, :, :], ps[:, 4 + b, 0:2 * P].rearrange(
                    "p (c h) -> p c h", h=P)[:, :, 0:HU]).then_inc(s("pT5_ready"), 1)
            step(dve.reciprocal(rs5[0:HU, :], sum5[0:HU, :]))
            for b in range(B):
                dve.wait_ge(s("o5_mm"), b + 1)
                dve.scalar_tensor_tensor(om5[0:HU, b, :], ps[0:HU, 6 + b, 0:D], rs5[0:HU, b:b + 1], bdT5[:, :],
                                         ALU.mult, ALU.mult).then_inc(s("om5_ready"), 1)
            dve.wait_ge(s("oT5_mm"), B)
            dve.tensor_copy(oT5.rearrange("p c t -> p (c t)"), ps[:, 0:2, :].rearrange("p a b -> p (a b)")
                            ).then_inc(s("oT5_ready"), 1)
            dve.wait_ge(s("y5_ready"), 1)
            step(dve.tensor_tensor(X[:, :, :], X[:, :, :], tiles(2), ALU.add))
            dve.sem_inc(s("a5_done"), 1)

            layernorm(6, X)
            xnT_1(6)
            dve.wait_ge(s("r_mm"), 1)
            dve.tensor_copy(r6.rearrange("p a b -> p (a b)"), ps[:, 4, 0:NT * E]).then_inc(s("r_copied"), 1)
            dve.wait_ge(s("r_copied"), 1)
            step(dve.tensor_reduce(c6[:, :, 0:1], r6, AX.X, ALU.max))
            dve.tensor_tensor(r6, r6, c6[:, :, 0:1].to_broadcast([P, NT, E]), ALU.subtract).then_inc(s("r_ready"), 1)
            dve.wait_ge(s("r_exp"), 1)
            step(dve.tensor_reduce(c6[:, :, 1:2], p6, AX.X, ALU.add))
            step(dve.reciprocal(c6[:, :, 2:3], c6[:, :, 1:2]))
            step(dve.tensor_tensor(p6, p6, c6[:, :, 2:3].to_broadcast([P, NT, E]), ALU.mult))
            for j in range(NT):
                ins = dve.max(t6[:, j, :], p6[:, j, :])
            step(ins)
            for j in range(NT):
                ins = dve.max_index(i6[:, j, :].bitcast(U32), t6[:, j, :], p6[:, j, :])
            step(ins)
            step(dve.tensor_copy(f6, i6.bitcast(U32)))
            step(dve.tensor_tensor(c6[:, :, 3:4], t6[:, :, 0:1], t6[:, :, 1:2], ALU.add))
            step(dve.reciprocal(c6[:, :, 4:5], c6[:, :, 3:4]))
            step(dve.tensor_tensor(t6[:, :, 0:2], t6[:, :, 0:2], c6[:, :, 4:5].to_broadcast([P, NT, 2]), ALU.mult))
            for j in range(NT):
                for r, dst in ((0, gates), (1, g6)):
                    ins = dve.tensor_scalar(dst[:, j, :], iota6, f6[:, j, r:r + 1], t6[:, j, r:r + 1],
                                            ALU.is_equal, ALU.mult)
            step(ins)
            step(dve.tensor_tensor(gates, gates, g6, ALU.add))
            with dve.Fori(0, E // 2) as i:
                for par in range(2):
                    e = 2 * i + par
                    for j in range(NT):
                        dve.wait_ge(s("y_ready"), NT * e + j + 1 + NT)
                        dve.wait_ge(s("y_used"), NT * e + j + 1)
                        dve.scalar_tensor_tensor(X[:, j, :], ps[:, 4 + j, 0:D], gates[:, j, bass.ds(e, 1)], X[:, j, :],
                                                 ALU.mult, ALU.add).then_inc(s("y_used"), 1)
            dve.wait_ge(s("y_used"), NT * E + NT)
            dve.sem_inc(s("x_done"), 1)


_LAYOUT = {
    "x": ("x", lambda v: v.reshape(T, D)),
    "ctx": ("ctx_512", lambda v: v),
    "ctxT": ("ctx_512", lambda v: v.transpose(2, 0, 1).reshape(LAT, B * S)),
    "wqT": ("L0_xattn_Wq", lambda v: v.T),
    "wkvT": ("L0_xattn_Wkv", lambda v: v.T),
    "woT": ("L0_xattn_Wo", lambda v: v.T),
    "conv_w": ("L0_attn_conv_w", lambda v: v.reshape(D, TAPS)),
    "a_log": ("L0_attn_A", lambda v: v),
    "bpT": ("L0_attn_Bp_w", lambda v: v.T),
    "bpb": ("L0_attn_Bp_b", lambda v: v),
    "cpT": ("L0_attn_Cp_w", lambda v: v.T),
    "cpb": ("L0_attn_Cp_b", lambda v: v),
    "gateT": ("L0_attn_gate_w", lambda v: v.T),
    "outT": ("L0_attn_out_w", lambda v: v.T),
    "frT": ("L0_ffn_w_freq_real", lambda v: v.T),
    "fiT": ("L0_ffn_w_freq_imag", lambda v: v.T),
    "wq1": ("L1_xattn_Wq", lambda v: v),
    "wk1T": ("L1_xattn_Wk", lambda v: v.T),
    "wv1": ("L1_xattn_Wv", lambda v: v),
    "wq5T": ("L1_attn_wq", lambda v: v.T),
    "wk5T": ("L1_attn_wk", lambda v: v.T),
    "wv5T": ("L1_attn_wv", lambda v: v.T),
    "wo5T": ("L1_attn_wo", lambda v: v.T),
    "w1T": ("L1_ffn_W1", lambda v: v.transpose(0, 2, 1)),
    "w2T": ("L1_ffn_W2", lambda v: v.transpose(0, 2, 1)),
    "wrT": ("L1_ffn_Wr", lambda v: v.T),
}


def dft_tables():
    k = np.arange(D)
    w = 2 * np.pi * ((k[:, None] * k[None, :]) % D) / D
    c, sn = np.cos(w), np.sin(w)
    return np.stack([c, sn, -sn, c / D, sn / D]).astype(np.float32)


def kernel(**inputs):
    import concourse.bacc as _bacc
    from concourse.bass_utils import run_bass_kernel_spmd as _run

    nc = _bacc.Bacc("TRN2", target_bir_lowering=False, num_devices=1)
    arrays, a = {}, {}
    for name, (source, layout) in _LAYOUT.items():
        arrays[f"in_{name}"] = np.ascontiguousarray(layout(np.asarray(inputs[source])))
    arrays["in_vecs"] = np.ascontiguousarray(
        np.stack([np.asarray(inputs[n]).reshape(KF, P).T for n in VECS], axis=1))
    arrays["in_rows"] = np.stack([np.asarray(inputs[n]) for n in ROWS])
    arrays["in_dft"] = dft_tables()
    for name, v in arrays.items():
        a[name[3:]] = nc.dram_tensor(name, v.shape, mybir.dt.from_np(v.dtype), kind="ExternalInput").ap()
    a["out"] = nc.dram_tensor("out", (T, D), F32, kind="ExternalOutput").ap()
    perceiver(nc, a)
    r = _run(nc, [arrays], core_ids=[0])
    return r.results[0]["out"].reshape(B, L, D)
```

```python
from contextlib import ExitStack

import numpy as np

import concourse.bass as bass
from concourse import mybir

F32 = mybir.dt.float32
F32R = mybir.dt.float32r
U32 = mybir.dt.uint32
ALU = mybir.AluOpType
ACT = mybir.ActivationFunctionType
AX = mybir.AxisListType

P = 128
B, L, D = 2, 256, 256
T = B * L
NT = T // P
QT = L // P
KF = D // P
S, LAT = 4096, 128
H, DH = 16, 16
SCALE = DH ** -0.5
EPS = 1e-5
NST, TAPS = 16, 4
E, F = 8, 1024
FT = F // P
TOPU = 5
HU = H * TOPU

GH = 4
NG = B * H // GH
KT = S // P
CK = 1024
NC = S // CK
PK = 512
NPC = B * S // PK
RB = 3 * DH
RS = 2 * RB
VW = GH * (DH + 1)
UNITS = 32
MAX_SLOTS = 84
TURN_SLOT = 29, 1
PRING = 4
ARENA = 11936
TURNS = {0: 1, 1: 2, 3: 3, 4: 4, 5: 5, 6: 6}
KST, VST = 16 * 2, 16
LOADQ, LOADK = 16 * 6, 16 * 3


VECS = ("L0_attn_conv_b", "L0_attn_D", "L0_attn_gate_b", "L1_xattn_bq", "L1_xattn_bk", "L1_attn_bq", "L1_attn_bk")
PACK = (("L0_attn_gate_w", D), ("L0_attn_out_w", D), ("L0_attn_Bp_w", NST), ("L0_attn_Cp_w", NST), ("L0_attn_Bp_w", NST),
        ("L0_attn_Cp_w", NST), ("L1_xattn_Wq", D), ("L1_xattn_Wk", LAT), ("L1_attn_wq", D), ("L1_attn_wk", D),
        ("L1_attn_wv", D), ("L1_attn_wo", D), ("L1_ffn_Wr", E), ("L0_attn_conv_w", TAPS), ("L0_attn_A", NST))
AS_IS = ("L1_xattn_Wq", "L0_attn_conv_w", "L0_attn_A")
ROWS = ("L0_attn_out_b", "L0_attn_ln_g", "L0_attn_ln_b", "L0_ffn_bias", "L1_xattn_bv", "L1_attn_bv", "L1_attn_bo",
        "L1_attn_bq")


def perceiver(nc, a):
    ctx = ExitStack()
    with ctx:
        def sb(name, shape, dt=F32):
            return ctx.enter_context(nc.sbuf_tensor(name, shape, dt))

        def sem(name):
            return ctx.enter_context(nc.semaphore(name))

        ps = ctx.enter_context(nc.psum_tensor("ps", [P, 8, 512], F32))

        def f32(v):
            return v.bitcast(F32)

        k_stack = sb("k_stack", [P, 2, 2, S], F32R)
        qm_stack = sb("qm_stack", [P, 2, 2, 2 * L], F32R)
        qe_stack = sb("qe_stack", [P, 2, 2, 2 * L], F32R)
        k_hi = sb("k_hi", [P, 2, 2, PK], F32R)
        k_lo = sb("k_lo", [P, 2, 2, PK], F32R)
        xn_hi = sb("xn_hi", [P, KF, T], F32R)[:, :, :]
        xn_lo = sb("xn_lo", [P, KF, T], F32R)[:, :, :]
        nm_t = sb("nm", [P, 8], F32R)
        ident_r = sb("ident_r", [P, P], F32R)
        bc_hl = sb("bc_hl", [64, T], F32R)
        sel_n = sb("sel_n", [64, 2 * NST], F32R)
        nm4 = sb("nm4", [1, L], F32R)
        ones_r = sb("ones_r", [1, P], F32R)
        q_hi = k_stack[:, 1, 0, 0:2 * T].rearrange("p (c t) -> p c t", c=2)
        q_lo = k_stack[:, 1, 0, 2 * T:4 * T].rearrange("p (c t) -> p c t", c=2)

        ident = sb("ident", [P, P])
        X = sb("X", [P, NT, D])
        xn = sb("xn", [P, NT, D])
        xnT = sb("xnT", [P, KF, T])
        stats = sb("stats", [P, NT, 6])
        mv = sb("mv", [P, NT, 2])
        minus_half = sb("minus_half", [P, NT])
        rstd = sb("rstd", [P, NT])
        w_a = sb("w_a", [P, KF, D])
        w_kv = sb("w_kv", [P, 2 * D])
        w_o = sb("w_o", [P, NG // B, D])
        w_all = sb("w_all", [P, KF, sum(n for _, n in PACK)])
        col = [0]

        def packed(*names):
            n = sum(w for _, w in names)
            v = w_all[:, :, col[0]:col[0] + n]
            col[0] += n
            return v

        w_gate, w_out, bc_w, w_q1, w_k1 = (packed(*PACK[i:j]) for i, j in ((0, 1), (1, 2), (2, 6), (6, 7), (7, 8)))
        w5 = [packed(PACK[i]) for i in range(8, 12)]
        w_r, conv_w, a_log = (packed(PACK[i]) for i in range(12, 15))
        bc_b = sb("bc_b", [64, 1])
        vecs = sb("vecs", [P, len(VECS), KF])
        a_dec = sb("a_dec", [P, KF, NST])
        rows = sb("rows", [P, len(ROWS), D])
        m_dft = w_a
        w_v1 = sb("w_v1", [P, D])
        head_mask = sb("head_mask", [P, 8])
        arena = sb("arena", [P, ARENA])

        CB, DD, GB, BQ1, BK1, BQ5, BK5 = range(len(VECS))
        OB, LG, LB, FB, BV1, BV5, BO5, BQ5R = range(len(ROWS))

        off = [0]

        def carve(*shape):
            n = int(np.prod(shape))
            v = arena[:, off[0]:off[0] + n]
            off[0] += n
            assert off[0] <= ARENA, off[0]
            names = "abcd"[:len(shape)]
            if len(shape) == 1:
                return v
            return v.rearrange("p (%s) -> p %s" % (" ".join(names), " ".join(names)),
                               **{c: s for c, s in zip(names[1:], shape[1:])})

        v_grp = carve(2, KT, VW)
        probs = carve(PRING, 512)
        o_raw = carve(NG + 1, L)
        cx = carve(2, PK)
        v_stage = carve(2, NG // B, PK // P, VW)
        mxp = carve(8, NC)
        k_full = o_raw[:, 0:NG, :].rearrange("p g l -> p (g l)").rearrange("p (r k f) -> p r k f", r=2, k=2)
        off[0] = 0
        dft = carve(5, KF, D)
        wf = carve(2, KF, D)
        uf = carve(2, KF, D)
        assert off[0] <= 2 * KT * VW + PRING * 512 + (NG + 1) * L
        off[0] = 2 * KT * VW + PRING * 512 + (NG + 1) * L
        o_sum = carve(2, L)
        o_n = carve(NG, L)
        head_ones_t = sb("head_ones", [P, P])
        head_ones = head_ones_t[:, :]
        off[0] = 0
        xpad_all = carve(KF * B * (L + TAPS - 1))
        xpad = xpad_all.rearrange("p (c b l) -> p c b l", c=KF, b=B)
        conv = carve(KF, T)
        u = carve(KF, T)
        gate = carve(KF, T)
        b_in = carve(4, T)
        h_st = carve(4, T)
        c_bc = carve(2, T)
        hc = carve(4, T)
        yT = xpad_all[:, 0:KF * T].rearrange("p (c t) -> p c t", c=KF)
        bcf = carve(T)
        xn_T2 = xn[:, :, :].rearrange("p j f -> p (j f)").rearrange("p (c t) -> p c t", c=KF)
        off[0] = 0
        ctxT = carve(S)
        ctxN = carve(KT, LAT)
        q1T = xn_T2
        qpT = carve(T)
        qbk = carve(8)
        p4 = carve(2, 4 * L)
        psumP = xnT[:, :, :].rearrange("p c t -> p (c t)")
        mx4 = carve(QT, 8)
        ones = carve(P)
        ocT = carve(L)
        rs4 = carve(L)
        nm4f = carve(QT)
        off[0] = 0
        qT5 = xn_T2
        kT5 = carve(KF, T)
        qn5 = carve(NT, D)
        vn5 = carve(NT, D)
        mx5 = carve(QT, B * H)
        mT5 = carve(L)
        i5 = carve(16)
        idx5 = carve(8)
        c5 = carve(2, 16)
        s5 = carve(2, 16)
        oneT = carve(B, L)
        oneN = carve(B, QT, HU)
        qsel = carve(B, KF, HU)
        p5 = carve(B, L)
        pT5 = carve(B, QT, HU)
        sum5 = carve(B)
        rs5 = carve(B)
        om5 = carve(B, D)
        oT5 = carve(KF, T)
        qm5 = carve(4, 4, P)
        assert off[0] <= ARENA - KF * F
        off[0] = 0
        w1_1, w2_0, w2_1 = carve(KF, F), carve(FT, D), carve(FT, D)
        h_f = carve(4, T)
        off[0] = ARENA - KF * F
        w1, w2 = (carve(KF, F), w1_1), (w2_0, w2_1)
        parts6 = k_stack[:, :, :, :].rearrange("p a b k -> p (a b k)")

        def part6(i, par, n):
            lo = (4 * par + i) * KF * F
            return parts6[:, lo:lo + KF * F].rearrange("p (a b) -> p a b", a=n)

        w1_hi, w1_lo = ([part6(i, par, KF) for par in range(2)] for i in (0, 1))
        w2_hi, w2_lo = ([part6(i, par, FT) for par in range(2)] for i in (2, 3))
        stage1 = [v[:, :, :, :].rearrange("p a b k -> p (a b) k") for v in (qm_stack, qe_stack, k_hi, k_lo)]
        h_hi = [stage1[ft // 4][:, ft % 4, :] for ft in range(FT)]
        h_lo = [stage1[2 + ft // 4][:, ft % 4, :] for ft in range(FT)]
        gates_t = sb("gates", [P, NT, E])
        gates = gates_t[:, :, :]
        r6_t = sb("r6", [P, NT, 8])
        r6 = r6_t[:, :, :]
        p6_t = sb("p6", [P, NT, 8])
        p6 = p6_t[:, :, :]
        t6_t = sb("t6", [P, NT, 8])
        t6 = t6_t[:, :, :]
        i6_t = sb("i6", [P, NT, 8])
        i6 = i6_t[:, :, :]
        f6_t = sb("f6", [P, NT, 8])
        f6 = f6_t[:, :, :]
        g6_t = sb("g6", [P, NT, 8])
        g6 = g6_t[:, :, :]
        c6_t = sb("c6", [P, NT, 8])
        c6 = c6_t[:, :, :]
        iota_t = sb("iota", [P, L])
        iota5, iota6 = iota_t[:, :], iota_t[:, 0:E]

        def flat6(v):
            return v.rearrange("p a b -> p (a b)")

        umask3 = sb("umask3", [HU, H, TOPU])
        umask = sb("umask", [HU, 8])
        sel_e = sb("sel_e", [2 * H, B, HU])
        bd5 = sb("bd5", [P, KF, HU])
        bdT5 = sb("bdT5", [HU, D])

        qd = nc.dram_tensor("q_parts", [2, NG, GH * DH, L], F32, kind="Internal").ap()
        kd = nc.dram_tensor("k_parts", [2, NG, GH * DH, S], F32, kind="Internal").ap()
        vd = nc.dram_tensor("v_parts", [NG, P, KT, VW], F32, kind="Internal").ap()

        sems = {}

        def s(name):
            if name not in sems:
                sems[name] = ctx.enter_context(nc.semaphore(name))
            return sems[name]

        block = ctx.enter_context(nc.Block())

        def scaled_rows(v, n):
            return v.unsqueeze(1).to_broadcast([P, n, D])

        @block.sync
        def _(sp):
            for par in range(2):
                sp.sem_inc(s(f"k_out{par}"), KST)
                sp.sem_inc(s(f"v_out{par}"), VST)
            sp.dma_start(cx[:, 0, :], a["ctxT"][:, 0:PK]).then_inc(s("cx_in0"), 16)
            sp.dma_start(w_kv[:, :], a["wkvT"]).then_inc(s("wkv_in"), 16)
            sp.dma_start(X[:, :, :], a["x"].rearrange("(j p) f -> p j f", p=P)).then_inc(s("x_in"), 16)
            sp.dma_start(cx[:, 1, :], a["ctxT"][:, PK:2 * PK]).then_inc(s("cx_in1"), 16)
            sp.dma_start(w_a[:, :, :], a["wqT"].rearrange("(c p) n -> p c n", p=P)).then_inc(s("w0_in"), 16)

            def store_parts(b, nb, n, par):
                sp.wait_ge(s("kl_done"), 2 * n + 2)
                for i, part in enumerate((k_hi, k_lo)):
                    sp.dma_start(kd[i, 4 * b:4 * b + 4, :, bass.ds(nb * PK, PK)].rearrange(
                        "(c g) r k -> (g r) c k", g=2), f32(part[:, par, :, :])).then_inc(s(f"k_out{par}"), 16)
                sp.wait_ge(s("v_done"), 2 * n + 2 + 2)
                sp.dma_start(vd[4 * b:4 * b + 4, :, bass.ds(nb * 4, 4), :].rearrange("g p k v -> p g k v"),
                             v_stage[:, par, :, :, :]).then_inc(s(f"v_out{par}"), 16)

            def load_q(buf, name, g, par):
                for ab in range(2):
                    for blk, hl in enumerate((0, 0, 1)):
                        r = blk * 2 * DH + ab * DH
                        src = qd[hl, bass.ds(g, 1)].rearrange("g (r a d) q -> d (g r) a q", a=2, d=DH)[:, :, ab, :]
                        sp.dma_start(f32(buf[r:r + DH, par, :, ab * L:(ab + 1) * L]), src).then_inc(s(f"{name}{par}"), 16)

            def load_k(g, par, c):
                for blk, hl in enumerate((0, 1, 0)):
                    src = kd[hl, bass.ds(g, 1), :, c * CK:(c + 1) * CK].rearrange("g (r d) k -> d (g r) k", d=2 * DH)
                    sp.dma_start(f32(k_stack[blk * 2 * DH:(blk + 1) * 2 * DH, par, :, c * CK:(c + 1) * CK]), src
                                 ).then_inc(s(f"ks_in{par}{c}"), 16)

            def load_v(g, par):
                sp.dma_start(v_grp[:, par, :, :], vd[bass.ds(g, 1)].rearrange("g p k v -> p (g k) v")
                             ).then_inc(s(f"vs_in{par}"), 16)

            def chunk_traffic(b, nb, par, last=False):
                n = b * NPC // B + nb
                if not last:
                    sp.wait_ge(s("kv_ready"), 4 * n + 4)
                    load_ctx(n + 2, par)
                store_parts(b, nb, n, par)

            for n in range(NPC):
                b, nb, par = n // (NPC // B), n % (NPC // B), n % 2
                store_parts(b, nb, n, par)
                if n == 2:
                    sp.wait_ge(s("q_hi_ready"), KF)
                    sp.wait_ge(s("q_lo_ready"), KF)
                    for i, part in enumerate((q_hi, q_lo)):
                        for bb in range(B):
                            sp.dma_start(qd[i, 4 * bb:4 * bb + 4].rearrange("(c g) r q -> (g r) c q", g=2),
                                         f32(part[:, :, bb * L:(bb + 1) * L])).then_inc(s("q_out"), 16)
                elif n == 3:
                    sp.wait_ge(s("q_out"), 16 * 2 * B)
                    sp.wait_ge(s("q_zero"), 1)
                    load_q(qm_stack, "qm_in", 0, 0)
                if n in (3, 5, 7, 9):
                    c = (n - 3) // 2
                    for p2 in range(2):
                        sp.wait_ge(s(f"k_out{p2}"), KST * (c + 2))
                    load_k(0, 0, c)
                elif n == 11:
                    for p2 in range(2):
                        sp.wait_ge(s(f"v_out{p2}"), VST * (NC + 1))
                    sp.wait_ge(s("dft_done"), 1)
                    sp.wait_ge(s("q_zero"), 2)
                    load_q(qe_stack, "qe_in", 0, 0)
                    load_v(0, 0)
                elif n == 12:
                    load_q(qm_stack, "qm_in", 1, 1)
                elif n in (13, 14):
                    load_k(1, 1, n - 13)
            for c in range(2, NC):
                load_k(1, 1, c)
            load_q(qe_stack, "qe_in", 1, 1)
            load_v(1, 1)
            for par in range(2):
                sp.wait_ge(s(f"k_out{par}"), KST * (NPC // 2 + 1))
                sp.wait_ge(s(f"v_out{par}"), VST * (NPC // 2 + 1))

            with sp.Fori(0, NG // 2 - 1) as i:
                for par in range(2):
                    g = i * 2 + par
                    sp.wait_ge(s("mx_ready"), (g + 1) * UNITS)
                    load_q(qm_stack, "qm_in", g + 2, par)
                    for c in range(NC):
                        sp.wait_ge(s("s_ready"), 2 * KT * g + 2 * (KT // NC) * (c + 1))
                        load_k(g + 2, par, c)
                    load_q(qe_stack, "qe_in", g + 2, par)
                    sp.wait_ge(s("pv_done"), KT * (g + 1) + 2)
                    load_v(g + 2, par)

            for b in range(B):
                if b == 0:
                    sp.wait_ge(s("y2_ready"), 1)
                else:
                    sp.wait_ge(s("oc_ready"), 1)
                sp.dma_start(ctxT, a["ctxT"][:, b * S:(b + 1) * S]).then_inc(s("c4_in"), 16)
                sp.dma_start(ctxN, a["ctx"][b].rearrange("(k p) l -> p k l", p=P)).then_inc(s("c4_in"), 16)

            def load_w1(e, par):
                sp.dma_start(w1[par].unsqueeze(1), a["w1T"][bass.ds(e, 1)].rearrange("e (c p) f -> p e c f", p=P)
                             ).then_inc(s(f"w1_in{par}"), 16)

            def load_w2(e, par):
                sp.dma_start(w2[par].unsqueeze(1), a["w2T"][bass.ds(e, 1)].rearrange("e (c p) d -> p e c d", p=P)
                             ).then_inc(s(f"w2_in{par}"), 16)

            sp.wait_ge(s("y4_ready"), B)
            load_w1(0, 0)
            sp.wait_ge(s("a5_done"), 1)
            load_w2(0, 0)
            load_w1(1, 1)
            load_w2(1, 1)
            with sp.Fori(1, E // 2) as i:
                for par in range(2):
                    e = 2 * i + par
                    sp.wait_ge(s("w1_split"), e - 1)
                    load_w1(e, par)
                    sp.wait_ge(s("w2_split"), e - 1)
                    load_w2(e, par)
            sp.wait_ge(s("x_done"), 1)
            sp.dma_start(a["out"].rearrange("(j p) f -> p j f", p=P), X[:, :, :]).then_inc(s("out_done"), 16)
            sp.wait_ge(s("out_done"), 16)

        @block.gpsimd
        def _(pool):
            steps = [0]

            def step(ins):
                steps[0] += 1
                ins.then_inc(s("pool_step"), 1)
                pool.wait_ge(s("pool_step"), steps[0])

            def rstd_of(k):
                pool.wait_ge(s("ln_var"), k + 1)
                pool.tensor_tensor(rstd[:, :], mv[:, :, 1], minus_half[:, :], ALU.pow).then_inc(s("ln_rstd"), 1)

            def onezero(view, conds, fill=0.0):
                step(pool.memset(view, 1.0))
                for op, base, pat, mul in conds:
                    step(pool.affine_select(out=view, in_=view, compare_op=op, fill=fill, base=base,
                                            pattern=pat, channel_multiplier=mul))

            step(pool.memset(minus_half[:, :], -0.5))
            onezero(ident[:, :], [(ALU.is_equal, 0, [[-1, P]], 1)])
            step(pool.memset(f32(ident_r[:, :]), 1.0))
            step(pool.affine_select(out=ident_r[:, :], in_=f32(ident_r[:, :]), compare_op=ALU.is_equal, fill=0.0,
                                    base=0, pattern=[[-1, P]], channel_multiplier=1))
            rstd_of(0)

            with pool.Fori(0, NPC // 2) as i:
                for par in range(2):
                    n = 2 * i + par
                    for k in range(2):
                        pool.wait_ge(s("k_copied"), 2 * n + k + 3)
                        pool.wait_ge(s(f"k_out{par}"), KST * (i + 1))
                        pool.tensor_tensor(k_lo[:, par, k, :], k_full[:, par, k, :], f32(k_hi[:, par, k, :]),
                                           ALU.subtract).then_inc(s("kl_done"), 1)

            pool.wait_ge(s("wo_zero"), 1)
            for j in range(GH):
                pool.dma_start(w_o[32 * j:32 * j + DH, :, :],
                               a["woT"].rearrange("(g j d) o -> j d g o", j=GH, d=DH)[j]).then_inc(s("wo_in"), 16)
            step(pool.memset(head_ones, 1.0))
            hv = head_ones.rearrange("p (g c) -> p g c", g=4)
            step(pool.affine_select(out=hv, in_=hv, compare_op=ALU.is_equal, fill=0.0, base=-DH,
                                    pattern=[[-32, 4], [0, 32]], channel_multiplier=1))
            onezero(head_mask[:, :], [(ALU.is_ge, 0, [[-DH, 8]], 1), (ALU.is_ge, DH - 1, [[DH, 8]], -1)])
            sn = f32(sel_n[:, :])
            step(pool.memset(sn[0:32, :], 1.0))
            step(pool.memset(sn[32:64, :], 1.0))
            for r in (0, 32):
                step(pool.affine_select(out=sel_n[r:r + 32, :], in_=sn[r:r + 32, :], compare_op=ALU.is_equal,
                                        fill=0.0, base=0, pattern=[[-1, 32]], channel_multiplier=1))
            step(pool.memset(f32(ones_r[:, :]), 1.0))
            onezero(umask3[:, :, :], [(ALU.is_equal, 0, [[-TOPU, H], [-1, TOPU]], 1)])
            onezero(sel_e[:, :, :].rearrange("p b (h u) -> p b h u", u=TOPU),
                    [(ALU.is_equal, 0, [[-H, B], [-1, H], [0, TOPU]], 1)])
            onezero(bd5[:, :, :].rearrange("p c (h u) -> p c h u", u=TOPU),
                    [(ALU.is_ge, 0, [[P, KF], [-DH, H], [0, TOPU]], 1),
                     (ALU.is_ge, DH - 1, [[-P, KF], [DH, H], [0, TOPU]], -1)])
            onezero(bdT5[:, :].rearrange("p (h d) -> p h d", d=DH),
                    [(ALU.is_ge, 0, [[-TOPU, H], [0, DH]], 1), (ALU.is_ge, TOPU - 1, [[TOPU, H], [0, DH]], -1)])
            pool.sem_inc(s("masks_ready"), 1)

            rstd_of(1)
            k = 0
            for n in range(NST):
                for c in range(KF):
                    pool.wait_ge(s("c_bc_ready"), n + 1)
                    pool.wait_ge(s("h_ready"), k + 1)
                    if k >= 4:
                        pool.wait_ge(s("hc_used"), k - 3)
                    pool.tensor_tensor(hc[:, k % 4, :], h_st[:, k % 4, :], c_bc[:, n % 2, :], ALU.mult
                                       ).then_inc(s("hc_ready"), 1)
                    k += 1

            def w1_low(e, par):
                pool.wait_ge(s("w1_hi_ready"), e + 1)
                pool.tensor_tensor(flat6(w1_lo[par]), flat6(w1[par]), f32(flat6(w1_hi[par])), ALU.subtract
                                   ).then_inc(s("w1_split"), 1)

            def w2_low(e, par):
                pool.wait_ge(s("w2_hi_ready"), e + 1)
                pool.tensor_tensor(flat6(w2_lo[par]), flat6(w2[par]), f32(flat6(w2_hi[par])), ALU.subtract
                                   ).then_inc(s("w2_split"), 1)

            for k in range(2, 6):
                rstd_of(k)

            pool.wait_ge(s("q5_ready"), 1)
            step(pool.iota(iota5.bitcast(mybir.dt.int32), pattern=[[1, L]], base=0, channel_multiplier=0))
            pool.tensor_copy(iota5, iota5.bitcast(mybir.dt.int32)).then_inc(s("iota_ready"), 1)
            for k in range(16):
                b, qt, hq = k // 8, (k // 4) % 2, k % 4
                if k >= 4:
                    pool.wait_ge(s("mx5_ready"), k - 3)
                c = hq // 2
                q = qT5[:, c, b * L + qt * P:b * L + (qt + 1) * P]
                pool.tensor_tensor(qm5[:, k % 4, :, :], q.unsqueeze(1).to_broadcast([P, 4, P]),
                                   head_mask[:, 4 * (hq % 2):4 * (hq % 2) + 4].unsqueeze(2).to_broadcast([P, 4, P]),
                                   ALU.mult).then_inc(s("qm5_ready"), 1)
            w1_low(0, 0)
            rstd_of(6)

            w2_low(0, 0)
            w1_low(1, 1)
            w2_low(1, 1)
            with pool.Fori(1, E // 2) as i:
                for par in range(2):
                    w1_low(2 * i + par, par)
                    w2_low(2 * i + par, par)

        @block.scalar
        def _(act):
            act.sem_inc(s("v_done"), 2)
            act.sem_inc(s("k_copied"), 2)
            act.sem_inc(s("p_ready"), 2)
            act.sem_inc(s("o_evac"), 1)
            act.sem_inc(s("hs_ready"), 4)

            act.wait_ge(s("x_in"), 16)
            act.dma_start(wf[:, :, :, :], a["freqT"].rearrange("m (c p) n -> p m c n", p=P)).then_inc(s("dft_in"), 16)
            act.dma_start(dft[:, :, :, :], a["dft"].rearrange("m (c p) n -> p m c n", p=P)).then_inc(s("dft_in"), 16)
            def xnT_0(k):
                act.wait_ge(s("ln_tr"), TURNS[k])
                act.activation(xnT[:, 0, :], ps[:, 6, :], ACT.Copy).then_inc(s("lnT_a"), 1)

            def project_out(n, par, turn, more=True):
                act.wait_ge(s(f"k_out{par}"), KST * (turn + 1))
                for k in range(2):
                    act.wait_ge(s("kv_ready"), 4 * n + k + 1)
                    act.activation(k_hi[:, par, k, :], ps[:, 4 + k, :], ACT.Copy)
                    act.activation(k_full[:, par, k, :], ps[:, 4 + k, :], ACT.Copy).then_inc(s("k_copied"), 1)
                act.wait_ge(s(f"v_out{par}"), VST * (turn + 1))
                for k in range(2):
                    act.wait_ge(s("kv_ready"), 4 * n + k + 3)
                    for kk in range(2):
                        dst = v_stage[:, par, :, 2 * k + kk, :].rearrange("p g (j v) -> p g j v", v=DH + 1)
                        src = ps[:, 6 + k, kk * D:(kk + 1) * D].rearrange("p (g j v) -> p g j v", g=4, j=GH)
                        ins = act.activation(dst[:, :, :, 0:DH], src, ACT.Copy)
                    ins.then_inc(s("v_done"), 1)
                    if k == 1 and more:
                        act.dma_start(cx[:, par, :], a["ctxT"][:, bass.ds((n + 2) * PK, PK)]
                                      ).then_inc(s(f"cx_in{par}"), 16)

            act.wait_ge(s("v_ones"), 1)
            for n in range(2):
                project_out(n, n, 0)
            act.wait_ge(s("ln_tr"), 1)
            act.activation(xnT[:, 0, :], ps[:, 2, :], ACT.Copy).then_inc(s("lnT_a"), 1)
            for c in range(KF):
                act.wait_ge(s("q_ready"), c + 1)
                act.activation(q_hi[:, c, :], ps[:, c, :], ACT.Copy).then_inc(s("q_hi_ready"), 1)
            project_out(2, 0, 1)
            act.wait_ge(s("uf_ready"), 1)
            act.activation(uf[:, :, :, :].rearrange("p a b c -> p (a b c)"),
                           ps[:, 0:2, :].rearrange("p a b -> p (a b)"), ACT.Copy).then_inc(s("uf_done"), 1)
            project_out(3, 1, 1)
            with act.Fori(1, NPC // 4 - 1) as i:
                for u4 in range(4):
                    project_out(4 * i + u4, u4 % 2, 2 * i + u4 // 2)
            for n in range(NPC - 4, NPC):
                project_out(n, n % 2, n // 2, more=n + 2 < NPC)
            act.dma_start(w_all[:, :, :], a["packed"].rearrange("(c p) n -> p c n", p=P)).then_inc(s("w_in"), 16)
            act.dma_start(w_v1[:, :], a["wv1"]).then_inc(s("w_in"), 16)
            act.dma_start(bc_b[:, :], a["bc_b"]).then_inc(s("w_in"), 16)
            act.dma_start(vecs[:, :, :], a["vecs"]).then_inc(s("w_in"), 16)
            act.dma_start(rows[:, :, :], a["rows"].unsqueeze(0).to_broadcast([P, len(ROWS), D])
                          ).then_inc(s("w_in"), 16)

            def exp_pass(g, par):
                for st in range(KT):
                    for bk in range(2):
                        act.wait_ge(s("s_ready"), 2 * KT * g + 2 * st + bk + 1)
                        act.wait_ge(s("pv_done"), KT * g + st + 1)
                        act.activation(probs[:, (2 * st + bk) % PRING, :], ps[:, 4 + bk, :], ACT.Exp,
                                       scale=SCALE).then_inc(s("p_ready"), 1)
                    if st == 2:
                        act.wait_ge(s("pv_done"), KT * g + 2)
                        act.activation(o_raw[:, bass.ds(g, 1), :], ps[:, 7 - par, 0:L].unsqueeze(1),
                                       ACT.Copy).then_inc(s("o_evac"), 1)

            act.wait_ge(s("kl_done"), 2 * NPC)
            act.wait_ge(s("pv_zero"), 1)
            with act.Fori(0, NG // 2 - 1) as i:
                for par in range(2):
                    exp_pass(2 * i + par, par)
            for par in range(2):
                exp_pass(NG - 2 + par, par)
            act.wait_ge(s("pv_done"), KT * NG + 2)
            act.activation(o_raw[:, NG, :], ps[:, 7, 0:L], ACT.Copy).then_inc(s("o_evac"), 1)

            act.wait_ge(s("w_in"), 16 * 5)
            act.activation(a_dec[:, :, :], a_log[:, :, :], ACT.Exp).then_inc(s("act_step"), 1)
            act.wait_ge(s("act_step"), 1)
            act.activation(a_dec[:, :, :], a_dec[:, :, :], ACT.Exp, scale=-1.0).then_inc(s("a_dec_ready"), 1)
            xnT_0(1)
            for c in range(KF):
                act.wait_ge(s("conv_ready"), c + 1)
                act.activation(u[:, c, :], conv[:, c, :], ACT.Silu).then_inc(s("u_ready"), 1)
            for c in range(KF):
                act.wait_ge(s("gate_mm"), c + 1)
                act.activation(gate[:, c, :], ps[:, c, :], ACT.Silu, bias=vecs[:, GB, c:c + 1]
                               ).then_inc(s("gate_ready"), 1)
            for n in range(NST):
                act.wait_ge(s("c_ready"), n + 1)
                if n >= 2:
                    act.wait_ge(s("hc_ready"), 2 * (n - 1))
                act.activation(c_bc[:, n % 2, :], ps[:, 2 + n % 2, :], ACT.Copy).then_inc(s("c_bc_ready"), 1)

            xnT_0(3)

            def w1_high(e, par, i):
                act.wait_ge(s(f"w1_in{par}"), 16 * (i + 1))
                act.activation(flat6(w1_hi[par]), flat6(w1[par]), ACT.Copy).then_inc(s("w1_hi_ready"), 1)

            def w2_high(e, par, i):
                act.wait_ge(s(f"w2_in{par}"), 16 * (i + 1))
                act.activation(flat6(w2_hi[par]), flat6(w2[par]), ACT.Copy).then_inc(s("w2_hi_ready"), 1)

            xnT_0(4)
            for c in range(KF):
                act.wait_ge(s("q1_mm"), c + 1)
                act.activation(q1T[:, c, :], ps[:, c, :], ACT.Identity, bias=vecs[:, BQ1, c:c + 1]
                               ).then_inc(s("q1_ready"), 1)
            for b in range(B):
                for un in range(8):
                    k = b * 8 + un
                    act.wait_ge(s("s4_ready"), k + 1)
                    if k >= 2:
                        act.wait_ge(s("av4_done"), k - 1)
                        act.wait_ge(s("p4_summed"), k - 1)
                    act.activation(p4[:, k % 2, :], ps[:, 4 + 2 * (k % 2):6 + 2 * (k % 2), :].rearrange(
                        "p a b -> p (a b)"), ACT.Exp).then_inc(s("p4_ready"), 1)

            xnT_0(5)
            for c in range(KF):
                act.wait_ge(s("qk5_mm"), c + 1)
                ins = act.activation(qT5[:, c, :], ps[:, c, :], ACT.Identity, bias=vecs[:, BQ5, c:c + 1])
            ins.then_inc(s("q5_ready"), 1)
            for c in range(KF):
                act.wait_ge(s("qk5_mm"), c + 3)
                ins = act.activation(kT5[:, c, :], ps[:, 2 + c, :], ACT.Identity, bias=vecs[:, BK5, c:c + 1])
            ins.then_inc(s("k5_ready"), 1)
            w1_high(0, 0, 0)
            for b in range(B):
                act.wait_ge(s("ss5_ready"), b + 1)
                act.wait_ge(s("nm5_ready"), b + 1)
                act.activation(p5[0:HU, b, :], ps[0:HU, 2 + b, 0:L], ACT.Exp, scale=SCALE, bias=c5[0:HU, b, 0:1],
                               accum_out=sum5[0:HU, b:b + 1]).then_inc(s("p5_ready"), 1)

            xnT_0(6)
            w2_high(0, 0, 0)
            act.wait_ge(s("r_ready"), 1)
            act.activation(p6.rearrange("p a b -> p (a b)"), r6.rearrange("p a b -> p (a b)"), ACT.Exp
                           ).then_inc(s("r_exp"), 1)
            def expert(e, between):
                for ft in range(FT):
                    act.wait_ge(s("hm_ready"), FT * e + ft + 1)
                    act.wait_ge(s("h_split"), FT * e + ft + 1)
                    act.activation(h_f[:, ft % 4, :], ps[:, ft % 4, :], ACT.Silu).then_inc(s("hs_ready"), 1)
                    if ft in between:
                        between[ft]()

            def w2_next(e, par, i):
                act.wait_ge(s("y_ready"), e)
                w2_high(e + 1, 1 - par, i)

            expert(0, {1: lambda: w1_high(1, 1, 0), 3: lambda: w2_high(1, 1, 0), 7: lambda: w1_high(2, 0, 1)})
            with act.Fori(0, 2) as i:
                expert(2 * i + 1, {3: lambda: w2_next(2 * i + 1, 1, i + 1), 7: lambda: w1_high(2 * i + 3, 1, i + 1)})
                expert(2 * i + 2, {3: lambda: w2_next(2 * i + 2, 0, i + 1), 7: lambda: w1_high(2 * i + 4, 0, i + 2)})
            expert(5, {3: lambda: w2_next(5, 1, 3), 7: lambda: w1_high(7, 1, 3)})
            expert(6, {3: lambda: w2_next(6, 0, 3)})
            expert(7, {})

        @block.tensor
        def _(pe):
            def mm(out, lhsT, rhs, start=True, stop=True):
                return pe.matmul(out, lhsT, rhs, start=start, stop=stop, skip_group_check=True)

            pe.sem_inc(s("pv_done"), 2)

            def transpose_xn(k, bank=6):
                pe.wait_ge(s("ln_xn"), TURNS[k])
                for c in range(KF):
                    for j in range(NT):
                        ins = pe.transpose(ps[:, bank + c, j * P:(j + 1) * P], xn[:, j, c * P:(c + 1) * P], ident[:, :])
                ins.then_inc(s("ln_tr"), 1)
                pe.wait_ge(s("lnT_a"), TURNS[k])
                pe.wait_ge(s("lnT_d"), TURNS[k])

            def project(par, i, m):
                n = 2 * i + par
                if m == 0:
                    pe.wait_ge(s(f"cx_in{par}"), 16 * (i + 1))
                if m < 2:
                    pe.wait_ge(s("k_copied"), 2 * n + m + 1)
                    ins = mm(ps[:, 4 + m, :], w_kv[:, m * P:(m + 1) * P], cx[:, par, :])
                else:
                    pe.wait_ge(s("v_done"), 2 * n + m - 1)
                    for kk in range(2):
                        t = 2 * (m - 2) + kk
                        ins = mm(ps[:, 4 + m, kk * D:(kk + 1) * D], cx[:, par, t * P:(t + 1) * P], w_kv[:, D:2 * D])
                ins.then_inc(s("kv_ready"), 1)

            pe.wait_ge(s("wkv_in"), 16)
            for n in range(2):
                for m in range(4):
                    project(n, 0, m)

            pe.wait_ge(s("pool_step"), 3)
            transpose_xn(0, 2)
            pe.wait_ge(s("w0_in"), 16)
            for m in range(KF):
                for c in range(KF):
                    ins = mm(ps[:, m, :], w_a[:, c, m * P:(m + 1) * P], xnT[:, c, :], c == 0, c == KF - 1)
                ins.then_inc(s("q_ready"), 1)
            for m in range(4):
                project(0, 1, m)

            pe.wait_ge(s("dft_in"), 32)
            pe.wait_ge(s("q_hi_ready"), KF)
            pe.wait_ge(s("q_lo_ready"), KF)
            terms = (((0, 0), (1, 2)), ((0, 1), (1, 0)))
            for r in range(2):
                for m in range(KF):
                    n = 0
                    for wi, ti in terms[r]:
                        for c in range(KF):
                            ins = mm(ps[:, r, m * D:(m + 1) * D], wf[:, wi, c, m * P:(m + 1) * P], dft[:, ti, c, :],
                                     n == 0, n == 3)
                            n += 1
            ins.then_inc(s("uf_ready"), 1)
            for m in range(4):
                project(1, 1, m)
            pe.wait_ge(s("uf_done"), 1)
            for m in range(KF):
                n = 0
                for r in range(2):
                    for c in range(KF):
                        ins = mm(ps[:, 2, m * D:(m + 1) * D], dft[:, 3 + r, c, m * P:(m + 1) * P], uf[:, r, c, :],
                                 n == 0, n == 3)
                        n += 1
            ins.then_inc(s("m_mm"), 1)

            def max_half(g, par, k):
                un, hf = k // 2, k % 2
                c, j, qt = un // 8, (un % 8) // 2, un % 2
                if k == 0:
                    pe.wait_ge(s(f"qm_in{par}"), LOADQ * grp(g, par))
                if k % 16 == 0:
                    pe.wait_ge(s(f"ks_in{par}{c}"), LOADK * grp(g, par))
                if k == 0 and not (isinstance(g, int) and g == 0):
                    pe.wait_ge(s("nm_row"), g)
                if hf == 0:
                    pe.wait_ge(s("mx_used"), UNITS * g + un + 1)
                q0 = (j % 2) * L + qt * P
                k0 = c * CK + hf * 512
                ins = mm(ps[:, 2 * (un % 2) + hf, :], qm_stack[0:RS, par, j // 2, q0:q0 + P],
                         k_stack[0:RS, par, j // 2, k0:k0 + 512])
                if hf == 1:
                    ins.then_inc(s("mx_ready"), 1)

            def grp(g, par):
                if isinstance(g, int):
                    return g // 2 + 1
                return loads[0]

            loads = [None]

            def max_turn(g):
                pe.wait_ge(s("nm_ready"), g + 1)
                for c in range(8):
                    ins = mm(ps[0:1, c // 4, (c % 4) * P:(c % 4 + 1) * P], nm_t[:, c:c + 1], ident_r[:, :])
                ins.then_inc(s("nmt_ready"), 1)

            def scores(g, par, st, bk):
                if st == 0 and bk == 0:
                    pe.wait_ge(s(f"qe_in{par}"), LOADQ * grp(g, par))
                    pe.wait_ge(s("nm_row"), (g + 1))
                pe.wait_ge(s("p_ready"), 2 * KT * g + 2 * st + bk + 1)
                mm(ps[:, 4 + bk, :], k_stack[0:RS + 1, par, bk, st * P:(st + 1) * P], qe_stack[0:RS + 1, par, bk, :]
                   ).then_inc(s("s_ready"), 1)

            def values(g, par, st):
                if st == 0:
                    pe.wait_ge(s(f"vs_in{par}"), 16 * grp(g, par))
                    pe.wait_ge(s("o_evac"), g + 1)
                pe.wait_ge(s("p_ready"), 2 * KT * g + 2 * st + 4)
                for j in range(GH):
                    ins = mm(ps[32 * j:32 * j + DH + 1, 6 + par, 0:L],
                             v_grp[:, par, st, j * (DH + 1):(j + 1) * (DH + 1)],
                             probs[:, (2 * st + j // 2) % PRING, (j % 2) * L:(j % 2 + 1) * L], st == 0, st == KT - 1)
                ins.then_inc(s("pv_done"), 1)

            def halves_at(st, slot):
                return [k for k in range(2 * UNITS) if k * MAX_SLOTS // (2 * UNITS) == 3 * st + slot]

            def group_pass(g, par, following, load_now, load_next):
                def max_part(st, slot):
                    if following:
                        loads[0] = load_next
                        for k in halves_at(st, slot):
                            max_half(g + 1, 1 - par, k)
                        if (st, slot) == TURN_SLOT:
                            max_turn(g + 1)

                def scores_part(st, bk):
                    if st + 1 < KT:
                        loads[0] = load_now
                        scores(g, par, st + 1, bk)
                    elif following:
                        loads[0] = load_next
                        scores(g + 1, 1 - par, 0, bk)

                for st in range(KT):
                    scores_part(st, 0)
                    max_part(st, 0)
                    scores_part(st, 1)
                    max_part(st, 1)
                    loads[0] = load_now
                    values(g, par, st)
                    max_part(st, 2)

            un = 0
            for n in range(4, NPC):
                for m in range(4):
                    project(n % 2, n // 2, m)
                    if n >= 5 and m >= 1 and un < UNITS:
                        if un == 0:
                            pe.wait_ge(s("m_ready"), 1)
                        max_half(0, 0, 2 * un)
                        max_half(0, 0, 2 * un + 1)
                        un += 1
            max_turn(0)
            pe.wait_ge(s("k_copied"), 2 * NPC + 2)
            pe.wait_ge(s("v_done"), 2 * NPC + 2)
            pe.wait_ge(s("pv_zero"), 1)
            pe.wait_ge(s("ones_rows"), 2)
            for bk in range(2):
                scores(0, 0, 0, bk)
            with pe.Fori(0, NG // 2 - 1) as i:
                group_pass(2 * i, 0, True, i + 1, i + 1)
                group_pass(2 * i + 1, 1, True, i + 1, i + 2)
            group_pass(NG - 2, 0, True, NG // 2, NG // 2)
            group_pass(NG - 1, 1, False, NG // 2, NG // 2)

            pe.wait_ge(s("o_evac"), NG + 2)
            pe.wait_ge(s("masks_ready"), 1)
            for g in range(NG):
                if g >= 2:
                    pe.wait_ge(s("o_norm"), g - 1)
                mm(ps[:, g % 2, 0:L], head_ones, o_raw[:, g + 1, :]).then_inc(s("o_sums"), 1)
            pe.wait_ge(s("wo_in"), 16 * GH)
            for j in range(NT):
                b = j // QT
                pe.wait_ge(s("o_norm"), 4 * (b + 1))
                for g in range(4):
                    ins = mm(ps[:, 2 + j // 2, (j % 2) * D:(j % 2 + 1) * D], o_n[:, 4 * b + g, (j % 2) * P:(j % 2 + 1) * P],
                             w_o[:, g, :], g == 0, g == 3)
            ins.then_inc(s("y1_ready"), 1)

            transpose_xn(1)
            pe.wait_ge(s("w_in"), 16 * 5)
            for m in range(KF):
                for c in range(KF):
                    ins = mm(ps[:, m, :], w_gate[:, c, m * P:(m + 1) * P], xnT[:, c, :], c == 0, c == KF - 1)
                ins.then_inc(s("gate_mm"), 1)
            pe.wait_ge(s("u_ready"), KF)
            for c in range(KF):
                ins = mm(ps[0:64, 2, :], bc_w[:, c, :], u[:, c, :], c == 0, c == KF - 1)
            ins.then_inc(s("bc_mm"), 1)
            pe.wait_ge(s("gate_ready"), KF)
            pe.wait_ge(s("bc_ready"), 1)

            def add_states(n):
                for c in range(KF):
                    k = KF * n + c
                    pe.wait_ge(s("hc_ready"), k + 1)
                    mm(ps[:, 4 + c, :], ident[:, :], hc[:, k % 4, :], n == 0, n == NST - 1).then_inc(s("hc_used"), 1)

            for n in range(NST):
                if n >= 2:
                    pe.wait_ge(s("b_used"), n - 1)
                mm(ps[:, n % 2, :], sel_n[:, n:n + 1].to_broadcast([64, P]), bc_hl[:, :]).then_inc(s("b_ready"), 1)
                if n >= 2:
                    pe.wait_ge(s("c_bc_ready"), n - 1)
                mm(ps[:, 2 + n % 2, :], sel_n[:, 16 + n:17 + n].to_broadcast([64, P]), bc_hl[:, :]
                   ).then_inc(s("c_ready"), 1)
                if n >= 1:
                    add_states(n - 1)
            add_states(NST - 1)
            pe.wait_ge(s("yT_ready"), 1)
            for j in range(NT):
                for c in range(KF):
                    ins = mm(ps[:, 6 + j // 2, (j % 2) * D:(j % 2 + 1) * D], yT[:, c, j * P:(j + 1) * P], w_out[:, c, :],
                             c == 0, c == KF - 1)
            ins.then_inc(s("y2_ready"), 1)

            transpose_xn(3)
            for j in range(NT):
                for c in range(KF):
                    ins = mm(ps[:, j // 2, (j % 2) * D:(j % 2 + 1) * D], xnT[:, c, j * P:(j + 1) * P], m_dft[:, c, :],
                             c == 0, c == KF - 1)
            ins.then_inc(s("y3_ready"), 1)

            transpose_xn(4)
            for m in range(KF):
                for c in range(KF):
                    ins = mm(ps[:, m, :], w_q1[:, c, m * P:(m + 1) * P], xnT[:, c, :], c == 0, c == KF - 1)
                ins.then_inc(s("q1_mm"), 1)
            pe.wait_ge(s("q1_ready"), KF)
            for c in range(KF):
                ins = mm(ps[:, 2, :], w_k1[:, c, :], q1T[:, c, :], c == 0, c == KF - 1)
            ins.then_inc(s("qp_mm"), 1)
            for j in range(NT):
                for c in range(KF):
                    ins = mm(ps[:, 3, j:j + 1], q1T[:, c, j * P:(j + 1) * P], vecs[:, BK1, c:c + 1], c == 0, c == KF - 1)
            ins.then_inc(s("qbk_mm"), 1)
            pe.wait_ge(s("qp_ready"), 1)
            pe.wait_ge(s("qbk_ready"), 1)
            for b in range(B):
                pe.wait_ge(s("c4_in"), 32 * (b + 1))
                for un in range(8):
                    k = b * 8 + un
                    qt, c = un // 4, un % 4
                    if k >= 2:
                        pe.wait_ge(s("mx4_used"), k - 1)
                    if b and un < 2:
                        pe.wait_ge(s("p4_ready"), 8 * b)
                    for hf in range(2):
                        ins = mm(ps[:, 4 + 2 * (k % 2) + hf, :], qpT[:, b * L + qt * P:b * L + (qt + 1) * P],
                                 ctxT[:, c * CK + hf * 512:c * CK + (hf + 1) * 512])
                    ins.then_inc(s("mx4_ready"), 1)
                pe.wait_ge(s("nm4_cols"), b + 1)
                for qt in range(QT):
                    ins = mm(ps[0:1, 3, qt * P:(qt + 1) * P], nm4f[:, qt:qt + 1], ident[:, :])
                ins.then_inc(s("nm4_turned"), 1)
                pe.wait_ge(s("nm4_ready"), b + 1)

                def scores4(un):
                    k = b * 8 + un
                    if un >= 2:
                        pe.wait_ge(s("p4_ready"), k - 1)
                    for t in range(4):
                        kt = 4 * un + t
                        o = ps[:, 4 + 2 * (k % 2) + t // 2, (t % 2) * L:(t % 2 + 1) * L]
                        mm(o, ctxT[:, kt * P:(kt + 1) * P], qpT[:, b * L:(b + 1) * L], True, False)
                        ins = mm(o, ones_r[:, :], nm4[:, :], False, True)
                    ins.then_inc(s("s4_ready"), 1)

                def values4(un):
                    k = b * 8 + un
                    pe.wait_ge(s("p4_ready"), k + 1)
                    for t in range(4):
                        kt = 4 * un + t
                        ins = mm(ps[:, 0, 0:L], ctxN[:, kt, :], p4[:, k % 2, t * L:(t + 1) * L], kt == 0, kt == KT - 1)
                    ins.then_inc(s("av4_done"), 1)

                scores4(0)
                for un in range(8):
                    if un < 7:
                        scores4(un + 1)
                    values4(un)
                pe.wait_ge(s("p4_summed"), 8 * (b + 1))
                for t in range(4):
                    ins = mm(ps[:, 1, 0:L], ones, psumP[:, t * L:(t + 1) * L], t == 0, t == 3)
                ins.then_inc(s("oc_sum"), 1)
                pe.wait_ge(s("oc_ready"), b + 1)
                for qt in range(QT):
                    ins = mm(ps[:, 2, qt * D:(qt + 1) * D], ocT[:, qt * P:(qt + 1) * P], w_v1[:, :])
                ins.then_inc(s("y4_ready"), 1)

            transpose_xn(5)
            for w in range(2):
                for m in range(KF):
                    for c in range(KF):
                        ins = mm(ps[:, 2 * w + m, :], w5[w][:, c, m * P:(m + 1) * P], xnT[:, c, :], c == 0, c == KF - 1)
                    ins.then_inc(s("qk5_mm"), 1)
            for w in range(2):
                for j in range(NT):
                    for c in range(KF):
                        ins = mm(ps[:, 4 + 2 * w + j // 2, (j % 2) * D:(j % 2 + 1) * D], xnT[:, c, j * P:(j + 1) * P],
                                 w5[2 * w][:, c, :], c == 0, c == KF - 1)
                ins.then_inc(s("qv5_mm"), 1)
            pe.wait_ge(s("k5_ready"), 1)
            pe.wait_ge(s("qv5_ready"), 2)
            for k in range(16):
                b, qt, hq = k // 8, (k // 4) % 2, k % 4
                pe.wait_ge(s("qm5_ready"), k + 1)
                if k >= 2:
                    pe.wait_ge(s("mx5_used"), k - 1)
                for j in range(4):
                    ins = mm(ps[:, 2 * (k % 2) + j // 2, (j % 2) * L:(j % 2 + 1) * L], qm5[:, k % 4, j, :],
                             kT5[:, hq // 2, b * L:(b + 1) * L])
                ins.then_inc(s("mx5_ready"), 1)
            pe.wait_ge(s("mx5_used"), 16)
            for qt in range(QT):
                ins = pe.transpose(ps[0:B * H, 4, qt * P:(qt + 1) * P], mx5[:, qt, :], ident[:, :])
            ins.then_inc(s("mT5_mm"), 1)
            pe.wait_ge(s("idx5_ready"), 1)
            for b in range(B):
                ins = mm(ps[0:HU, 5, 16 * b:16 * b + 16], sel_e[:, b, :], i5[0:B * H, :])
            ins.then_inc(s("c5_mm"), 1)
            pe.wait_ge(s("oneT_ready"), 1)
            for b in range(B):
                for qt in range(QT):
                    ins = pe.transpose(ps[:, 4, (2 * b + qt) * P:(2 * b + qt) * P + HU],
                                       oneT[0:HU, b, qt * P:(qt + 1) * P], ident[0:HU, 0:HU])
            ins.then_inc(s("oneN_mm"), 1)
            pe.wait_ge(s("oneN_ready"), 1)
            for b in range(B):
                for c in range(KF):
                    for qt in range(QT):
                        ins = mm(ps[:, 0, (2 * b + c) * P:(2 * b + c) * P + HU], qn5[:, 2 * b + qt, c * P:(c + 1) * P],
                                 oneN[:, b, qt, :], qt == 0, qt == QT - 1)
            ins.then_inc(s("qsel_mm"), 1)
            pe.wait_ge(s("qsel_ready"), 1)
            for b in range(B):
                for c in range(KF):
                    ins = mm(ps[0:HU, 2 + b, 0:L], qsel[:, b, c, :], kT5[:, c, b * L:(b + 1) * L], c == 0, c == KF - 1)
                ins.then_inc(s("ss5_ready"), 1)
            for b in range(B):
                pe.wait_ge(s("p5_ready"), b + 1)
                for kt in range(QT):
                    ins = pe.transpose(ps[:, 4 + b, kt * P:kt * P + HU],
                                       p5[0:HU, b, kt * P:(kt + 1) * P], ident[0:HU, 0:HU])
                ins.then_inc(s("pT5_mm"), 1)
            for b in range(B):
                pe.wait_ge(s("pT5_ready"), b + 1)
                for kt in range(QT):
                    ins = mm(ps[0:HU, 6 + b, 0:D], pT5[:, b, kt, :], vn5[:, 2 * b + kt, :], kt == 0, kt == QT - 1)
                ins.then_inc(s("o5_mm"), 1)
            for b in range(B):
                pe.wait_ge(s("om5_ready"), b + 1)
                for c in range(KF):
                    ins = mm(ps[:, c, b * L:(b + 1) * L], om5[0:HU, b, c * P:(c + 1) * P], oneT[0:HU, b, :])
                ins.then_inc(s("oT5_mm"), 1)
            pe.wait_ge(s("oT5_ready"), 1)
            for j in range(NT):
                for c in range(KF):
                    ins = mm(ps[:, 2 + j // 2, (j % 2) * D:(j % 2 + 1) * D], oT5[:, c, j * P:(j + 1) * P], w5[3][:, c, :],
                             c == 0, c == KF - 1)
            ins.then_inc(s("y5_ready"), 1)

            transpose_xn(6)
            for j in range(NT):
                for c in range(KF):
                    ins = mm(ps[:, 4, E * j:E * (j + 1)], xnT[:, c, j * P:(j + 1) * P], w_r[:, c, :], c == 0, c == KF - 1)
            ins.then_inc(s("r_mm"), 1)
            pe.wait_ge(s("r_copied"), 1)
            pe.wait_ge(s("xn_hi_ready"), 1)
            pe.wait_ge(s("xn_lo_ready"), 1)
            with pe.Fori(0, E // 2) as i:
                for par in range(2):
                    e = 2 * i + par
                    pe.wait_ge(s("w1_split"), e + 1)
                    for ft in range(FT):
                        pe.wait_ge(s("hs_ready"), FT * e + ft + 1)
                        n = 0
                        for w, v in ((w1_hi, xn_hi), (w1_hi, xn_lo), (w1_lo, xn_hi)):
                            for c in range(KF):
                                ins = mm(ps[:, ft % 4, :], w[par][:, c, ft * P:(ft + 1) * P], v[:, c, :], n == 0, n == 5)
                                n += 1
                        ins.then_inc(s("hm_ready"), 1)
                    pe.wait_ge(s("w2_split"), e + 1)
                    pe.wait_ge(s("y_used"), NT * (e + 1))
                    for ft in range(FT):
                        pe.wait_ge(s("h_split"), FT * e + ft + 1 + 4)
                        for j in range(NT):
                            n = 0
                            for v, w in ((h_hi, w2_hi), (h_hi, w2_lo), (h_lo, w2_hi)):
                                ins = mm(ps[:, 4 + j, 0:D], v[ft][:, j * P:(j + 1) * P], w[par][:, ft, :],
                                         ft == 0 and n == 0, ft == FT - 1 and n == 2)
                                n += 1
                    ins.then_inc(s("y_ready"), 1)

        @block.vector
        def _(dve):
            steps = [0]

            def step(ins):
                steps[0] += 1
                ins.then_inc(s("dve_step"), 1)
                dve.wait_ge(s("dve_step"), steps[0])

            dve.sem_inc(s("mx_used"), 2)
            dve.sem_inc(s("y_used"), NT)
            dve.sem_inc(s("h_split"), 4)

            def tiles(bank):
                return ps[:, bank:bank + 2, :].rearrange("p a (b d) -> p (a b) d", d=D)

            def layernorm(k, src, transposed=True):
                for j in range(NT):
                    ins = dve.bn_stats(stats[:, j, :], src[:, j, :])
                step(ins)
                for j in range(NT):
                    ins = dve.bn_aggr(mv[:, j, :], stats[:, j, :])
                step(ins)
                dve.tensor_scalar(mv[:, :, 1], mv[:, :, 1], EPS, None, ALU.add).then_inc(s("ln_var"), 1)
                dve.wait_ge(s("ln_rstd"), k + 1)
                for j in range(NT):
                    ins = dve.tensor_scalar(xn[:, j, :], src[:, j, :], mv[:, j, 0:1], rstd[:, j:j + 1],
                                            ALU.subtract, ALU.mult)
                if not transposed:
                    step(ins)
                    return
                ins.then_inc(s("ln_xn"), 1)

            def xnT_1(k):
                dve.wait_ge(s("ln_tr"), TURNS[k])
                dve.tensor_copy(xnT[:, 1, :], ps[:, 7, :]).then_inc(s("lnT_d"), 1)

            dve.memset(v_stage, 1.0).then_inc(s("v_ones"), 1)
            dve.wait_ge(s("x_in"), 16)
            layernorm(0, X)
            dve.memset(f32(qm_stack[:, :, :, :]), 0.0).then_inc(s("q_zero"), 1)
            dve.wait_ge(s("ln_tr"), 1)
            dve.tensor_copy(xnT[:, 1, :], ps[:, 3, :]).then_inc(s("lnT_d"), 1)
            for c in range(KF):
                dve.wait_ge(s("q_hi_ready"), c + 1)
                dve.tensor_tensor(q_lo[:, c, :], ps[:, c, :], f32(q_hi[:, c, :]), ALU.subtract
                                  ).then_inc(s("q_lo_ready"), 1)
            dve.memset(f32(qe_stack[:, :, :, :]), 0.0).then_inc(s("q_zero"), 1)
            dve.memset(w_o[:, :, :], 0.0).then_inc(s("wo_zero"), 1)
            dve.memset(f32(k_stack[RS:RS + 1, 0, :, :]), 1.0).then_inc(s("ones_rows"), 1)
            dve.wait_ge(s("q_out"), 16 * 2 * B)
            dve.memset(f32(k_stack[RS:RS + 1, 1, :, :]), 1.0).then_inc(s("ones_rows"), 1)
            dve.wait_ge(s("m_mm"), 1)
            dve.tensor_copy(m_dft[:, :, :].rearrange("p a b -> p (a b)"), ps[:, 2, :]).then_inc(s("m_ready"), 1)
            dve.wait_ge(s("m_ready"), 1)
            dve.sem_inc(s("dft_done"), 1)

            def max_pass(g, par):
                for un in range(UNITS):
                    c, j, qt = un // 8, (un % 8) // 2, un % 2
                    dve.wait_ge(s("mx_ready"), UNITS * g + un + 1)
                    dve.tensor_reduce(mxp[:, 2 * j + qt, c:c + 1],
                                      ps[:, 2 * (un % 2):2 * (un % 2) + 2, :].rearrange("p a b -> p (a b)"),
                                      AX.X, ALU.max).then_inc(s("mx_used"), 1)
                dve.wait_ge(s("mx_used"), UNITS * (g + 1) + 2)
                dve.tensor_reduce(nm_t[:, :], mxp, AX.X, ALU.max, negate=True).then_inc(s("nm_ready"), 1)
                dve.wait_ge(s("nmt_ready"), g + 1)
                dve.tensor_copy(qe_stack[RS:RS + 1, par, :, :], ps[0:1, 0:2, :]).then_inc(s("nm_row"), 1)

            dve.wait_ge(s("q_zero"), 2)
            max_pass(0, 0)
            dve.wait_ge(s("v_done"), 2 * NPC + 2)
            dve.memset(ps[:, 6:8, 0:L], 0.0).then_inc(s("pv_zero"), 1)
            with dve.Fori(0, NG // 2 - 1) as i:
                for par in range(2):
                    max_pass(2 * i + par + 1, 1 - par)
            max_pass(NG - 1, 1)

            for g in range(NG):
                dve.wait_ge(s("o_sums"), g + 1)
                step(dve.reciprocal(o_sum[:, g % 2, :], ps[:, g % 2, 0:L]))
                dve.tensor_tensor(o_n[:, g, :], o_raw[:, g + 1, :], o_sum[:, g % 2, :], ALU.mult
                                  ).then_inc(s("o_norm"), 1)
            dve.wait_ge(s("y1_ready"), 1)
            step(dve.tensor_tensor(X[:, :, :], X[:, :, :], tiles(2), ALU.add))

            layernorm(1, X)
            for c in range(KF):
                step(dve.memset(xpad[:, c, :, 0:TAPS - 1], 0.0))
            dve.wait_ge(s("ln_tr"), 2)
            xnT_1(1)
            dve.wait_ge(s("lnT_d"), 2)
            dve.wait_ge(s("lnT_a"), 2)
            dve.wait_ge(s("w_in"), 16 * 5)
            for c in range(KF):
                step(dve.tensor_copy(xpad[:, c, :, TAPS - 1:], xnT[:, c, :].rearrange("p (b l) -> p b l", b=B)))
                cv = conv[:, c, :].rearrange("p (b l) -> p b l", b=B)
                step(dve.tensor_scalar(cv, xpad[:, c, :, 0:L], conv_w[:, c, 0:1], vecs[:, CB, c:c + 1],
                                       ALU.mult, ALU.add))
                for t in range(1, TAPS):
                    ins = dve.scalar_tensor_tensor(cv, xpad[:, c, :, t:t + L], conv_w[:, c, t:t + 1], cv,
                                                   ALU.mult, ALU.add)
                    if t < TAPS - 1:
                        step(ins)
                ins.then_inc(s("conv_ready"), 1)
            dve.wait_ge(s("bc_mm"), 1)
            step(dve.tensor_scalar(bcf[0:64, :], ps[0:64, 2, :], bc_b[:, 0:1], None, ALU.add))
            step(dve.tensor_copy(bc_hl[:, :], bcf[0:64, :]))
            dve.tensor_tensor(bc_hl[32:64, :], bcf[32:64, :], f32(bc_hl[32:64, :]), ALU.subtract
                              ).then_inc(s("bc_ready"), 1)
            dve.wait_ge(s("u_ready"), KF)
            dve.wait_ge(s("a_dec_ready"), 1)
            k = 0
            for n in range(NST):
                dve.wait_ge(s("b_ready"), n + 1)
                if n >= 2:
                    dve.wait_ge(s("h_ready"), KF * (n - 1))
                for c in range(KF):
                    ins = dve.tensor_tensor(b_in[:, 2 * (n % 2) + c, :], u[:, c, :], ps[:, n % 2, :], ALU.mult)
                    if c == KF - 1:
                        ins.then_inc(s("b_used"), 1)
                dve.wait_ge(s("b_used"), n + 1)
                for c in range(KF):
                    if k >= 4:
                        dve.wait_ge(s("hc_ready"), k - 3)
                    for b in range(B):
                        ins = dve.tensor_tensor_scan(h_st[:, k % 4, b * L:(b + 1) * L],
                                                     a_dec[:, c, n:n + 1].to_broadcast([P, L]),
                                                     b_in[:, 2 * (n % 2) + c, b * L:(b + 1) * L], 0.0, ALU.mult, ALU.add)
                    ins.then_inc(s("h_ready"), 1)
                    k += 1
            dve.wait_ge(s("h_ready"), k)
            dve.wait_ge(s("gate_ready"), KF)
            dve.wait_ge(s("hc_used"), k)
            for c in range(KF):
                step(dve.scalar_tensor_tensor(yT[:, c, :], u[:, c, :], vecs[:, DD, c:c + 1], ps[:, 4 + c, :],
                                              ALU.mult, ALU.add))
                ins = dve.tensor_tensor(yT[:, c, :], yT[:, c, :], gate[:, c, :], ALU.mult)
            ins.then_inc(s("yT_ready"), 1)
            step(dve.tensor_tensor(xn[:, :, :], xn[:, :, :], scaled_rows(rows[:, OB, :], NT), ALU.add))
            dve.wait_ge(s("y2_ready"), 1)
            step(dve.tensor_tensor(xn[:, :, :], xn[:, :, :], tiles(6), ALU.add))
            layernorm(2, xn, transposed=False)
            step(dve.tensor_tensor(xn[:, :, :], xn[:, :, :], scaled_rows(rows[:, LG, :], NT), ALU.mult))
            step(dve.tensor_tensor(X[:, :, :], X[:, :, :], scaled_rows(rows[:, LB, :], NT), ALU.add))
            step(dve.tensor_tensor(X[:, :, :], X[:, :, :], xn[:, :, :], ALU.add))

            def add_rows(i):
                step(dve.tensor_tensor(X[:, :, :], X[:, :, :], scaled_rows(rows[:, i, :], NT), ALU.add))

            layernorm(3, X)
            xnT_1(3)
            add_rows(FB)
            dve.wait_ge(s("y3_ready"), 1)
            step(dve.tensor_tensor(X[:, :, :], X[:, :, :], tiles(0), ALU.add))

            layernorm(4, X)
            xnT_1(4)
            add_rows(BV1)
            step(dve.memset(ones, 1.0))
            dve.wait_ge(s("qp_mm"), 1)
            dve.tensor_copy(qpT, ps[:, 2, :]).then_inc(s("qp_ready"), 1)
            dve.wait_ge(s("qbk_mm"), 1)
            dve.tensor_copy(qbk[:, 0:NT], ps[:, 3, 0:NT]).then_inc(s("qbk_ready"), 1)
            for b in range(B):
                for un in range(8):
                    k = b * 8 + un
                    dve.wait_ge(s("mx4_ready"), k + 1)
                    dve.tensor_reduce(mx4[:, un // 4, un % 4:un % 4 + 1],
                                      ps[:, 4 + 2 * (k % 2):6 + 2 * (k % 2), :].rearrange("p a b -> p (a b)"),
                                      AX.X, ALU.max).then_inc(s("mx4_used"), 1)
                dve.wait_ge(s("mx4_used"), 8 * (b + 1))
                step(dve.tensor_reduce(mx4[:, :, 4:5], mx4[:, :, 0:4], AX.X, ALU.max))
                qb = qbk[:, 2 * b:2 * b + 2].unsqueeze(2)
                step(dve.tensor_tensor(mx4[:, :, 5:6], mx4[:, :, 4:5], qb, ALU.add))
                dve.tensor_tensor(nm4f.unsqueeze(2), qb, mx4[:, :, 5:6], ALU.subtract).then_inc(s("nm4_cols"), 1)
                dve.wait_ge(s("nm4_turned"), b + 1)
                dve.tensor_copy(nm4[:, :], ps[0:1, 3, 0:L]).then_inc(s("nm4_ready"), 1)
                for un in range(8):
                    k = b * 8 + un
                    dve.wait_ge(s("p4_ready"), k + 1)
                    if un == 0:
                        if b:
                            dve.wait_ge(s("oc_sum"), b)
                        dve.tensor_copy(psumP, p4[:, k % 2, :]).then_inc(s("p4_summed"), 1)
                    else:
                        dve.wait_ge(s("p4_summed"), k)
                        dve.tensor_tensor(psumP, psumP, p4[:, k % 2, :], ALU.add).then_inc(s("p4_summed"), 1)
                dve.wait_ge(s("oc_sum"), b + 1)
                step(dve.reciprocal(rs4, ps[:, 1, 0:L]))
                dve.wait_ge(s("av4_done"), 8 * (b + 1))
                dve.tensor_tensor(ocT, ps[:, 0, 0:L], rs4, ALU.mult).then_inc(s("oc_ready"), 1)
                dve.wait_ge(s("y4_ready"), b + 1)
                step(dve.tensor_tensor(X[:, 2 * b:2 * b + 2, :], X[:, 2 * b:2 * b + 2, :],
                                       ps[:, 2, :].rearrange("p (a d) -> p a d", d=D), ALU.add))

            layernorm(5, X)
            xnT_1(5)
            add_rows(BO5)
            for w, dst in ((0, qn5), (1, vn5)):
                dve.wait_ge(s("qv5_mm"), w + 1)
                dve.tensor_tensor(dst, tiles(4 + 2 * w), scaled_rows(rows[:, BQ5R if w == 0 else BV5, :], NT), ALU.add
                                  ).then_inc(s("qv5_ready"), 1)
            for k in range(16):
                b, qt, hq = k // 8, (k // 4) % 2, k % 4
                dve.wait_ge(s("mx5_ready"), k + 1)
                dve.tensor_reduce(mx5[:, qt, b * H + 4 * hq:b * H + 4 * hq + 4],
                                  ps[:, 2 * (k % 2):2 * (k % 2) + 2, :].rearrange("p a (b q) -> p (a b) q", q=L),
                                  AX.X, ALU.max).then_inc(s("mx5_used"), 1)
            dve.wait_ge(s("mT5_mm"), 1)
            mT = mT5[0:B * H, :]
            step(dve.tensor_copy(mT, ps[0:B * H, 4, 0:L]))
            step(dve.max(i5[0:B * H, 8:16], mT))
            ix = idx5[0:B * H, :].bitcast(U32)
            step(dve.max_index(ix, i5[0:B * H, 8:16], mT))
            dve.tensor_copy(i5[0:B * H, 0:8], ix).then_inc(s("idx5_ready"), 1)
            dve.wait_ge(s("masks_ready"), 1)
            step(dve.tensor_reduce(umask[:, 0:TOPU], umask3[:, :, :].rearrange("p h u -> p u h"), AX.X, ALU.max))
            dve.wait_ge(s("c5_mm"), 1)
            for b in range(B):
                for r in range(2):
                    step(dve.tensor_tensor(s5[0:HU, 0, 0:TOPU], ps[0:HU, 5, 16 * b + 8 * r:16 * b + 8 * r + TOPU],
                                           umask[:, 0:TOPU], ALU.mult))
                    step(dve.tensor_reduce(c5[0:HU, b, 1 - r:2 - r], s5[0:HU, 0, 0:TOPU], AX.X, ALU.add))
            dve.wait_ge(s("iota_ready"), 1)
            for b in range(B):
                ins = dve.tensor_scalar(oneT[0:HU, b, :], iota5[0:HU, :], c5[0:HU, b, 1:2], None, ALU.is_equal)
            ins.then_inc(s("oneT_ready"), 1)
            for b in range(B):
                dve.tensor_scalar(c5[0:HU, b, 0:1], c5[0:HU, b, 0:1], -SCALE, None, ALU.mult).then_inc(s("nm5_ready"), 1)
            dve.wait_ge(s("oneN_mm"), 1)
            dve.tensor_copy(oneN.rearrange("p b q h -> p (b q) h"),
                            ps[:, 4, :].rearrange("p (k h) -> p k h", h=P)[:, :, 0:HU]).then_inc(s("oneN_ready"), 1)
            dve.wait_ge(s("qsel_mm"), 1)
            for b in range(B):
                ins = dve.tensor_tensor(qsel[:, b, :, :], ps[:, 0, 2 * b * P:(2 * b + 2) * P].rearrange(
                    "p (c h) -> p c h", h=P)[:, :, 0:HU], bd5[:, :, :], ALU.mult)
            ins.then_inc(s("qsel_ready"), 1)
            for b in range(B):
                dve.wait_ge(s("pT5_mm"), b + 1)
                dve.tensor_copy(pT5[:, b, :, :], ps[:, 4 + b, 0:2 * P].rearrange(
                    "p (c h) -> p c h", h=P)[:, :, 0:HU]).then_inc(s("pT5_ready"), 1)
            step(dve.reciprocal(rs5[0:HU, :], sum5[0:HU, :]))
            for b in range(B):
                dve.wait_ge(s("o5_mm"), b + 1)
                dve.scalar_tensor_tensor(om5[0:HU, b, :], ps[0:HU, 6 + b, 0:D], rs5[0:HU, b:b + 1], bdT5[:, :],
                                         ALU.mult, ALU.mult).then_inc(s("om5_ready"), 1)
            dve.wait_ge(s("oT5_mm"), B)
            dve.tensor_copy(oT5.rearrange("p c t -> p (c t)"), ps[:, 0:2, :].rearrange("p a b -> p (a b)")
                            ).then_inc(s("oT5_ready"), 1)
            dve.wait_ge(s("y5_ready"), 1)
            step(dve.tensor_tensor(X[:, :, :], X[:, :, :], tiles(2), ALU.add))
            dve.sem_inc(s("a5_done"), 1)

            layernorm(6, X)
            xnT_1(6)
            dve.wait_ge(s("lnT_d"), TURNS[6])
            dve.wait_ge(s("lnT_a"), TURNS[6])
            dve.tensor_copy(xn_hi, xnT[:, :, :]).then_inc(s("xn_hi_ready"), 1)
            dve.wait_ge(s("xn_hi_ready"), 1)
            dve.tensor_tensor(xn_lo, xnT[:, :, :], f32(xn_hi), ALU.subtract).then_inc(s("xn_lo_ready"), 1)
            dve.wait_ge(s("r_mm"), 1)
            dve.tensor_copy(r6.rearrange("p a b -> p (a b)"), ps[:, 4, 0:NT * E]).then_inc(s("r_copied"), 1)
            dve.wait_ge(s("r_copied"), 1)
            step(dve.tensor_reduce(c6[:, :, 0:1], r6, AX.X, ALU.max))
            dve.tensor_tensor(r6, r6, c6[:, :, 0:1].to_broadcast([P, NT, E]), ALU.subtract).then_inc(s("r_ready"), 1)
            dve.wait_ge(s("r_exp"), 1)
            step(dve.tensor_reduce(c6[:, :, 1:2], p6, AX.X, ALU.add))
            step(dve.reciprocal(c6[:, :, 2:3], c6[:, :, 1:2]))
            step(dve.tensor_tensor(p6, p6, c6[:, :, 2:3].to_broadcast([P, NT, E]), ALU.mult))
            for j in range(NT):
                ins = dve.max(t6[:, j, :], p6[:, j, :])
            step(ins)
            for j in range(NT):
                ins = dve.max_index(i6[:, j, :].bitcast(U32), t6[:, j, :], p6[:, j, :])
            step(ins)
            step(dve.tensor_copy(f6, i6.bitcast(U32)))
            step(dve.tensor_tensor(c6[:, :, 3:4], t6[:, :, 0:1], t6[:, :, 1:2], ALU.add))
            step(dve.reciprocal(c6[:, :, 4:5], c6[:, :, 3:4]))
            step(dve.tensor_tensor(t6[:, :, 0:2], t6[:, :, 0:2], c6[:, :, 4:5].to_broadcast([P, NT, 2]), ALU.mult))
            for j in range(NT):
                for r, dst in ((0, gates), (1, g6)):
                    ins = dve.tensor_scalar(dst[:, j, :], iota6, f6[:, j, r:r + 1], t6[:, j, r:r + 1],
                                            ALU.is_equal, ALU.mult)
            step(ins)
            step(dve.tensor_tensor(gates, gates, g6, ALU.add))
            with dve.Fori(0, E // 2) as i:
                for par in range(2):
                    e = 2 * i + par
                    for ft in range(FT):
                        dve.wait_ge(s("hs_ready"), FT * e + ft + 1 + 4)
                        dve.tensor_copy(h_hi[ft], h_f[:, ft % 4, :]).then_inc(s("h_hi_ready"), 1)
                        dve.wait_ge(s("h_hi_ready"), FT * e + ft + 1)
                        dve.tensor_tensor(h_lo[ft], h_f[:, ft % 4, :], f32(h_hi[ft]), ALU.subtract
                                          ).then_inc(s("h_split"), 1)
                    dve.wait_ge(s("y_ready"), e + 1)
                    for j in range(NT):
                        dve.wait_ge(s("y_used"), NT * e + j + 1)
                        dve.scalar_tensor_tensor(X[:, j, :], ps[:, 4 + j, 0:D], gates[:, j, bass.ds(e, 1)], X[:, j, :],
                                                 ALU.mult, ALU.add).then_inc(s("y_used"), 1)
            dve.wait_ge(s("y_used"), NT * E + NT)
            dve.sem_inc(s("x_done"), 1)


_LAYOUT = {
    "x": ("x", lambda v: v.reshape(T, D)),
    "ctx": ("ctx_512", lambda v: v),
    "ctxT": ("ctx_512", lambda v: v.transpose(2, 0, 1).reshape(LAT, B * S)),
    "wqT": ("L0_xattn_Wq", lambda v: v.T),
    "wkvT": ("L0_xattn_Wkv", lambda v: v.T),
    "woT": ("L0_xattn_Wo", lambda v: v.T),
    "wv1": ("L1_xattn_Wv", lambda v: v),
    "w1T": ("L1_ffn_W1", lambda v: v.transpose(0, 2, 1)),
    "w2T": ("L1_ffn_W2", lambda v: v.transpose(0, 2, 1)),
}


def dft_tables():
    k = np.arange(D)
    w = 2 * np.pi * ((k[:, None] * k[None, :]) % D) / D
    c, sn = np.cos(w), np.sin(w)
    return np.stack([c, sn, -sn, c / D, sn / D]).astype(np.float32)


def kernel(**inputs):
    import concourse.bacc as _bacc
    from concourse.bass_utils import run_bass_kernel_spmd as _run

    nc = _bacc.Bacc("TRN2", target_bir_lowering=False, num_devices=1)
    arrays, a = {}, {}
    for name, (source, layout) in _LAYOUT.items():
        arrays[f"in_{name}"] = np.ascontiguousarray(layout(np.asarray(inputs[source])))
    arrays["in_vecs"] = np.ascontiguousarray(
        np.stack([np.asarray(inputs[n]).reshape(KF, P).T for n in VECS], axis=1))
    arrays["in_rows"] = np.stack([np.asarray(inputs[n]) for n in ROWS])
    arrays["in_packed"] = np.concatenate(
        [v.reshape(D, n) if name in AS_IS else v.T for name, n, v in
         ((name, n, np.asarray(inputs[name])) for name, n in PACK)], axis=1)
    arrays["in_bc_b"] = np.concatenate([np.asarray(inputs["L0_attn_Bp_b"]), np.asarray(inputs["L0_attn_Cp_b"])] * 2
                                       ).reshape(4 * NST, 1)
    arrays["in_freqT"] = np.stack([np.asarray(inputs["L0_ffn_w_freq_real"]).T, np.asarray(inputs["L0_ffn_w_freq_imag"]).T])
    arrays["in_dft"] = dft_tables()
    for name, v in arrays.items():
        a[name[3:]] = nc.dram_tensor(name, v.shape, mybir.dt.from_np(v.dtype), kind="ExternalInput").ap()
    a["out"] = nc.dram_tensor("out", (T, D), F32, kind="ExternalOutput").ap()
    perceiver(nc, a)
    r = _run(nc, [arrays], core_ids=[0])
    return r.results[0]["out"].reshape(B, L, D)
```

```python
from contextlib import ExitStack

import numpy as np

import concourse.bass as bass
from concourse import mybir

F32 = mybir.dt.float32
F32R = mybir.dt.float32r
U32 = mybir.dt.uint32
ALU = mybir.AluOpType
ACT = mybir.ActivationFunctionType
AX = mybir.AxisListType

P = 128
B, L, D = 2, 256, 256
T = B * L
NT = T // P
QT = L // P
KF = D // P
S, LAT = 4096, 128
H, DH = 16, 16
SCALE = DH ** -0.5
EPS = 1e-5
NST, TAPS = 16, 4
E, F = 8, 1024
FT = F // P
TOPU = 5
HU = H * TOPU

GH = 4
NG = B * H // GH
KT = S // P
CK = 1024
NC = S // CK
PK = 512
NPC = B * S // PK
RB = 3 * DH
RS = 2 * RB
VW = GH * (DH + 1)
UNITS = 32
MAX_SLOTS = 84
TURN_SLOT = 29, 1
SUM_SLOT = 30, 0
UN4 = KT // 2
PRING = 4
ARENA = 11936
HALF = (slice(0, NT // 2), slice(NT // 2, NT))
TURNS = {0: 1, 1: 2, 3: 3, 4: 4, 5: 5, 6: 6}
KST, VST = 16 * 2, 16
LOADQ, LOADK = 16 * 6, 16 * 3


VECS = ("L0_attn_conv_b", "L0_attn_D", "L0_attn_gate_b", "L1_xattn_bq", "L1_xattn_bk", "L1_attn_bq", "L1_attn_bk")
PACK = (("L0_attn_gate_w", D), ("L0_attn_out_w", D), ("L0_attn_Bp_w", NST), ("L0_attn_Cp_w", NST), ("L0_attn_Bp_w", NST),
        ("L0_attn_Cp_w", NST), ("L1_xattn_Wq", D), ("L1_xattn_Wk", LAT), ("L1_attn_wq", D), ("L1_attn_wk", D),
        ("L1_attn_wv", D), ("L1_attn_wo", D), ("L1_ffn_Wr", E), ("L0_attn_conv_w", TAPS), ("L0_attn_A", NST))
AS_IS = ("L1_xattn_Wq", "L0_attn_conv_w", "L0_attn_A")
ROWS = ("L0_attn_out_b", "L0_attn_ln_g", "L0_attn_ln_b", "L0_ffn_bias", "L1_xattn_bv", "L1_attn_bv", "L1_attn_bo",
        "L1_attn_bq")


def perceiver(nc, a):
    ctx = ExitStack()
    with ctx:
        def sb(name, shape, dt=F32):
            return ctx.enter_context(nc.sbuf_tensor(name, shape, dt))

        def sem(name):
            return ctx.enter_context(nc.semaphore(name))

        ps = ctx.enter_context(nc.psum_tensor("ps", [P, 8, 512], F32))

        def f32(v):
            return v.bitcast(F32)

        k_stack = sb("k_stack", [P, 2, 2, S], F32R)
        qm_stack = sb("qm_stack", [P, 2, 2, 2 * L], F32R)
        qe_stack = sb("qe_stack", [P, 2, 2, 2 * L], F32R)
        k_hi = sb("k_hi", [P, 2, 2, PK], F32R)
        k_lo = sb("k_lo", [P, 2, 2, PK], F32R)
        xn_hi = sb("xn_hi", [P, KF, T], F32R)[:, :, :]
        xn_lo = sb("xn_lo", [P, KF, T], F32R)[:, :, :]
        nm_t = sb("nm", [P, 8], F32R)
        ident_r = sb("ident_r", [P, P], F32R)
        bc_hl = sb("bc_hl", [64, T], F32R)
        sel_n = sb("sel_n", [64, 2 * NST], F32R)
        nm4 = sb("nm4", [1, L], F32R)
        ones_r = sb("ones_r", [1, P], F32R)
        q_hi = k_stack[:, 1, 0, 0:2 * T].rearrange("p (c t) -> p c t", c=2)
        q_lo = k_stack[:, 1, 0, 2 * T:4 * T].rearrange("p (c t) -> p c t", c=2)

        ident = sb("ident", [P, P])
        X = sb("X", [P, NT, D])
        xn = sb("xn", [P, NT, D])
        xnT = sb("xnT", [P, KF, T])
        stats = sb("stats", [P, NT, 6])
        mv = sb("mv", [P, NT, 2])
        minus_half = sb("minus_half", [P, NT])
        one_col = sb("one_col", [P, 1])
        rstd = sb("rstd", [P, NT])
        w_a = sb("w_a", [P, KF, D])
        w_kv = sb("w_kv", [P, 2 * D])
        w_o = sb("w_o", [P, NG // B, D])
        w_all = sb("w_all", [P, KF, sum(n for _, n in PACK)])
        col = [0]

        def packed(*names):
            n = sum(w for _, w in names)
            v = w_all[:, :, col[0]:col[0] + n]
            col[0] += n
            return v

        w_gate, w_out, bc_w, w_q1, w_k1 = (packed(*PACK[i:j]) for i, j in ((0, 1), (1, 2), (2, 6), (6, 7), (7, 8)))
        w5 = [packed(PACK[i]) for i in range(8, 12)]
        w_r, conv_w, a_log = (packed(PACK[i]) for i in range(12, 15))
        bc_b = sb("bc_b", [64, 1])
        vecs = sb("vecs", [P, len(VECS), KF])
        a_dec = sb("a_dec", [P, KF, NST])
        rows = sb("rows", [P, len(ROWS), D])
        m_dft = w_a
        w_v1 = sb("w_v1", [P, D])
        head_mask = sb("head_mask", [P, 8])
        arena = sb("arena", [P, ARENA])

        CB, DD, GB, BQ1, BK1, BQ5, BK5 = range(len(VECS))
        OB, LG, LB, FB, BV1, BV5, BO5, BQ5R = range(len(ROWS))

        off = [0]

        def carve(*shape):
            n = int(np.prod(shape))
            v = arena[:, off[0]:off[0] + n]
            off[0] += n
            assert off[0] <= ARENA, off[0]
            names = "abcd"[:len(shape)]
            if len(shape) == 1:
                return v
            return v.rearrange("p (%s) -> p %s" % (" ".join(names), " ".join(names)),
                               **{c: s for c, s in zip(names[1:], shape[1:])})

        v_grp = carve(2, KT, VW)
        probs = carve(PRING, 512)
        o_raw = carve(NG + 1, L)
        cx = carve(2, PK)
        v_stage = carve(2, NG // B, PK // P, VW)
        mxp = carve(8, NC)
        o_rec = xn[:, 0, :]
        c_raw = v_stage.rearrange("p r g k v -> p (r g k v)")[:, 0:2 * CK].rearrange("p (r k) -> p r k", r=2)
        k_full = o_raw[:, 0:NG, :].rearrange("p g l -> p (g l)").rearrange("p (r k f) -> p r k f", r=2, k=2)
        off[0] = 0
        dft = carve(5, KF, D)
        wf = carve(2, KF, D)
        uf = carve(2, KF, D)
        assert off[0] <= 2 * KT * VW + PRING * 512 + (NG + 1) * L
        head_ones_t = sb("head_ones", [P, P])
        head_ones = head_ones_t[:, :]
        off[0] = 0
        xpad_all = carve(KF * B * (L + TAPS - 1))
        xpad = xpad_all.rearrange("p (c b l) -> p c b l", c=KF, b=B)
        conv = carve(KF, T)
        u = carve(KF, T)
        gate = carve(KF, T)
        b_in = carve(4, T)
        h_st = carve(4, T)
        c_bc = carve(2, T)
        hc = carve(4, T)
        yT = xpad_all[:, 0:KF * T].rearrange("p (c t) -> p c t", c=KF)
        xn_T2 = xn[:, :, :].rearrange("p j f -> p (j f)").rearrange("p (c t) -> p c t", c=KF)
        off[0] = 0
        ctxN = carve(B, KT, LAT)
        ct_hi, ct_lo = ([k_stack[:, hl, b, :] for b in range(B)] for hl in range(2))
        qp_hi, qp_lo = (qm_stack[:, 0, hl, :] for hl in range(2))
        q1T = xn_T2
        qbk = carve(8)
        p4 = carve(4, 2 * L)
        psumP = xnT[:, 0, :]
        mx4 = carve(QT, 16)
        ones = carve(P)
        ocT = carve(L)
        rs4 = carve(L)
        nm4f = carve(QT)
        off[0] = 0
        qT5 = xn_T2
        kT5 = carve(KF, T)
        qn5 = carve(NT, D)
        vn5 = carve(NT, D)
        mx5 = carve(QT, B * H)
        mT5 = carve(L)
        i5 = carve(16)
        idx5 = carve(8)
        c5 = carve(2, 16)
        s5 = carve(2, 16)
        oneT = carve(B, L)
        oneN = carve(B, QT, HU)
        qsel = carve(B, KF, HU)
        p5 = carve(B, L)
        pT5 = carve(B, QT, HU)
        sum5 = carve(B)
        rs5 = carve(B)
        om5 = carve(B, D)
        oT5 = carve(KF, T)
        qm5 = carve(4, 4, P)
        assert off[0] <= ARENA - KF * F
        off[0] = 0
        w1_1, w2_0, w2_1 = carve(KF, F), carve(FT, D), carve(FT, D)
        h_f = carve(4, T)
        off[0] = ARENA - KF * F
        w1, w2 = (carve(KF, F), w1_1), (w2_0, w2_1)
        parts6 = k_stack[:, :, :, :].rearrange("p a b k -> p (a b k)")

        def part6(i, par, n):
            lo = (4 * par + i) * KF * F
            return parts6[:, lo:lo + KF * F].rearrange("p (a b) -> p a b", a=n)

        w1_hi, w1_lo = ([part6(i, par, KF) for par in range(2)] for i in (0, 1))
        w2_hi, w2_lo = ([part6(i, par, FT) for par in range(2)] for i in (2, 3))
        stage1 = [v[:, :, :, :].rearrange("p a b k -> p (a b) k") for v in (qm_stack, qe_stack, k_hi, k_lo)]
        h_hi = [stage1[ft // 4][:, ft % 4, :] for ft in range(FT)]
        h_lo = [stage1[2 + ft // 4][:, ft % 4, :] for ft in range(FT)]
        gates_t = sb("gates", [P, NT, E])
        gates = gates_t[:, :, :]
        r6_t = sb("r6", [P, NT, 8])
        r6 = r6_t[:, :, :]
        p6_t = sb("p6", [P, NT, 8])
        p6 = p6_t[:, :, :]
        t6_t = sb("t6", [P, NT, 8])
        t6 = t6_t[:, :, :]
        i6_t = sb("i6", [P, NT, 8])
        i6 = i6_t[:, :, :]
        f6_t = sb("f6", [P, NT, 8])
        f6 = f6_t[:, :, :]
        g6_t = sb("g6", [P, NT, 8])
        g6 = g6_t[:, :, :]
        c6_t = sb("c6", [P, NT, 8])
        c6 = c6_t[:, :, :]
        iota_t = sb("iota", [P, L])
        iota5, iota6 = iota_t[:, :], iota_t[:, 0:E]

        def flat6(v):
            return v.rearrange("p a b -> p (a b)")

        umask3 = sb("umask3", [HU, H, TOPU])
        umask = sb("umask", [HU, 8])
        sel_e = sb("sel_e", [2 * H, B, HU])
        bd5 = sb("bd5", [P, KF, HU])
        bdT5 = sb("bdT5", [HU, D])

        qd = nc.dram_tensor("q_parts", [2, NG, GH * DH, L], F32, kind="Internal").ap()
        kd = nc.dram_tensor("k_parts", [2, NG, GH * DH, S], F32, kind="Internal").ap()
        cd = nc.dram_tensor("c_parts", [2, P, B * S], F32, kind="Internal").ap()
        vd = nc.dram_tensor("v_parts", [NG, P, KT, VW], F32, kind="Internal").ap()

        sems = {}

        def s(name):
            if name not in sems:
                sems[name] = ctx.enter_context(nc.semaphore(name))
            return sems[name]

        block = ctx.enter_context(nc.Block())

        def scaled_rows(v, n):
            return v.unsqueeze(1).to_broadcast([P, n, D])

        @block.sync
        def _(sp):
            for par in range(2):
                sp.sem_inc(s(f"k_out{par}"), KST)
                sp.sem_inc(s(f"v_out{par}"), VST)
            sp.dma_start(cx[:, 0, :], a["ctxT"][:, 0:PK]).then_inc(s("cx_in0"), 16)
            sp.dma_start(w_kv[:, :], a["wkvT"]).then_inc(s("wkv_in"), 16)
            sp.dma_start(X[:, :, :], a["x"].rearrange("(j p) f -> p j f", p=P)).then_inc(s("x_in"), 16)
            sp.dma_start(cx[:, 1, :], a["ctxT"][:, PK:2 * PK]).then_inc(s("cx_in1"), 16)
            sp.dma_start(w_a[:, :, :], a["wqT"].rearrange("(c p) n -> p c n", p=P)).then_inc(s("w0_in"), 16)

            def store_parts(b, nb, n, par):
                sp.wait_ge(s("kl_done"), 2 * n + 2)
                for i, part in enumerate((k_hi, k_lo)):
                    sp.dma_start(kd[i, 4 * b:4 * b + 4, :, bass.ds(nb * PK, PK)].rearrange(
                        "(c g) r k -> (g r) c k", g=2), f32(part[:, par, :, :])).then_inc(s(f"k_out{par}"), 16)
                sp.wait_ge(s("v_done"), 2 * n + 2 + 2)
                sp.dma_start(vd[4 * b:4 * b + 4, :, bass.ds(nb * 4, 4), :].rearrange("g p k v -> p g k v"),
                             v_stage[:, par, :, :, :]).then_inc(s(f"v_out{par}"), 16)

            def load_q(buf, name, g, par):
                for ab in range(2):
                    for blk, hl in enumerate((0, 0, 1)):
                        r = blk * 2 * DH + ab * DH
                        src = qd[hl, bass.ds(g, 1)].rearrange("g (r a d) q -> d (g r) a q", a=2, d=DH)[:, :, ab, :]
                        sp.dma_start(f32(buf[r:r + DH, par, :, ab * L:(ab + 1) * L]), src).then_inc(s(f"{name}{par}"), 16)

            def load_k(g, par, c):
                for blk, hl in enumerate((0, 1, 0)):
                    src = kd[hl, bass.ds(g, 1), :, c * CK:(c + 1) * CK].rearrange("g (r d) k -> d (g r) k", d=2 * DH)
                    sp.dma_start(f32(k_stack[blk * 2 * DH:(blk + 1) * 2 * DH, par, :, c * CK:(c + 1) * CK]), src
                                 ).then_inc(s(f"ks_in{par}{c}"), 16)

            def load_v(g, par):
                sp.dma_start(v_grp[:, par, :, :], vd[bass.ds(g, 1)].rearrange("g p k v -> p (g k) v")
                             ).then_inc(s(f"vs_in{par}"), 16)

            for n in range(NPC):
                b, nb, par = n // (NPC // B), n % (NPC // B), n % 2
                store_parts(b, nb, n, par)
                if n == 2:
                    sp.wait_ge(s("q_hi_ready"), KF)
                    sp.wait_ge(s("q_lo_ready"), KF)
                    for i, part in enumerate((q_hi, q_lo)):
                        for bb in range(B):
                            sp.dma_start(qd[i, 4 * bb:4 * bb + 4].rearrange("(c g) r q -> (g r) c q", g=2),
                                         f32(part[:, :, bb * L:(bb + 1) * L])).then_inc(s("q_out"), 16)
                elif n == 3:
                    sp.wait_ge(s("q_out"), 16 * 2 * B)
                    sp.wait_ge(s("q_zero"), 1)
                    load_q(qm_stack, "qm_in", 0, 0)
                if n in (3, 5, 7, 9):
                    c = (n - 3) // 2
                    for p2 in range(2):
                        sp.wait_ge(s(f"k_out{p2}"), KST * (c + 2))
                    load_k(0, 0, c)
                elif n == 11:
                    for p2 in range(2):
                        sp.wait_ge(s(f"v_out{p2}"), VST * (NC + 1))
                    sp.wait_ge(s("dft_done"), 1)
                    sp.wait_ge(s("q_zero"), 2)
                    load_q(qe_stack, "qe_in", 0, 0)
                    load_v(0, 0)
                elif n == 12:
                    load_q(qm_stack, "qm_in", 1, 1)
                elif n in (13, 14):
                    load_k(1, 1, n - 13)
            for c in range(2, NC):
                load_k(1, 1, c)
            load_q(qe_stack, "qe_in", 1, 1)
            load_v(1, 1)
            for par in range(2):
                sp.wait_ge(s(f"k_out{par}"), KST * (NPC // 2 + 1))
                sp.wait_ge(s(f"v_out{par}"), VST * (NPC // 2 + 1))

            with sp.Fori(0, NG // 2 - 1) as i:
                for par in range(2):
                    g = i * 2 + par
                    sp.wait_ge(s("mx_ready"), (g + 1) * UNITS)
                    load_q(qm_stack, "qm_in", g + 2, par)
                    for c in range(NC):
                        sp.wait_ge(s("s_ready"), 2 * KT * g + 2 * (KT // NC) * (c + 1))
                        load_k(g + 2, par, c)
                    load_q(qe_stack, "qe_in", g + 2, par)
                    sp.wait_ge(s("pv_done"), KT * (g + 1) + 2)
                    load_v(g + 2, par)

            for par in range(2):
                sp.wait_ge(s(f"c_out{par}"), 32 * B * NC // 2)
            sp.wait_ge(s("mx_ready"), NG * UNITS)
            sp.wait_ge(s("s_ready"), 2 * KT * NG)
            for b in range(B):
                for hl, part in enumerate((ct_hi, ct_lo)):
                    sp.dma_start(f32(part[b]), cd[hl, :, b * S:(b + 1) * S]).then_inc(s(f"c4_in{b}"), 16)
            sp.wait_ge(s("y2_ready"), 2)
            sp.dma_start(ctxN, a["ctx"].rearrange("b (k p) l -> p b k l", p=P)).then_inc(s("c4n_in"), 16)

            def load_w1(e, par):
                sp.dma_start(w1[par].unsqueeze(1), a["w1T"][bass.ds(e, 1)].rearrange("e (c p) f -> p e c f", p=P)
                             ).then_inc(s(f"w1_in{par}"), 16)

            def load_w2(e, par):
                sp.dma_start(w2[par].unsqueeze(1), a["w2T"][bass.ds(e, 1)].rearrange("e (c p) d -> p e c d", p=P)
                             ).then_inc(s(f"w2_in{par}"), 16)

            sp.wait_ge(s("y4_ready"), B)
            load_w1(0, 0)
            sp.wait_ge(s("a5_done"), 1)
            load_w2(0, 0)
            load_w1(1, 1)
            load_w2(1, 1)
            with sp.Fori(1, E // 2) as i:
                for par in range(2):
                    e = 2 * i + par
                    sp.wait_ge(s("w1_split"), e - 1)
                    load_w1(e, par)
                    sp.wait_ge(s("w2_split"), e - 1)
                    load_w2(e, par)
            sp.wait_ge(s("x_done"), 1)
            sp.dma_start(a["out"].rearrange("(j p) f -> p j f", p=P), X[:, :, :]).then_inc(s("out_done"), 16)
            sp.wait_ge(s("out_done"), 16)

        @block.gpsimd
        def _(pool):
            steps = [0]

            def step(ins):
                steps[0] += 1
                ins.then_inc(s("pool_step"), 1)
                pool.wait_ge(s("pool_step"), steps[0])

            def rstd_of(k):
                for h in range(2):
                    pool.wait_ge(s("ln_var"), 2 * k + h + 1)
                    pool.tensor_tensor(rstd[:, HALF[h]], mv[:, HALF[h], 1], minus_half[:, HALF[h]], ALU.pow
                                       ).then_inc(s("ln_rstd"), 1)

            def onezero(view, conds, fill=0.0):
                step(pool.memset(view, 1.0))
                for op, base, pat, mul in conds:
                    step(pool.affine_select(out=view, in_=view, compare_op=op, fill=fill, base=base,
                                            pattern=pat, channel_multiplier=mul))

            step(pool.memset(minus_half[:, :], -0.5))
            onezero(ident[:, :], [(ALU.is_equal, 0, [[-1, P]], 1)])
            step(pool.memset(f32(ident_r[:, :]), 1.0))
            step(pool.affine_select(out=ident_r[:, :], in_=f32(ident_r[:, :]), compare_op=ALU.is_equal, fill=0.0,
                                    base=0, pattern=[[-1, P]], channel_multiplier=1))
            rstd_of(0)

            with pool.Fori(0, NPC // 2) as i:
                for par in range(2):
                    n = 2 * i + par
                    for k in range(2):
                        pool.wait_ge(s("k_copied"), 2 * n + k + 3)
                        pool.wait_ge(s(f"k_out{par}"), KST * (i + 1))
                        pool.tensor_tensor(k_lo[:, par, k, :], k_full[:, par, k, :], f32(k_hi[:, par, k, :]),
                                           ALU.subtract).then_inc(s("kl_done"), 1)

            pool.wait_ge(s("wo_zero"), 1)
            for j in range(GH):
                pool.dma_start(w_o[32 * j:32 * j + DH, :, :],
                               a["woT"].rearrange("(g j d) o -> j d g o", j=GH, d=DH)[j]).then_inc(s("wo_in"), 16)
            step(pool.memset(head_ones, 1.0))
            hv = head_ones.rearrange("p (g c) -> p g c", g=4)
            step(pool.affine_select(out=hv, in_=hv, compare_op=ALU.is_equal, fill=0.0, base=-DH,
                                    pattern=[[-32, 4], [0, 32]], channel_multiplier=1))
            onezero(head_mask[:, :], [(ALU.is_ge, 0, [[-DH, 8]], 1), (ALU.is_ge, DH - 1, [[DH, 8]], -1)])
            sn = f32(sel_n[:, :])
            step(pool.memset(sn[0:32, :], 1.0))
            step(pool.memset(sn[32:64, :], 1.0))
            for r in (0, 32):
                step(pool.affine_select(out=sel_n[r:r + 32, :], in_=sn[r:r + 32, :], compare_op=ALU.is_equal,
                                        fill=0.0, base=0, pattern=[[-1, 32]], channel_multiplier=1))
            step(pool.memset(f32(ones_r[:, :]), 1.0))
            onezero(umask3[:, :, :], [(ALU.is_equal, 0, [[-TOPU, H], [-1, TOPU]], 1)])
            onezero(sel_e[:, :, :].rearrange("p b (h u) -> p b h u", u=TOPU),
                    [(ALU.is_equal, 0, [[-H, B], [-1, H], [0, TOPU]], 1)])
            onezero(bd5[:, :, :].rearrange("p c (h u) -> p c h u", u=TOPU),
                    [(ALU.is_ge, 0, [[P, KF], [-DH, H], [0, TOPU]], 1),
                     (ALU.is_ge, DH - 1, [[-P, KF], [DH, H], [0, TOPU]], -1)])
            onezero(bdT5[:, :].rearrange("p (h d) -> p h d", d=DH),
                    [(ALU.is_ge, 0, [[-TOPU, H], [0, DH]], 1), (ALU.is_ge, TOPU - 1, [[TOPU, H], [0, DH]], -1)])
            pool.sem_inc(s("masks_ready"), 1)

            step(pool.memset(one_col[:, :], 1.0))
            for par in range(2):
                pool.wait_ge(s(f"k_out{par}"), KST * (NPC // 2 + 1))
                pool.wait_ge(s(f"v_out{par}"), VST * (NPC // 2 + 1))
            for par in range(2):
                pool.dma_start(c_raw[:, par, :], a["ctxT"][:, par * CK:(par + 1) * CK]).then_inc(s(f"c_in{par}"), 16)

            def context_parts(n, par, i, more):
                hi, lo = (v[:, par, :, :].rearrange("p a k -> p (a k)") for v in (k_hi, k_lo))
                pool.wait_ge(s(f"c_in{par}"), 16 * (i + 1))
                if more != "first":
                    pool.wait_ge(s(f"c_out{par}"), 32 * i)
                pool.tensor_tensor(hi, c_raw[:, par, :], one_col[:, :].to_broadcast([P, CK]), ALU.mult
                                   ).then_inc(s("c_split"), 1)
                pool.wait_ge(s("c_split"), 2 * n + 1)
                pool.tensor_tensor(lo, c_raw[:, par, :], f32(hi), ALU.subtract).then_inc(s("c_split"), 1)
                pool.wait_ge(s("c_split"), 2 * n + 2)
                for hl, part in enumerate((hi, lo)):
                    pool.dma_start(cd[hl, :, bass.ds(n * CK, CK)], f32(part)).then_inc(s(f"c_out{par}"), 16)
                if more != "last":
                    pool.dma_start(c_raw[:, par, :], a["ctxT"][:, bass.ds((n + 2) * CK, CK)]
                                   ).then_inc(s(f"c_in{par}"), 16)

            for par in range(2):
                context_parts(par, par, 0, "first")
            with pool.Fori(1, B * NC // 2 - 1) as i:
                for par in range(2):
                    context_parts(2 * i + par, par, i, "")
            for par in range(2):
                context_parts(B * NC - 2 + par, par, B * NC // 2 - 1, "last")

            rstd_of(1)
            k = 0
            for n in range(NST):
                for c in range(KF):
                    pool.wait_ge(s("c_bc_ready"), n + 1)
                    pool.wait_ge(s("h_ready"), k + 1)
                    if k >= 4:
                        pool.wait_ge(s("hc_used"), k - 3)
                    pool.tensor_tensor(hc[:, k % 4, :], h_st[:, k % 4, :], c_bc[:, n % 2, :], ALU.mult
                                       ).then_inc(s("hc_ready"), 1)
                    k += 1

            def w1_low(e, par):
                pool.wait_ge(s("w1_hi_ready"), e + 1)
                pool.tensor_tensor(flat6(w1_lo[par]), flat6(w1[par]), f32(flat6(w1_hi[par])), ALU.subtract
                                   ).then_inc(s("w1_split"), 1)

            def w2_low(e, par):
                pool.wait_ge(s("w2_hi_ready"), e + 1)
                pool.tensor_tensor(flat6(w2_lo[par]), flat6(w2[par]), f32(flat6(w2_hi[par])), ALU.subtract
                                   ).then_inc(s("w2_split"), 1)

            for k in range(2, 6):
                rstd_of(k)

            pool.wait_ge(s("q5_ready"), 1)
            step(pool.iota(iota5.bitcast(mybir.dt.int32), pattern=[[1, L]], base=0, channel_multiplier=0))
            pool.tensor_copy(iota5, iota5.bitcast(mybir.dt.int32)).then_inc(s("iota_ready"), 1)
            for k in range(16):
                b, qt, hq = k // 8, (k // 4) % 2, k % 4
                if k >= 4:
                    pool.wait_ge(s("mx5_ready"), k - 3)
                c = hq // 2
                q = qT5[:, c, b * L + qt * P:b * L + (qt + 1) * P]
                pool.tensor_tensor(qm5[:, k % 4, :, :], q.unsqueeze(1).to_broadcast([P, 4, P]),
                                   head_mask[:, 4 * (hq % 2):4 * (hq % 2) + 4].unsqueeze(2).to_broadcast([P, 4, P]),
                                   ALU.mult).then_inc(s("qm5_ready"), 1)
            w1_low(0, 0)
            rstd_of(6)

            w2_low(0, 0)
            w1_low(1, 1)
            w2_low(1, 1)
            with pool.Fori(1, E // 2) as i:
                for par in range(2):
                    w1_low(2 * i + par, par)
                    w2_low(2 * i + par, par)

        @block.scalar
        def _(act):
            act.sem_inc(s("v_done"), 2)
            act.sem_inc(s("k_copied"), 2)
            act.sem_inc(s("p_ready"), 2)
            act.sem_inc(s("o_evac"), 1)
            act.sem_inc(s("hs_ready"), 4)

            act.wait_ge(s("x_in"), 16)
            act.dma_start(wf[:, :, :, :], a["freqT"].rearrange("m (c p) n -> p m c n", p=P)).then_inc(s("dft_in"), 16)
            act.dma_start(dft[:, :, :, :], a["dft"].rearrange("m (c p) n -> p m c n", p=P)).then_inc(s("dft_in"), 16)
            def xnT_copy(k, bank=6):
                for h in range(2):
                    act.wait_ge(s("ln_tr"), 2 * TURNS[k] - 1 + h)
                    act.activation(xnT[:, :, h * L:(h + 1) * L], ps[:, bank + h, :].rearrange("p (c t) -> p c t", c=KF),
                                   ACT.Copy).then_inc(s("xnT_ready"), 1)

            def project_out(n, par, turn, more=True):
                act.wait_ge(s(f"k_out{par}"), KST * (turn + 1))
                for k in range(2):
                    act.wait_ge(s("kv_ready"), 4 * n + k + 1)
                    act.activation(k_hi[:, par, k, :], ps[:, 4 + k, :], ACT.Copy)
                    act.activation(k_full[:, par, k, :], ps[:, 4 + k, :], ACT.Copy).then_inc(s("k_copied"), 1)
                act.wait_ge(s(f"v_out{par}"), VST * (turn + 1))
                for k in range(2):
                    act.wait_ge(s("kv_ready"), 4 * n + k + 3)
                    for kk in range(2):
                        dst = v_stage[:, par, :, 2 * k + kk, :].rearrange("p g (j v) -> p g j v", v=DH + 1)
                        src = ps[:, 6 + k, kk * D:(kk + 1) * D].rearrange("p (g j v) -> p g j v", g=4, j=GH)
                        ins = act.activation(dst[:, :, :, 0:DH], src, ACT.Copy)
                    ins.then_inc(s("v_done"), 1)
                    if k == 1 and more:
                        act.dma_start(cx[:, par, :], a["ctxT"][:, bass.ds((n + 2) * PK, PK)]
                                      ).then_inc(s(f"cx_in{par}"), 16)

            act.wait_ge(s("v_ones"), 1)
            for n in range(2):
                project_out(n, n, 0)
            xnT_copy(0, 2)
            for c in range(KF):
                act.wait_ge(s("q_ready"), c + 1)
                act.activation(q_hi[:, c, :], ps[:, c, :], ACT.Copy).then_inc(s("q_hi_ready"), 1)
            project_out(2, 0, 1)
            act.wait_ge(s("uf_ready"), 1)
            act.activation(uf[:, :, :, :].rearrange("p a b c -> p (a b c)"),
                           ps[:, 0:2, :].rearrange("p a b -> p (a b)"), ACT.Copy).then_inc(s("uf_done"), 1)
            project_out(3, 1, 1)
            with act.Fori(1, NPC // 4 - 1) as i:
                for u4 in range(4):
                    project_out(4 * i + u4, u4 % 2, 2 * i + u4 // 2)
            for n in range(NPC - 4, NPC):
                project_out(n, n % 2, n // 2, more=n + 2 < NPC)
            act.dma_start(w_all[:, :, :], a["packed"].rearrange("(c p) n -> p c n", p=P)).then_inc(s("w_in"), 16)
            act.dma_start(w_v1[:, :], a["wv1"]).then_inc(s("w_in"), 16)
            act.dma_start(bc_b[:, :], a["bc_b"]).then_inc(s("w_in"), 16)
            act.dma_start(vecs[:, :, :], a["vecs"]).then_inc(s("w_in"), 16)
            act.dma_start(rows[:, :, :], a["rows"].unsqueeze(0).to_broadcast([P, len(ROWS), D])
                          ).then_inc(s("w_in"), 16)

            def exp_pass(g, par):
                for st in range(KT):
                    for bk in range(2):
                        act.wait_ge(s("s_ready"), 2 * KT * g + 2 * st + bk + 1)
                        act.wait_ge(s("pv_done"), KT * g + st + 1)
                        act.activation(probs[:, (2 * st + bk) % PRING, :], ps[:, 4 + bk, :], ACT.Exp,
                                       scale=SCALE).then_inc(s("p_ready"), 1)
                    if st == 2:
                        act.wait_ge(s("pv_done"), KT * g + 2)
                        act.activation(o_raw[:, bass.ds(g, 1), :], ps[:, 7 - par, 0:L].unsqueeze(1),
                                       ACT.Copy).then_inc(s("o_evac"), 1)

            act.wait_ge(s("kl_done"), 2 * NPC)
            act.wait_ge(s("pv_zero"), 1)
            with act.Fori(0, NG // 2 - 1) as i:
                for par in range(2):
                    exp_pass(2 * i + par, par)
            for par in range(2):
                exp_pass(NG - 2 + par, par)
            act.wait_ge(s("pv_done"), KT * NG + 2)
            act.activation(o_raw[:, NG, :], ps[:, 7, 0:L], ACT.Copy).then_inc(s("o_evac"), 1)

            act.wait_ge(s("w_in"), 16 * 5)
            act.activation(a_dec[:, :, :], a_log[:, :, :], ACT.Exp).then_inc(s("act_step"), 1)
            act.wait_ge(s("act_step"), 1)
            act.activation(a_dec[:, :, :], a_dec[:, :, :], ACT.Exp, scale=-1.0).then_inc(s("a_dec_ready"), 1)
            xnT_copy(1)
            for c in range(KF):
                act.wait_ge(s("conv_ready"), c + 1)
                act.activation(u[:, c, :], conv[:, c, :], ACT.Silu).then_inc(s("u_ready"), 1)
            for c in range(KF):
                act.wait_ge(s("gate_mm"), c + 1)
                act.activation(gate[:, c, :], ps[:, c, :], ACT.Silu, bias=vecs[:, GB, c:c + 1]
                               ).then_inc(s("gate_ready"), 1)
            act.wait_ge(s("bc_mm"), 1)
            act.activation(bc_hl[:, :], ps[0:64, 2, :], ACT.Identity, bias=bc_b[:, 0:1]).then_inc(s("bc_hi_ready"), 1)
            for n in range(NST):
                act.wait_ge(s("c_ready"), n + 1)
                if n >= 2:
                    act.wait_ge(s("hc_ready"), 2 * (n - 1))
                act.activation(c_bc[:, n % 2, :], ps[:, 2 + n % 2, :], ACT.Copy).then_inc(s("c_bc_ready"), 1)

            xnT_copy(3)

            def w1_high(e, par, i):
                act.wait_ge(s(f"w1_in{par}"), 16 * (i + 1))
                act.activation(flat6(w1_hi[par]), flat6(w1[par]), ACT.Copy).then_inc(s("w1_hi_ready"), 1)

            def w2_high(e, par, i):
                act.wait_ge(s(f"w2_in{par}"), 16 * (i + 1))
                act.activation(flat6(w2_hi[par]), flat6(w2[par]), ACT.Copy).then_inc(s("w2_hi_ready"), 1)

            xnT_copy(4)
            for c in range(KF):
                act.wait_ge(s("q1_mm"), c + 1)
                act.activation(q1T[:, c, :], ps[:, c, :], ACT.Identity, bias=vecs[:, BQ1, c:c + 1]
                               ).then_inc(s("q1_ready"), 1)
            for k in range(B * UN4):
                act.wait_ge(s("s4_ready"), k + 1)
                if k >= 4:
                    act.wait_ge(s("av4_done"), k - 3)
                    act.wait_ge(s("p4_summed"), k - 3)
                act.activation(p4[:, k % 4, :], ps[:, 4 + k % 2, :], ACT.Exp).then_inc(s("p4_ready"), 1)

            xnT_copy(5)
            for c in range(KF):
                act.wait_ge(s("qk5_mm"), c + 1)
                ins = act.activation(qT5[:, c, :], ps[:, c, :], ACT.Identity, bias=vecs[:, BQ5, c:c + 1])
            ins.then_inc(s("q5_ready"), 1)
            for c in range(KF):
                act.wait_ge(s("qk5_mm"), c + 3)
                ins = act.activation(kT5[:, c, :], ps[:, 2 + c, :], ACT.Identity, bias=vecs[:, BK5, c:c + 1])
            ins.then_inc(s("k5_ready"), 1)
            w1_high(0, 0, 0)
            for b in range(B):
                act.wait_ge(s("ss5_ready"), b + 1)
                act.wait_ge(s("nm5_ready"), b + 1)
                act.activation(p5[0:HU, b, :], ps[0:HU, 2 + b, 0:L], ACT.Exp, scale=SCALE, bias=c5[0:HU, b, 0:1],
                               accum_out=sum5[0:HU, b:b + 1]).then_inc(s("p5_ready"), 1)

            xnT_copy(6)
            w2_high(0, 0, 0)
            act.wait_ge(s("r_ready"), 1)
            act.activation(p6.rearrange("p a b -> p (a b)"), r6.rearrange("p a b -> p (a b)"), ACT.Exp
                           ).then_inc(s("r_exp"), 1)
            def expert(e, between):
                for ft in range(FT):
                    act.wait_ge(s("hm_ready"), FT * e + ft + 1)
                    act.wait_ge(s("h_split"), FT * e + ft + 1)
                    act.activation(h_f[:, ft % 4, :], ps[:, ft % 4, :], ACT.Silu).then_inc(s("hs_ready"), 1)
                    if ft in between:
                        between[ft]()

            def w2_next(e, par, i):
                act.wait_ge(s("y_ready"), e)
                w2_high(e + 1, 1 - par, i)

            expert(0, {1: lambda: w1_high(1, 1, 0), 3: lambda: w2_high(1, 1, 0), 7: lambda: w1_high(2, 0, 1)})
            with act.Fori(0, 2) as i:
                expert(2 * i + 1, {3: lambda: w2_next(2 * i + 1, 1, i + 1), 7: lambda: w1_high(2 * i + 3, 1, i + 1)})
                expert(2 * i + 2, {3: lambda: w2_next(2 * i + 2, 0, i + 1), 7: lambda: w1_high(2 * i + 4, 0, i + 2)})
            expert(5, {3: lambda: w2_next(5, 1, 3), 7: lambda: w1_high(7, 1, 3)})
            expert(6, {3: lambda: w2_next(6, 0, 3)})
            expert(7, {})

        @block.tensor
        def _(pe):
            def mm(out, lhsT, rhs, start=True, stop=True):
                return pe.matmul(out, lhsT, rhs, start=start, stop=stop, skip_group_check=True)

            pe.sem_inc(s("pv_done"), 2)

            def transpose_xn(k, bank=6):
                for h in range(2):
                    pe.wait_ge(s("ln_xn"), 2 * TURNS[k] - 1 + h)
                    for c in range(KF):
                        for j in range(QT):
                            ins = pe.transpose(ps[:, bank + h, c * L + j * P:c * L + (j + 1) * P],
                                               xn[:, QT * h + j, c * P:(c + 1) * P], ident[:, :])
                    ins.then_inc(s("ln_tr"), 1)
                pe.wait_ge(s("xnT_ready"), 2 * TURNS[k])

            def project(par, i, m):
                n = 2 * i + par
                if m == 0:
                    pe.wait_ge(s(f"cx_in{par}"), 16 * (i + 1))
                if m < 2:
                    pe.wait_ge(s("k_copied"), 2 * n + m + 1)
                    ins = mm(ps[:, 4 + m, :], w_kv[:, m * P:(m + 1) * P], cx[:, par, :])
                else:
                    pe.wait_ge(s("v_done"), 2 * n + m - 1)
                    for kk in range(2):
                        t = 2 * (m - 2) + kk
                        ins = mm(ps[:, 4 + m, kk * D:(kk + 1) * D], cx[:, par, t * P:(t + 1) * P], w_kv[:, D:2 * D])
                ins.then_inc(s("kv_ready"), 1)

            pe.wait_ge(s("wkv_in"), 16)
            for n in range(2):
                for m in range(4):
                    project(n, 0, m)

            pe.wait_ge(s("pool_step"), 3)
            transpose_xn(0, 2)
            pe.wait_ge(s("w0_in"), 16)
            for m in range(KF):
                for c in range(KF):
                    ins = mm(ps[:, m, :], w_a[:, c, m * P:(m + 1) * P], xnT[:, c, :], c == 0, c == KF - 1)
                ins.then_inc(s("q_ready"), 1)
            for m in range(4):
                project(0, 1, m)

            pe.wait_ge(s("dft_in"), 32)
            pe.wait_ge(s("q_hi_ready"), KF)
            pe.wait_ge(s("q_lo_ready"), KF)
            terms = (((0, 0), (1, 2)), ((0, 1), (1, 0)))
            for r in range(2):
                for m in range(KF):
                    n = 0
                    for wi, ti in terms[r]:
                        for c in range(KF):
                            ins = mm(ps[:, r, m * D:(m + 1) * D], wf[:, wi, c, m * P:(m + 1) * P], dft[:, ti, c, :],
                                     n == 0, n == 3)
                            n += 1
            ins.then_inc(s("uf_ready"), 1)
            for m in range(4):
                project(1, 1, m)
            pe.wait_ge(s("uf_done"), 1)
            for m in range(KF):
                n = 0
                for r in range(2):
                    for c in range(KF):
                        ins = mm(ps[:, 2, m * D:(m + 1) * D], dft[:, 3 + r, c, m * P:(m + 1) * P], uf[:, r, c, :],
                                 n == 0, n == 3)
                        n += 1
            ins.then_inc(s("m_mm"), 1)

            def max_half(g, par, k):
                un, hf = k // 2, k % 2
                c, j, qt = un // 8, (un % 8) // 2, un % 2
                if k == 0:
                    pe.wait_ge(s(f"qm_in{par}"), LOADQ * grp(g, par))
                if k % 16 == 0:
                    pe.wait_ge(s(f"ks_in{par}{c}"), LOADK * grp(g, par))
                if k == 0 and not (isinstance(g, int) and g == 0):
                    pe.wait_ge(s("nm_row"), g)
                if hf == 0:
                    pe.wait_ge(s("mx_used"), UNITS * g + un + 1)
                q0 = (j % 2) * L + qt * P
                k0 = c * CK + hf * 512
                ins = mm(ps[:, 2 * (un % 2) + hf, :], qm_stack[0:RS, par, j // 2, q0:q0 + P],
                         k_stack[0:RS, par, j // 2, k0:k0 + 512])
                if hf == 1:
                    ins.then_inc(s("mx_ready"), 1)

            def grp(g, par):
                if isinstance(g, int):
                    return g // 2 + 1
                return loads[0]

            loads = [None]

            def max_turn(g):
                pe.wait_ge(s("nm_ready"), g + 1)
                for c in range(8):
                    ins = mm(ps[0:1, c // 4, (c % 4) * P:(c % 4 + 1) * P], nm_t[:, c:c + 1], ident_r[:, :])
                ins.then_inc(s("nmt_ready"), 1)

            def scores(g, par, st, bk):
                if st == 0 and bk == 0:
                    pe.wait_ge(s(f"qe_in{par}"), LOADQ * grp(g, par))
                    pe.wait_ge(s("nm_row"), (g + 1))
                pe.wait_ge(s("p_ready"), 2 * KT * g + 2 * st + bk + 1)
                mm(ps[:, 4 + bk, :], k_stack[0:RS + 1, par, bk, st * P:(st + 1) * P], qe_stack[0:RS + 1, par, bk, :]
                   ).then_inc(s("s_ready"), 1)

            def values(g, par, st):
                if st == 0:
                    pe.wait_ge(s(f"vs_in{par}"), 16 * grp(g, par))
                    pe.wait_ge(s("o_evac"), g + 1)
                    pe.wait_ge(s("o_inv"), g + 1)
                pe.wait_ge(s("p_ready"), 2 * KT * g + 2 * st + 4)
                for j in range(GH):
                    ins = mm(ps[32 * j:32 * j + DH + 1, 6 + par, 0:L],
                             v_grp[:, par, st, j * (DH + 1):(j + 1) * (DH + 1)],
                             probs[:, (2 * st + j // 2) % PRING, (j % 2) * L:(j % 2 + 1) * L], st == 0, st == KT - 1)
                ins.then_inc(s("pv_done"), 1)

            def halves_at(st, slot):
                return [k for k in range(2 * UNITS) if k * MAX_SLOTS // (2 * UNITS) == 3 * st + slot]

            def out_product(b, qt, gg):
                out = ps[:, 1, qt * D:(qt + 1) * D] if b == 0 else ps[:, 2 + qt, 0:D]
                return mm(out, o_raw[:, NG // B * b + gg + 1, qt * P:(qt + 1) * P], w_o[:, gg, :],
                          gg == 0, gg == NG // B - 1)

            def last_outputs(st):
                if st == 4:
                    pe.wait_ge(s("o_evac"), NG + 1)
                    pe.wait_ge(s("nm_row"), NG)
                    mm(ps[:, 0, 0:L], head_ones, o_raw[:, NG - 1, :]).then_inc(s("o_sums"), 1)
                elif 6 <= st < 10:
                    if st == 6:
                        pe.wait_ge(s("wo_in"), 16 * GH)
                        pe.wait_ge(s("o_norm"), NG // B + 1)
                    for gg in range(2):
                        ins = out_product(0, (st - 6) // 2, 2 * (st % 2) + gg)
                    if st == 9:
                        ins.then_inc(s("y1_ready"), 1)
                elif 10 <= st < 10 + NG // B - 1:
                    if st == 10:
                        pe.wait_ge(s("o_norm"), NG)
                    for qt in range(QT):
                        out_product(1, qt, st - 10)

            def group_pass(g, par, following, load_now, load_next):
                def max_part(st, slot):
                    if following:
                        loads[0] = load_next
                        for k in halves_at(st, slot):
                            max_half(g + 1, 1 - par, k)
                        if (st, slot) == TURN_SLOT:
                            max_turn(g + 1)
                        if (st, slot) == SUM_SLOT:
                            pe.wait_ge(s("o_evac"), g + 2)
                            pe.wait_ge(s("masks_ready"), 1)
                            mm(ps[:, 7 - par, L:2 * L], head_ones, o_raw[:, bass.ds(g, 1), :].rearrange(
                                "p g l -> p (g l)")).then_inc(s("o_sums"), 1)

                def scores_part(st, bk):
                    if st + 1 < KT:
                        loads[0] = load_now
                        scores(g, par, st + 1, bk)
                    elif following:
                        loads[0] = load_next
                        scores(g + 1, 1 - par, 0, bk)

                for st in range(KT):
                    scores_part(st, 0)
                    max_part(st, 0)
                    scores_part(st, 1)
                    max_part(st, 1)
                    loads[0] = load_now
                    values(g, par, st)
                    max_part(st, 2)
                    if not following:
                        last_outputs(st)

            un = 0
            for n in range(4, NPC):
                for m in range(4):
                    project(n % 2, n // 2, m)
                    if n >= 5 and m >= 1 and un < UNITS:
                        if un == 0:
                            pe.wait_ge(s("m_ready"), 1)
                        max_half(0, 0, 2 * un)
                        max_half(0, 0, 2 * un + 1)
                        un += 1
            max_turn(0)
            pe.wait_ge(s("k_copied"), 2 * NPC + 2)
            pe.wait_ge(s("v_done"), 2 * NPC + 2)
            pe.wait_ge(s("pv_zero"), 1)
            pe.wait_ge(s("ones_rows"), 2)
            for bk in range(2):
                scores(0, 0, 0, bk)
            with pe.Fori(0, NG // 2 - 1) as i:
                group_pass(2 * i, 0, True, i + 1, i + 1)
                group_pass(2 * i + 1, 1, True, i + 1, i + 2)
            group_pass(NG - 2, 0, True, NG // 2, NG // 2)
            group_pass(NG - 1, 1, False, NG // 2, NG // 2)

            pe.wait_ge(s("o_evac"), NG + 2)
            mm(ps[:, 0, 0:L], head_ones, o_raw[:, NG, :]).then_inc(s("o_sums"), 1)
            pe.wait_ge(s("o_norm"), NG + 1)
            for qt in range(QT):
                ins = out_product(1, qt, NG // B - 1)
            ins.then_inc(s("y1_ready"), 1)

            transpose_xn(1)
            pe.wait_ge(s("w_in"), 16 * 5)
            for m in range(KF):
                for c in range(KF):
                    ins = mm(ps[:, m, :], w_gate[:, c, m * P:(m + 1) * P], xnT[:, c, :], c == 0, c == KF - 1)
                ins.then_inc(s("gate_mm"), 1)
            pe.wait_ge(s("u_ready"), KF)
            for c in range(KF):
                ins = mm(ps[0:64, 2, :], bc_w[:, c, :], u[:, c, :], c == 0, c == KF - 1)
            ins.then_inc(s("bc_mm"), 1)
            pe.wait_ge(s("gate_ready"), KF)
            pe.wait_ge(s("bc_ready"), 1)

            def add_states(n):
                for c in range(KF):
                    k = KF * n + c
                    pe.wait_ge(s("hc_ready"), k + 1)
                    mm(ps[:, 4 + c, :], ident[:, :], hc[:, k % 4, :], n == 0, n == NST - 1).then_inc(s("hc_used"), 1)

            def broadcast(n):
                if n >= 2:
                    pe.wait_ge(s("b_used"), n - 1)
                mm(ps[:, n % 2, :], sel_n[:, n:n + 1].to_broadcast([64, P]), bc_hl[:, :]).then_inc(s("b_ready"), 1)
                if n >= 2:
                    pe.wait_ge(s("c_bc_ready"), n - 1)
                mm(ps[:, 2 + n % 2, :], sel_n[:, 16 + n:17 + n].to_broadcast([64, P]), bc_hl[:, :]
                   ).then_inc(s("c_ready"), 1)

            broadcast(0)
            for n in range(NST):
                if n + 1 < NST:
                    broadcast(n + 1)
                if n >= 1:
                    add_states(n - 1)
            add_states(NST - 1)
            for j in range(NT):
                pe.wait_ge(s("yT_ready"), j // QT + 1)
                for c in range(KF):
                    ins = mm(ps[:, 6 + j // 2, (j % 2) * D:(j % 2 + 1) * D], yT[:, c, j * P:(j + 1) * P], w_out[:, c, :],
                             c == 0, c == KF - 1)
                if j % QT == QT - 1:
                    ins.then_inc(s("y2_ready"), 1)

            transpose_xn(3)
            for j in range(NT):
                for c in range(KF):
                    ins = mm(ps[:, j // 2, (j % 2) * D:(j % 2 + 1) * D], xnT[:, c, j * P:(j + 1) * P], m_dft[:, c, :],
                             c == 0, c == KF - 1)
                if j % QT == QT - 1:
                    ins.then_inc(s("y3_ready"), 1)

            transpose_xn(4)
            for m in range(KF):
                for c in range(KF):
                    ins = mm(ps[:, m, :], w_q1[:, c, m * P:(m + 1) * P], xnT[:, c, :], c == 0, c == KF - 1)
                ins.then_inc(s("q1_mm"), 1)
            pe.wait_ge(s("q1_ready"), KF)
            for c in range(KF):
                ins = mm(ps[:, 2, :], w_k1[:, c, :], q1T[:, c, :], c == 0, c == KF - 1)
            ins.then_inc(s("qp_mm"), 1)
            for j in range(NT):
                for c in range(KF):
                    ins = mm(ps[:, 3, j:j + 1], q1T[:, c, j * P:(j + 1) * P], vecs[:, BK1, c:c + 1], c == 0, c == KF - 1)
            ins.then_inc(s("qbk_mm"), 1)
            pe.wait_ge(s("qp_parts"), 3)

            def passes(out, pairs, start=True, stop=True):
                for n, (lhsT, rhs) in enumerate(pairs):
                    ins = mm(out, lhsT, rhs, start and n == 0, stop and n == len(pairs) - 1)
                return ins

            def max4(b, h):
                k, qt, c = b * UN4 + h, h // 8, h % 8
                if h == 0:
                    pe.wait_ge(s(f"c4_in{b}"), 32)
                if k >= 2:
                    pe.wait_ge(s("mx4_used"), k - 1)
                q = slice(b * L + qt * P, b * L + (qt + 1) * P)
                kk = slice(c * 512, (c + 1) * 512)
                passes(ps[:, 6 + k % 2, :], ((qp_hi[:, q], ct_hi[b][:, kk]), (qp_hi[:, q], ct_lo[b][:, kk]),
                                             (qp_lo[:, q], ct_hi[b][:, kk]))).then_inc(s("mx4_ready"), 1)

            def turn4(b):
                pe.wait_ge(s("nm4_cols"), b + 1)
                for qt in range(QT):
                    ins = mm(ps[0:1, 3, qt * P:(qt + 1) * P], nm4f[:, qt:qt + 1], ident[:, :])
                ins.then_inc(s("nm4_turned"), 1)

            def scores4(b, e):
                k = b * UN4 + e
                if e == 0:
                    pe.wait_ge(s("nm4_ready"), b + 1)
                if k >= 2:
                    pe.wait_ge(s("p4_ready"), k - 1)
                q = slice(b * L, (b + 1) * L)
                for t in range(2):
                    kk = slice((2 * e + t) * P, (2 * e + t + 1) * P)
                    o = ps[:, 4 + k % 2, t * L:(t + 1) * L]
                    passes(o, ((ct_hi[b][:, kk], qp_hi[:, q]), (ct_hi[b][:, kk], qp_lo[:, q]),
                               (ct_lo[b][:, kk], qp_hi[:, q])), stop=False)
                    ins = mm(o, ones_r[:, :], nm4[:, :], False, True)
                ins.then_inc(s("s4_ready"), 1)

            def values4(b, e):
                k = b * UN4 + e
                if k == 0:
                    pe.wait_ge(s("c4n_in"), 16)
                if b and e == 0:
                    pe.wait_ge(s("oc_ready"), b)
                pe.wait_ge(s("p4_ready"), k + 1)
                for t in range(2):
                    kt = 2 * e + t
                    ins = mm(ps[:, 0, 0:L], ctxN[:, b, kt, :], p4[:, k % 4, t * L:(t + 1) * L], kt == 0, kt == KT - 1)
                ins.then_inc(s("av4_done"), 1)

            def sums4(b):
                pe.wait_ge(s("p4_summed"), UN4 * (b + 1))
                for t in range(2):
                    ins = mm(ps[:, 1, 0:L], ones, psumP[:, t * L:(t + 1) * L], t == 0, t == 1)
                ins.then_inc(s("oc_sum"), 1)

            def out4(b):
                pe.wait_ge(s("oc_ready"), b + 1)
                for qt in range(QT):
                    ins = mm(ps[:, 2, qt * D:(qt + 1) * D], ocT[:, qt * P:(qt + 1) * P], w_v1[:, :])
                ins.then_inc(s("y4_ready"), 1)

            for h in range(UN4):
                max4(0, h)
            turn4(0)
            scores4(0, 0)
            for e in range(UN4):
                if e + 1 < UN4:
                    scores4(0, e + 1)
                max4(1, e)
                values4(0, e)
            sums4(0)
            turn4(1)
            scores4(1, 0)
            for e in range(UN4):
                if e + 1 < UN4:
                    scores4(1, e + 1)
                values4(1, e)
                if e == 2:
                    out4(0)
            sums4(1)
            out4(1)

            transpose_xn(5)
            for w in range(2):
                for m in range(KF):
                    for c in range(KF):
                        ins = mm(ps[:, 2 * w + m, :], w5[w][:, c, m * P:(m + 1) * P], xnT[:, c, :], c == 0, c == KF - 1)
                    ins.then_inc(s("qk5_mm"), 1)
            for w in range(2):
                for j in range(NT):
                    for c in range(KF):
                        ins = mm(ps[:, 4 + 2 * w + j // 2, (j % 2) * D:(j % 2 + 1) * D], xnT[:, c, j * P:(j + 1) * P],
                                 w5[2 * w][:, c, :], c == 0, c == KF - 1)
                ins.then_inc(s("qv5_mm"), 1)
            pe.wait_ge(s("k5_ready"), 1)
            pe.wait_ge(s("qv5_ready"), 2)
            for k in range(16):
                b, qt, hq = k // 8, (k // 4) % 2, k % 4
                pe.wait_ge(s("qm5_ready"), k + 1)
                if k >= 2:
                    pe.wait_ge(s("mx5_used"), k - 1)
                for j in range(4):
                    ins = mm(ps[:, 2 * (k % 2) + j // 2, (j % 2) * L:(j % 2 + 1) * L], qm5[:, k % 4, j, :],
                             kT5[:, hq // 2, b * L:(b + 1) * L])
                ins.then_inc(s("mx5_ready"), 1)
            pe.wait_ge(s("mx5_used"), 16)
            for qt in range(QT):
                ins = pe.transpose(ps[0:B * H, 4, qt * P:(qt + 1) * P], mx5[:, qt, :], ident[:, :])
            ins.then_inc(s("mT5_mm"), 1)
            pe.wait_ge(s("sel5_ready"), 1)
            for b in range(B):
                ins = mm(ps[0:HU, 5, 16 * b:16 * b + 16], sel_e[:, b, :], i5[0:B * H, :])
            ins.then_inc(s("sel5_mm"), 1)
            pe.wait_ge(s("sel5_ready"), 2)
            for b in range(B):
                for qt in range(QT):
                    ins = pe.transpose(ps[:, 4, (2 * b + qt) * P:(2 * b + qt) * P + HU],
                                       oneT[0:HU, b, qt * P:(qt + 1) * P], ident[0:HU, 0:HU])
            ins.then_inc(s("sel5_mm"), 1)
            pe.wait_ge(s("sel5_ready"), 3)
            for b in range(B):
                for c in range(KF):
                    for qt in range(QT):
                        ins = mm(ps[:, 0, (2 * b + c) * P:(2 * b + c) * P + HU], qn5[:, 2 * b + qt, c * P:(c + 1) * P],
                                 oneN[:, b, qt, :], qt == 0, qt == QT - 1)
            ins.then_inc(s("sel5_mm"), 1)
            pe.wait_ge(s("sel5_ready"), 4)
            for b in range(B):
                for c in range(KF):
                    ins = mm(ps[0:HU, 2 + b, 0:L], qsel[:, b, c, :], kT5[:, c, b * L:(b + 1) * L], c == 0, c == KF - 1)
                ins.then_inc(s("ss5_ready"), 1)
            for b in range(B):
                pe.wait_ge(s("p5_ready"), b + 1)
                for kt in range(QT):
                    ins = pe.transpose(ps[:, 4 + b, kt * P:kt * P + HU],
                                       p5[0:HU, b, kt * P:(kt + 1) * P], ident[0:HU, 0:HU])
                ins.then_inc(s("pT5_mm"), 1)
            for b in range(B):
                pe.wait_ge(s("pT5_ready"), b + 1)
                for kt in range(QT):
                    ins = mm(ps[0:HU, 6 + b, 0:D], pT5[:, b, kt, :], vn5[:, 2 * b + kt, :], kt == 0, kt == QT - 1)
                ins.then_inc(s("o5_mm"), 1)
            for b in range(B):
                pe.wait_ge(s("om5_ready"), b + 1)
                for c in range(KF):
                    ins = mm(ps[:, c, b * L:(b + 1) * L], om5[0:HU, b, c * P:(c + 1) * P], oneT[0:HU, b, :])
                ins.then_inc(s("oT5_mm"), 1)
            pe.wait_ge(s("oT5_ready"), 1)
            for j in range(NT):
                for c in range(KF):
                    ins = mm(ps[:, 2 + j // 2, (j % 2) * D:(j % 2 + 1) * D], oT5[:, c, j * P:(j + 1) * P], w5[3][:, c, :],
                             c == 0, c == KF - 1)
                if j % QT == QT - 1:
                    ins.then_inc(s("y5_ready"), 1)

            transpose_xn(6)
            for j in range(NT):
                for c in range(KF):
                    ins = mm(ps[:, 4, E * j:E * (j + 1)], xnT[:, c, j * P:(j + 1) * P], w_r[:, c, :], c == 0, c == KF - 1)
            ins.then_inc(s("r_mm"), 1)
            pe.wait_ge(s("xn_parts"), 2)
            with pe.Fori(0, E // 2) as i:
                for par in range(2):
                    e = 2 * i + par
                    pe.wait_ge(s("w1_split"), e + 1)
                    for ft in range(FT):
                        pe.wait_ge(s("hs_ready"), FT * e + ft + 1)
                        n = 0
                        for w, v in ((w1_hi, xn_hi), (w1_hi, xn_lo), (w1_lo, xn_hi)):
                            for c in range(KF):
                                ins = mm(ps[:, ft % 4, :], w[par][:, c, ft * P:(ft + 1) * P], v[:, c, :], n == 0, n == 5)
                                n += 1
                        ins.then_inc(s("hm_ready"), 1)
                    pe.wait_ge(s("w2_split"), e + 1)
                    pe.wait_ge(s("y_used"), NT * (e + 1))
                    for ft in range(FT):
                        pe.wait_ge(s("h_split"), FT * e + ft + 1 + 4)
                        for j in range(NT):
                            n = 0
                            for v, w in ((h_hi, w2_hi), (h_hi, w2_lo), (h_lo, w2_hi)):
                                ins = mm(ps[:, 4 + j, 0:D], v[ft][:, j * P:(j + 1) * P], w[par][:, ft, :],
                                         ft == 0 and n == 0, ft == FT - 1 and n == 2)
                                n += 1
                    ins.then_inc(s("y_ready"), 1)

        @block.vector
        def _(dve):
            steps = [0]

            def step(ins):
                steps[0] += 1
                ins.then_inc(s("dve_step"), 1)
                dve.wait_ge(s("dve_step"), steps[0])

            dve.sem_inc(s("mx_used"), 2)
            dve.sem_inc(s("o_inv"), 1)
            dve.sem_inc(s("h_split"), 4)

            def tiles(bank):
                return ps[:, bank:bank + 2, :].rearrange("p a (b d) -> p (a b) d", d=D)

            def layernorm(k, src, before=None, transposed=True):
                for h in range(2):
                    if before is not None:
                        before(h)
                    for j in range(QT * h, QT * (h + 1)):
                        ins = dve.bn_stats(stats[:, j, :], src[:, j, :])
                    step(ins)
                    for j in range(QT * h, QT * (h + 1)):
                        ins = dve.bn_aggr(mv[:, j, :], stats[:, j, :])
                    step(ins)
                    dve.tensor_scalar(mv[:, HALF[h], 1], mv[:, HALF[h], 1], EPS, None, ALU.add
                                      ).then_inc(s("ln_var"), 1)
                for h in range(2):
                    dve.wait_ge(s("ln_rstd"), 2 * k + h + 1)
                    for j in range(QT * h, QT * (h + 1)):
                        ins = dve.tensor_scalar(xn[:, j, :], src[:, j, :], mv[:, j, 0:1], rstd[:, j:j + 1],
                                                ALU.subtract, ALU.mult)
                    if transposed:
                        ins.then_inc(s("ln_xn"), 1)
                    else:
                        step(ins)

            def half_tiles(bank):
                return ps[:, bank, :].rearrange("p (a d) -> p a d", d=D)

            def add_half(dst, h, bank, ready, count):
                dve.wait_ge(s(ready), count)
                step(dve.tensor_tensor(dst[:, HALF[h], :], dst[:, HALF[h], :], half_tiles(bank), ALU.add))

            dve.memset(v_stage, 1.0).then_inc(s("v_ones"), 1)
            dve.wait_ge(s("x_in"), 16)
            layernorm(0, X)
            dve.memset(f32(qm_stack[:, :, :, :]), 0.0).then_inc(s("q_zero"), 1)
            for c in range(KF):
                dve.wait_ge(s("q_hi_ready"), c + 1)
                dve.tensor_tensor(q_lo[:, c, :], ps[:, c, :], f32(q_hi[:, c, :]), ALU.subtract
                                  ).then_inc(s("q_lo_ready"), 1)
            dve.memset(f32(qe_stack[:, :, :, :]), 0.0).then_inc(s("q_zero"), 1)
            dve.memset(w_o[:, :, :], 0.0).then_inc(s("wo_zero"), 1)
            dve.memset(f32(k_stack[RS:RS + 1, 0, :, :]), 1.0).then_inc(s("ones_rows"), 1)
            dve.wait_ge(s("q_out"), 16 * 2 * B)
            dve.memset(f32(k_stack[RS:RS + 1, 1, :, :]), 1.0).then_inc(s("ones_rows"), 1)
            dve.wait_ge(s("m_mm"), 1)
            dve.tensor_copy(m_dft[:, :, :].rearrange("p a b -> p (a b)"), ps[:, 2, :]).then_inc(s("m_ready"), 1)
            dve.wait_ge(s("m_ready"), 1)
            dve.sem_inc(s("dft_done"), 1)

            def max_pass(g, par):
                for un in range(UNITS):
                    c, j, qt = un // 8, (un % 8) // 2, un % 2
                    dve.wait_ge(s("mx_ready"), UNITS * g + un + 1)
                    dve.tensor_reduce(mxp[:, 2 * j + qt, c:c + 1],
                                      ps[:, 2 * (un % 2):2 * (un % 2) + 2, :].rearrange("p a b -> p (a b)"),
                                      AX.X, ALU.max).then_inc(s("mx_used"), 1)
                dve.wait_ge(s("mx_used"), UNITS * (g + 1) + 2)
                dve.tensor_reduce(nm_t[:, :], mxp, AX.X, ALU.max, negate=True).then_inc(s("nm_ready"), 1)
                dve.wait_ge(s("nmt_ready"), g + 1)
                dve.tensor_copy(qe_stack[RS:RS + 1, par, :, :], ps[0:1, 0:2, :]).then_inc(s("nm_row"), 1)

            dve.wait_ge(s("q_zero"), 2)
            max_pass(0, 0)
            dve.wait_ge(s("v_done"), 2 * NPC + 2)
            dve.memset(ps[:, 6:8, 0:L], 1.0).then_inc(s("pv_zero"), 1)

            def normalise(slot, sums):
                dve.wait_ge(s("o_sums"), slot + 1)
                dve.reciprocal(o_rec, sums).then_inc(s("o_inv"), 1)
                dve.wait_ge(s("o_inv"), slot + 2)
                o = o_raw[:, bass.ds(slot, 1), :].rearrange("p g l -> p (g l)")
                dve.tensor_tensor(o, o, o_rec, ALU.mult).then_inc(s("o_norm"), 1)
                dve.wait_ge(s("o_norm"), slot + 1)

            with dve.Fori(0, NG // 2 - 1) as i:
                for par in range(2):
                    max_pass(2 * i + par + 1, 1 - par)
                    normalise(2 * i + par, ps[:, 7 - par, L:2 * L])
            max_pass(NG - 1, 1)
            normalise(NG - 2, ps[:, 7, L:2 * L])
            normalise(NG - 1, ps[:, 0, 0:L])

            def before_1(b):
                if b == 1:
                    normalise(NG, ps[:, 0, 0:L])
                dve.wait_ge(s("y1_ready"), b + 1)
                step(dve.tensor_tensor(X[:, HALF[b], :], X[:, HALF[b], :],
                                       half_tiles(1) if b == 0 else ps[:, 2:4, 0:D], ALU.add))

            layernorm(1, X, before_1)
            for c in range(KF):
                step(dve.memset(xpad[:, c, :, 0:TAPS - 1], 0.0))
            dve.wait_ge(s("xnT_ready"), 2 * TURNS[1])
            dve.wait_ge(s("w_in"), 16 * 5)
            for c in range(KF):
                step(dve.tensor_copy(xpad[:, c, :, TAPS - 1:], xnT[:, c, :].rearrange("p (b l) -> p b l", b=B)))
                cv = conv[:, c, :].rearrange("p (b l) -> p b l", b=B)
                step(dve.tensor_scalar(cv, xpad[:, c, :, 0:L], conv_w[:, c, 0:1], vecs[:, CB, c:c + 1],
                                       ALU.mult, ALU.add))
                for t in range(1, TAPS):
                    ins = dve.scalar_tensor_tensor(cv, xpad[:, c, :, t:t + L], conv_w[:, c, t:t + 1], cv,
                                                   ALU.mult, ALU.add)
                    if t < TAPS - 1:
                        step(ins)
                ins.then_inc(s("conv_ready"), 1)
            dve.wait_ge(s("bc_hi_ready"), 1)
            dve.scalar_tensor_tensor(bc_hl[32:64, :], ps[32:64, 2, :], bc_b[32:64, 0:1], f32(bc_hl[32:64, :]),
                                     ALU.add, ALU.subtract).then_inc(s("bc_ready"), 1)
            dve.wait_ge(s("u_ready"), KF)
            dve.wait_ge(s("a_dec_ready"), 1)
            k = 0
            for n in range(NST):
                dve.wait_ge(s("b_ready"), n + 1)
                if n >= 2:
                    dve.wait_ge(s("h_ready"), KF * (n - 1))
                for c in range(KF):
                    ins = dve.tensor_tensor(b_in[:, 2 * (n % 2) + c, :], u[:, c, :], ps[:, n % 2, :], ALU.mult)
                    if c == KF - 1:
                        ins.then_inc(s("b_used"), 1)
                dve.wait_ge(s("b_used"), n + 1)
                for c in range(KF):
                    if k >= 4:
                        dve.wait_ge(s("hc_ready"), k - 3)
                    for b in range(B):
                        ins = dve.tensor_tensor_scan(h_st[:, k % 4, b * L:(b + 1) * L],
                                                     a_dec[:, c, n:n + 1].to_broadcast([P, L]),
                                                     b_in[:, 2 * (n % 2) + c, b * L:(b + 1) * L], 0.0, ALU.mult, ALU.add)
                    ins.then_inc(s("h_ready"), 1)
                    k += 1
            dve.wait_ge(s("h_ready"), k)
            dve.wait_ge(s("gate_ready"), KF)
            dve.wait_ge(s("hc_used"), k)
            for h in range(2):
                tok = slice(h * L, (h + 1) * L)
                for c in range(KF):
                    ins = dve.scalar_tensor_tensor(yT[:, c, tok], u[:, c, tok], vecs[:, DD, c:c + 1], ps[:, 4 + c, tok],
                                                   ALU.mult, ALU.add)
                step(ins)
                dve.tensor_tensor(yT[:, :, tok], yT[:, :, tok], gate[:, :, tok], ALU.mult).then_inc(s("yT_ready"), 1)
            step(dve.tensor_tensor(xn[:, :, :], xn[:, :, :], scaled_rows(rows[:, OB, :], NT), ALU.add))
            step(dve.tensor_tensor(X[:, :, :], X[:, :, :], scaled_rows(rows[:, LB, :], NT), ALU.add))
            layernorm(2, xn, lambda h: add_half(xn, h, 6 + h, "y2_ready", h + 1), transposed=False)

            def before_3(h):
                step(dve.tensor_tensor(xn[:, HALF[h], :], xn[:, HALF[h], :], scaled_rows(rows[:, LG, :], QT), ALU.mult))
                step(dve.tensor_tensor(X[:, HALF[h], :], X[:, HALF[h], :], xn[:, HALF[h], :], ALU.add))

            def add_rows(i, k):
                dve.wait_ge(s("ln_xn"), 2 * TURNS[k])
                step(dve.tensor_tensor(X[:, :, :], X[:, :, :], scaled_rows(rows[:, i, :], NT), ALU.add))

            layernorm(3, X, before_3)
            add_rows(FB, 3)

            layernorm(4, X, lambda h: add_half(X, h, h, "y3_ready", h + 1))
            add_rows(BV1, 4)
            step(dve.memset(ones, 1.0))
            dve.wait_ge(s("qp_mm"), 1)
            dve.tensor_copy(qp_hi, ps[:, 2, :]).then_inc(s("qp_parts"), 1)
            dve.wait_ge(s("qp_parts"), 1)
            dve.tensor_tensor(qp_lo, ps[:, 2, :], f32(qp_hi), ALU.subtract).then_inc(s("qp_parts"), 1)
            dve.wait_ge(s("qbk_mm"), 1)
            dve.tensor_copy(qbk[:, 0:NT], ps[:, 3, 0:NT]).then_inc(s("qp_parts"), 1)

            def max_part4(b, h):
                k = b * UN4 + h
                dve.wait_ge(s("mx4_ready"), k + 1)
                dve.tensor_reduce(mx4[:, h // 8, h % 8:h % 8 + 1], ps[:, 6 + k % 2, :], AX.X, ALU.max
                                  ).then_inc(s("mx4_used"), 1)

            def max_row4(b):
                dve.wait_ge(s("mx4_used"), UN4 * (b + 1))
                step(dve.tensor_reduce(mx4[:, :, 8:9], mx4[:, :, 0:8], AX.X, ALU.max))
                qb = qbk[:, 2 * b:2 * b + 2].unsqueeze(2)
                step(dve.tensor_tensor(mx4[:, :, 9:10], mx4[:, :, 8:9], qb, ALU.add))
                dve.tensor_tensor(nm4f.unsqueeze(2), qb, mx4[:, :, 9:10], ALU.subtract).then_inc(s("nm4_cols"), 1)
                if b:
                    dve.wait_ge(s("s4_ready"), UN4 * b)
                dve.wait_ge(s("nm4_turned"), b + 1)
                dve.tensor_copy(nm4[:, :], ps[0:1, 3, 0:L]).then_inc(s("nm4_ready"), 1)

            def prob_sum4(b, e):
                k = b * UN4 + e
                dve.wait_ge(s("p4_ready"), k + 1)
                if e == 0:
                    if b:
                        dve.wait_ge(s("oc_sum"), b)
                    dve.tensor_copy(psumP, p4[:, k % 4, :]).then_inc(s("p4_summed"), 1)
                else:
                    dve.wait_ge(s("p4_summed"), k)
                    dve.tensor_tensor(psumP, psumP, p4[:, k % 4, :], ALU.add).then_inc(s("p4_summed"), 1)

            def normalise4(b):
                dve.wait_ge(s("oc_sum"), b + 1)
                step(dve.reciprocal(rs4, ps[:, 1, 0:L]))
                dve.wait_ge(s("av4_done"), UN4 * (b + 1))
                if b:
                    dve.wait_ge(s("y4_ready"), b)
                dve.tensor_tensor(ocT, ps[:, 0, 0:L], rs4, ALU.mult).then_inc(s("oc_ready"), 1)

            for h in range(UN4):
                max_part4(0, h)
            max_row4(0)
            for e in range(UN4):
                prob_sum4(0, e)
                max_part4(1, e)
            max_row4(1)
            normalise4(0)
            for e in range(UN4):
                prob_sum4(1, e)
                if e == 4:
                    add_half(X, 0, 2, "y4_ready", 1)
            normalise4(1)

            layernorm(5, X, lambda h: add_half(X, 1, 2, "y4_ready", 2) if h == 1 else None)
            add_rows(BO5, 5)
            for w, dst in ((0, qn5), (1, vn5)):
                dve.wait_ge(s("qv5_mm"), w + 1)
                dve.tensor_tensor(dst, tiles(4 + 2 * w), scaled_rows(rows[:, BQ5R if w == 0 else BV5, :], NT), ALU.add
                                  ).then_inc(s("qv5_ready"), 1)
            for k in range(16):
                b, qt, hq = k // 8, (k // 4) % 2, k % 4
                dve.wait_ge(s("mx5_ready"), k + 1)
                dve.tensor_reduce(mx5[:, qt, b * H + 4 * hq:b * H + 4 * hq + 4],
                                  ps[:, 2 * (k % 2):2 * (k % 2) + 2, :].rearrange("p a (b q) -> p (a b) q", q=L),
                                  AX.X, ALU.max).then_inc(s("mx5_used"), 1)
            dve.wait_ge(s("mT5_mm"), 1)
            mT = mT5[0:B * H, :]
            step(dve.tensor_copy(mT, ps[0:B * H, 4, 0:L]))
            step(dve.max(i5[0:B * H, 8:16], mT))
            ix = idx5[0:B * H, :].bitcast(U32)
            step(dve.max_index(ix, i5[0:B * H, 8:16], mT))
            dve.tensor_copy(i5[0:B * H, 0:8], ix).then_inc(s("sel5_ready"), 1)
            dve.wait_ge(s("masks_ready"), 1)
            step(dve.tensor_reduce(umask[:, 0:TOPU], umask3[:, :, :].rearrange("p h u -> p u h"), AX.X, ALU.max))
            dve.wait_ge(s("sel5_mm"), 1)
            for b in range(B):
                for r in range(2):
                    step(dve.tensor_tensor(s5[0:HU, 0, 0:TOPU], ps[0:HU, 5, 16 * b + 8 * r:16 * b + 8 * r + TOPU],
                                           umask[:, 0:TOPU], ALU.mult))
                    step(dve.tensor_reduce(c5[0:HU, b, 1 - r:2 - r], s5[0:HU, 0, 0:TOPU], AX.X, ALU.add))
            dve.wait_ge(s("iota_ready"), 1)
            for b in range(B):
                ins = dve.tensor_scalar(oneT[0:HU, b, :], iota5[0:HU, :], c5[0:HU, b, 1:2], None, ALU.is_equal)
            ins.then_inc(s("sel5_ready"), 1)
            for b in range(B):
                dve.tensor_scalar(c5[0:HU, b, 0:1], c5[0:HU, b, 0:1], -SCALE, None, ALU.mult).then_inc(s("nm5_ready"), 1)
            dve.wait_ge(s("sel5_mm"), 2)
            dve.tensor_copy(oneN.rearrange("p b q h -> p (b q) h"),
                            ps[:, 4, :].rearrange("p (k h) -> p k h", h=P)[:, :, 0:HU]).then_inc(s("sel5_ready"), 1)
            dve.wait_ge(s("sel5_mm"), 3)
            for b in range(B):
                ins = dve.tensor_tensor(qsel[:, b, :, :], ps[:, 0, 2 * b * P:(2 * b + 2) * P].rearrange(
                    "p (c h) -> p c h", h=P)[:, :, 0:HU], bd5[:, :, :], ALU.mult)
            ins.then_inc(s("sel5_ready"), 1)
            for b in range(B):
                dve.wait_ge(s("pT5_mm"), b + 1)
                dve.tensor_copy(pT5[:, b, :, :], ps[:, 4 + b, 0:2 * P].rearrange(
                    "p (c h) -> p c h", h=P)[:, :, 0:HU]).then_inc(s("pT5_ready"), 1)
            step(dve.reciprocal(rs5[0:HU, :], sum5[0:HU, :]))
            for b in range(B):
                dve.wait_ge(s("o5_mm"), b + 1)
                dve.scalar_tensor_tensor(om5[0:HU, b, :], ps[0:HU, 6 + b, 0:D], rs5[0:HU, b:b + 1], bdT5[:, :],
                                         ALU.mult, ALU.mult).then_inc(s("om5_ready"), 1)
            dve.wait_ge(s("oT5_mm"), B)
            dve.tensor_copy(oT5.rearrange("p c t -> p (c t)"), ps[:, 0:2, :].rearrange("p a b -> p (a b)")
                            ).then_inc(s("oT5_ready"), 1)

            def before_6(h):
                add_half(X, h, 2 + h, "y5_ready", h + 1)
                if h == 1:
                    dve.sem_inc(s("a5_done"), 1)

            layernorm(6, X, before_6)
            dve.wait_ge(s("xnT_ready"), 2 * TURNS[6])
            dve.tensor_copy(xn_hi, xnT[:, :, :]).then_inc(s("xn_parts"), 1)
            dve.wait_ge(s("xn_parts"), 1)
            dve.tensor_tensor(xn_lo, xnT[:, :, :], f32(xn_hi), ALU.subtract).then_inc(s("xn_parts"), 1)
            dve.wait_ge(s("r_mm"), 1)
            dve.tensor_copy(r6.rearrange("p a b -> p (a b)"), ps[:, 4, 0:NT * E]).then_inc(s("r_copied"), 1)
            dve.wait_ge(s("r_copied"), 1)
            dve.sem_inc(s("y_used"), NT)
            step(dve.tensor_reduce(c6[:, :, 0:1], r6, AX.X, ALU.max))
            dve.tensor_tensor(r6, r6, c6[:, :, 0:1].to_broadcast([P, NT, E]), ALU.subtract).then_inc(s("r_ready"), 1)
            dve.wait_ge(s("r_exp"), 1)
            step(dve.tensor_reduce(c6[:, :, 1:2], p6, AX.X, ALU.add))
            step(dve.reciprocal(c6[:, :, 2:3], c6[:, :, 1:2]))
            step(dve.tensor_tensor(p6, p6, c6[:, :, 2:3].to_broadcast([P, NT, E]), ALU.mult))
            for j in range(NT):
                ins = dve.max(t6[:, j, :], p6[:, j, :])
            step(ins)
            for j in range(NT):
                ins = dve.max_index(i6[:, j, :].bitcast(U32), t6[:, j, :], p6[:, j, :])
            step(ins)
            step(dve.tensor_copy(f6, i6.bitcast(U32)))
            step(dve.tensor_tensor(c6[:, :, 3:4], t6[:, :, 0:1], t6[:, :, 1:2], ALU.add))
            step(dve.reciprocal(c6[:, :, 4:5], c6[:, :, 3:4]))
            step(dve.tensor_tensor(t6[:, :, 0:2], t6[:, :, 0:2], c6[:, :, 4:5].to_broadcast([P, NT, 2]), ALU.mult))
            for j in range(NT):
                for r, dst in ((0, gates), (1, g6)):
                    ins = dve.tensor_scalar(dst[:, j, :], iota6, f6[:, j, r:r + 1], t6[:, j, r:r + 1],
                                            ALU.is_equal, ALU.mult)
            step(ins)
            step(dve.tensor_tensor(gates, gates, g6, ALU.add))
            with dve.Fori(0, E // 2) as i:
                for par in range(2):
                    e = 2 * i + par
                    for ft in range(FT):
                        dve.wait_ge(s("hs_ready"), FT * e + ft + 1 + 4)
                        dve.tensor_copy(h_hi[ft], h_f[:, ft % 4, :]).then_inc(s("h_hi_ready"), 1)
                        dve.wait_ge(s("h_hi_ready"), FT * e + ft + 1)
                        dve.tensor_tensor(h_lo[ft], h_f[:, ft % 4, :], f32(h_hi[ft]), ALU.subtract
                                          ).then_inc(s("h_split"), 1)
                    dve.wait_ge(s("y_ready"), e + 1)
                    for j in range(NT):
                        dve.wait_ge(s("y_used"), NT * e + j + 1)
                        dve.scalar_tensor_tensor(X[:, j, :], ps[:, 4 + j, 0:D], gates[:, j, bass.ds(e, 1)], X[:, j, :],
                                                 ALU.mult, ALU.add).then_inc(s("y_used"), 1)
            dve.wait_ge(s("y_used"), NT * E + NT)
            dve.sem_inc(s("x_done"), 1)


_LAYOUT = {
    "x": ("x", lambda v: v.reshape(T, D)),
    "ctx": ("ctx_512", lambda v: v),
    "ctxT": ("ctx_512", lambda v: v.transpose(2, 0, 1).reshape(LAT, B * S)),
    "wqT": ("L0_xattn_Wq", lambda v: v.T),
    "wkvT": ("L0_xattn_Wkv", lambda v: v.T),
    "woT": ("L0_xattn_Wo", lambda v: v.T),
    "wv1": ("L1_xattn_Wv", lambda v: v),
    "w1T": ("L1_ffn_W1", lambda v: v.transpose(0, 2, 1)),
    "w2T": ("L1_ffn_W2", lambda v: v.transpose(0, 2, 1)),
}


def dft_tables():
    k = np.arange(D)
    w = 2 * np.pi * ((k[:, None] * k[None, :]) % D) / D
    c, sn = np.cos(w), np.sin(w)
    return np.stack([c, sn, -sn, c / D, sn / D]).astype(np.float32)


def kernel(**inputs):
    import concourse.bacc as _bacc
    from concourse.bass_utils import run_bass_kernel_spmd as _run

    nc = _bacc.Bacc("TRN2", target_bir_lowering=False, num_devices=1)
    arrays, a = {}, {}
    for name, (source, layout) in _LAYOUT.items():
        arrays[f"in_{name}"] = np.ascontiguousarray(layout(np.asarray(inputs[source])))
    arrays["in_vecs"] = np.ascontiguousarray(
        np.stack([np.asarray(inputs[n]).reshape(KF, P).T for n in VECS], axis=1))
    arrays["in_rows"] = np.stack([np.asarray(inputs[n]) for n in ROWS])
    arrays["in_packed"] = np.concatenate(
        [v.reshape(D, n) if name in AS_IS else v.T for name, n, v in
         ((name, n, np.asarray(inputs[name])) for name, n in PACK)], axis=1)
    arrays["in_bc_b"] = np.concatenate([np.asarray(inputs["L0_attn_Bp_b"]), np.asarray(inputs["L0_attn_Cp_b"])] * 2
                                       ).reshape(4 * NST, 1)
    arrays["in_freqT"] = np.stack([np.asarray(inputs["L0_ffn_w_freq_real"]).T, np.asarray(inputs["L0_ffn_w_freq_imag"]).T])
    arrays["in_dft"] = dft_tables()
    for name, v in arrays.items():
        a[name[3:]] = nc.dram_tensor(name, v.shape, mybir.dt.from_np(v.dtype), kind="ExternalInput").ap()
    a["out"] = nc.dram_tensor("out", (T, D), F32, kind="ExternalOutput").ap()
    perceiver(nc, a)
    r = _run(nc, [arrays], core_ids=[0])
    return r.results[0]["out"].reshape(B, L, D)
```
